# Optimizing a Trainium2 kernel written in Bass

```python
import numpy as np
import jax
import jax.numpy as jnp

def _softmax(x, axis=-1):
    return jax.nn.softmax(x, axis=axis)

def _gelu(x):
    return jax.nn.gelu(x, approximate=True)

def _silu(x):
    return jax.nn.silu(x)

def _sigmoid(x):
    return jax.nn.sigmoid(x)

def _layernorm(x, axis=-1, eps=1e-05):
    m = jnp.mean(x, axis=axis, keepdims=True)
    v = jnp.var(x, axis=axis, keepdims=True)
    return (x - m) / jnp.sqrt(v + eps)

def _scatter_add(tgt, idx, src, axis=0):
    return tgt.at[idx].add(src)

def _segment_sum(src, seg, n):
    return jax.ops.segment_sum(src, seg, n)
kernel_name = 'mk_seq_postln_d4_jaxref_r8_d9510d'

def setup_inputs(seed: int=0):
    np.random.seed(seed)
    _w = jnp.asarray

    def _L0_attn_setup():
        import jax, jax.numpy as jnp
        import numpy as np
        HEADS = 16
        D_MODEL = 128
        EXPANSION = 2
        D_EXP = D_MODEL * EXPANSION
        D_HEAD = D_EXP // HEADS
        B, SEQ = (1, 256)
        LN_EPS = 1e-05
        NEG_BIG = -10000000000.0

        def layer_norm(x, w, b):
            mu = jnp.mean(x, axis=-1, keepdims=True)
            var = jnp.var(x, axis=-1, keepdims=True)
            return (x - mu) * jax.lax.rsqrt(var + LN_EPS) * w + b
        key = jax.random.key(seed)
        ks = jax.random.split(key, 8)
        d_out = 4 * D_EXP + HEADS
        x = jax.random.normal(ks[0], (B, SEQ, D_MODEL), dtype=jnp.float32)
        W_in = 0.02 * jax.random.normal(ks[1], (d_out, D_MODEL), dtype=jnp.float32)
        b_in = jnp.zeros((d_out,), dtype=jnp.float32)
        W_in = W_in.at[4 * D_EXP:].set(0.0)
        b_in = b_in.at[4 * D_EXP:].set(jnp.linspace(-8.0, 8.0, HEADS))
        W_out = 0.02 * (2 * 12) ** (-0.5) * jax.random.normal(ks[2], (D_MODEL, D_EXP), dtype=jnp.float32)
        in_ln_w = jnp.ones((D_MODEL,), dtype=jnp.float32)
        in_ln_b = jnp.zeros((D_MODEL,), dtype=jnp.float32)
        out_ln_w = jnp.ones((D_MODEL,), dtype=jnp.float32)
        out_ln_b = jnp.zeros((D_MODEL,), dtype=jnp.float32)
        smear_factor = jnp.linspace(-6.0, 6.0, HEADS)
        log_scale = jnp.zeros((HEADS,), dtype=jnp.float32)
        return {'x': x, 'W_in': W_in, 'b_in': b_in, 'in_ln_w': in_ln_w, 'in_ln_b': in_ln_b, 'W_out': W_out, 'out_ln_w': out_ln_w, 'out_ln_b': out_ln_b, 'smear_factor': smear_factor, 'log_scale': log_scale}
    _L0_attn_in = _L0_attn_setup()

    def _L0_ffn_setup():
        import jax, jax.numpy as jnp
        import numpy as np
        D_MODEL = 128
        HIDDEN = 512
        NUM_EXPERTS = 8
        TOP_K = 2
        key = jax.random.key(seed)
        k_x, k_g, k_in, k_out = jax.random.split(key, 4)
        bound_in = 1.0 / HIDDEN
        bound_out = 1.0 / D_MODEL
        x = jax.random.normal(k_x, (2, 256, D_MODEL), dtype=jnp.float32)
        w_gate = jax.random.uniform(k_g, (NUM_EXPERTS, D_MODEL), dtype=jnp.float32, minval=-D_MODEL ** (-0.5), maxval=D_MODEL ** (-0.5))
        w_in = jax.random.uniform(k_in, (NUM_EXPERTS, HIDDEN, D_MODEL), dtype=jnp.float32, minval=-bound_in, maxval=bound_in)
        w_out = jax.random.uniform(k_out, (NUM_EXPERTS, D_MODEL, HIDDEN), dtype=jnp.float32, minval=-bound_out, maxval=bound_out)
        return {'x': x, 'w_gate': w_gate, 'w_in': w_in, 'w_out': w_out}
    _L0_ffn_in = _L0_ffn_setup()

    def _L1_attn_setup():
        import jax, jax.numpy as jnp
        import numpy as np
        B, S, H, NH, P = (1, 256, 128, 16, 2)
        D = H // NH
        SCALE = 1.0 / np.sqrt(D).astype(np.float32)

        def _lin(x, W, b):
            return x @ W + b

        def _split_heads(x):
            return x.reshape(*x.shape[:-2], x.shape[-2], NH, D).swapaxes(-3, -2)

        def _merge_heads(x):
            return x.swapaxes(-3, -2).reshape(*x.shape[:-3], x.shape[-2], H)
        key = jax.random.key(seed)
        ks = jax.random.split(key, 20)
        w = lambda k, i, o: jax.random.normal(k, (i, o), jnp.float32) * 0.02
        inp = {'hidden_states': jax.random.normal(ks[0], (B, S, H), jnp.float32), 'past_states': jax.random.normal(ks[1], (P, B, S, H), jnp.float32), 'Wq': w(ks[2], H, H), 'bq': jnp.zeros((H,), jnp.float32), 'Wk': w(ks[3], H, H), 'bk': jnp.zeros((H,), jnp.float32), 'Wv': w(ks[4], H, H), 'bv': jnp.zeros((H,), jnp.float32), 'Wo': w(ks[5], H, H), 'bo': jnp.zeros((H,), jnp.float32), 'Wrq': w(ks[6], H, H), 'brq': jnp.zeros((H,), jnp.float32), 'Wrk': w(ks[7], H, H), 'brk': jnp.zeros((H,), jnp.float32), 'Wrv': w(ks[8], H, H), 'brv': jnp.zeros((H,), jnp.float32), 'Wg': w(ks[9], 2 * H, H), 'bg': jnp.zeros((H,), jnp.float32)}
        return inp
    _L1_attn_in = _L1_attn_setup()

    def _L1_ffn_setup():
        import jax, jax.numpy as jnp
        import numpy as np
        TOP_K = 2
        key = jax.random.key(seed)
        ks = jax.random.split(key, 8)
        B, S, D = (2, 256, 128)
        N_r, N_s = (16, 2)
        u = jax.random.normal(ks[0], (B, S, D), dtype=jnp.float32)
        centroids = jax.random.normal(ks[1], (N_r, D), dtype=jnp.float32)
        expert_biases = jnp.zeros((N_r,), dtype=jnp.float32)
        Wr = jax.random.normal(ks[2], (N_r, D, D), dtype=jnp.float32) * (1.0 / np.sqrt(D))
        br = jax.random.normal(ks[3], (N_r, D), dtype=jnp.float32) * 0.01
        Ws = jax.random.normal(ks[4], (N_s, D, D), dtype=jnp.float32) * (1.0 / np.sqrt(D))
        bs = jax.random.normal(ks[5], (N_s, D), dtype=jnp.float32) * 0.01
        return {'u': u, 'centroids': centroids, 'expert_biases': expert_biases, 'Wr': Wr, 'br': br, 'Ws': Ws, 'bs': bs}
    _L1_ffn_in = _L1_ffn_setup()

    def _L2_attn_setup():
        import jax, jax.numpy as jnp
        import numpy as np
        B, S, D, N, H = (4, 512, 128, 128, 64)
        TIME_DELTA = 0.1
        LN_EPS = 1e-05

        def _reference_tuple_inner(x, A_log, B_w, B_b, C_w, C_b, norm_g, norm_b, ff1_w, ff1_b, ff2_w, ff2_b, ta_w, ta_b, tb_w, tb_b, out_w, out_b):
            mu = x.mean(-1, keepdims=True)
            var = ((x - mu) ** 2).mean(-1, keepdims=True)
            xn = (x - mu) * jax.lax.rsqrt(var + LN_EPS) * norm_g + norm_b
            A = jax.nn.sigmoid(A_log)
            B_all = jnp.einsum('bsd,nd->bsn', xn, B_w) + B_b
            powers = jnp.arange(x.shape[1], dtype=x.dtype)[:, None]
            A_pow = A[None, :] ** powers
            A_safe = jnp.maximum(A_pow, 1e-08)
            states = A_pow[None] * jnp.cumsum(B_all / A_safe[None], axis=1)
            ssm_out = jnp.einsum('bsn,dn->bsd', states, C_w) + C_b
            final_ssm_state = states[:, -1, :]

            def step(h, xt):
                cat = jnp.concatenate([xt, h], axis=-1)
                ff1 = jnp.tanh(cat @ ff1_w.T + ff1_b)
                ff2 = jnp.tanh(cat @ ff2_w.T + ff2_b)
                t_i = jax.nn.sigmoid((cat @ ta_w.T + ta_b) * TIME_DELTA + (cat @ tb_w.T + tb_b))
                h_new = ff1 * (1.0 - t_i) + t_i * ff2
                return (h_new, h_new)
            h0 = jnp.zeros((x.shape[0], ff1_w.shape[0]), x.dtype)
            h_last, cfc_seq = jax.lax.scan(step, h0, jnp.swapaxes(ssm_out, 0, 1))
            cfc_out = jnp.swapaxes(cfc_seq, 0, 1)
            layer_out = x + cfc_out @ out_w.T + out_b
            return (layer_out, final_ssm_state, h_last)
        key = jax.random.key(seed)
        ks = jax.random.split(key, 12)
        w = lambda k, shape: jax.random.normal(k, shape, jnp.float32) * 0.02
        return {'x': jax.random.normal(ks[0], (B, S, D), jnp.float32), 'A_log': jax.random.normal(ks[1], (N,), jnp.float32), 'B_w': w(ks[2], (N, D)), 'B_b': jnp.zeros((N,), jnp.float32), 'C_w': w(ks[3], (D, N)), 'C_b': jnp.zeros((D,), jnp.float32), 'norm_g': jnp.ones((D,), jnp.float32), 'norm_b': jnp.zeros((D,), jnp.float32), 'ff1_w': w(ks[4], (H, D + H)), 'ff1_b': jnp.zeros((H,), jnp.float32), 'ff2_w': w(ks[5], (H, D + H)), 'ff2_b': jnp.zeros((H,), jnp.float32), 'ta_w': w(ks[6], (H, D + H)), 'ta_b': jnp.zeros((H,), jnp.float32), 'tb_w': w(ks[7], (H, D + H)), 'tb_b': jnp.zeros((H,), jnp.float32), 'out_w': w(ks[8], (D, H)), 'out_b': jnp.zeros((D,), jnp.float32)}
    _L2_attn_in = _L2_attn_setup()

    def _L2_ffn_setup():
        import jax, jax.numpy as jnp
        import numpy as np

        def _bitlinear(x, w_latent):
            scale = jax.lax.stop_gradient(jnp.clip(jnp.mean(jnp.abs(w_latent), axis=1, keepdims=True), 1e-05, None))
            tern = jnp.clip(jnp.round(w_latent / scale), -1.0, 1.0)
            w = w_latent + jax.lax.stop_gradient(tern - w_latent)
            return x @ (w * scale).T
        key = jax.random.key(seed)
        ks = jax.random.split(key, 6)
        dim, hidden, rank = (128, 512, 16)
        B, S = (4, 512)
        x = jax.random.normal(ks[0], (B, S, dim), dtype=jnp.float32)
        w_fc = 0.02 * jax.random.normal(ks[1], (hidden, dim), dtype=jnp.float32)
        w_proj = 0.02 * jax.random.normal(ks[2], (dim, hidden), dtype=jnp.float32)
        u = 0.02 * jax.random.normal(ks[3], (hidden, rank), dtype=jnp.float32)
        v = 0.02 * jax.random.normal(ks[4], (rank, dim), dtype=jnp.float32)
        fast_b = jax.random.normal(ks[5], (rank, rank), dtype=jnp.float32)
        gate = jnp.float32(0.05)
        return {'x': x, 'fast_b': fast_b, 'w_fc': w_fc, 'w_proj': w_proj, 'u': u, 'v': v, 'gate': gate}
    _L2_ffn_in = _L2_ffn_setup()

    def _L3_attn_setup():
        import jax, jax.numpy as jnp
        import numpy as np
        D_MODEL = 128
        N_LAYER = 4
        EXPAND = 2
        HEADDIM = 32
        D_STATE = 128
        D_CONV = 4
        NGROUPS = 1
        D_INNER = EXPAND * D_MODEL
        NHEADS = D_INNER // HEADDIM
        CONV_DIM = D_INNER + 2 * NGROUPS * D_STATE
        D_IN_PROJ = 2 * D_INNER + 2 * NGROUPS * D_STATE + NHEADS
        BATCH, SEQLEN = (4, 256)

        def _rmsnorm(x, w, eps=1e-05):
            return x * jax.lax.rsqrt(jnp.mean(x * x, axis=-1, keepdims=True) + eps) * w

        def _mamba2_layer(h, Wi, cw, cb, dtb, Alog, Dh, gw, Wo):
            B, L, _ = h.shape
            zxbcdt = h @ Wi
            z, xBC, dt = jnp.split(zxbcdt, [D_INNER, D_INNER + CONV_DIM], axis=-1)
            xp = jnp.pad(xBC, ((0, 0), (D_CONV - 1, 0), (0, 0)))
            conv = cb + sum((xp[:, k:k + L, :] * cw[:, k] for k in range(D_CONV)))
            xBC = jax.nn.silu(conv)
            xs, Bm, Cm = jnp.split(xBC, [D_INNER, D_INNER + D_STATE], axis=-1)
            xs = xs.reshape(B, L, NHEADS, HEADDIM)
            dt = jax.nn.softplus(dt + dtb)
            A = -jnp.exp(Alog)
            dA = jnp.exp(dt * A)
            dtx = dt[..., None] * xs

            def step(hs, inp):
                dA_t, dtx_t, B_t, C_t = inp
                hs = hs * dA_t[:, :, None, None] + dtx_t[..., None] * B_t[:, None, None, :]
                y = jnp.einsum('bhpn,bn->bhp', hs, C_t)
                return (hs, y)
            h0 = jnp.zeros((B, NHEADS, HEADDIM, D_STATE), h.dtype)
            _, ys = jax.lax.scan(step, h0, (dA.swapaxes(0, 1), dtx.swapaxes(0, 1), Bm.swapaxes(0, 1), Cm.swapaxes(0, 1)))
            y = ys.swapaxes(0, 1) + Dh[None, None, :, None] * xs
            y = y.reshape(B, L, D_INNER)
            y = _rmsnorm(y * jax.nn.silu(z), gw)
            return y @ Wo
        key = jax.random.key(seed)
        ks = jax.random.split(key, 8)
        x = jax.random.normal(ks[0], (BATCH, SEQLEN, D_MODEL), jnp.float32)
        s_in = 1.0 / np.sqrt(D_MODEL)
        s_out = 1.0 / np.sqrt(D_INNER)
        W_in = jax.random.normal(ks[1], (N_LAYER, D_MODEL, D_IN_PROJ), jnp.float32) * s_in
        conv_w = jax.random.normal(ks[2], (N_LAYER, CONV_DIM, D_CONV), jnp.float32) * 0.5
        conv_b = jnp.zeros((N_LAYER, CONV_DIM), jnp.float32)
        dt = jax.random.uniform(ks[3], (N_LAYER, NHEADS), jnp.float32, 0.001, 0.1)
        dt_bias = jnp.log(jnp.expm1(dt))
        A_log = jnp.log(jax.random.uniform(ks[4], (N_LAYER, NHEADS), jnp.float32, 1.0, 16.0))
        D = jnp.ones((N_LAYER, NHEADS), jnp.float32)
        gate_norm_w = jnp.ones((N_LAYER, D_INNER), jnp.float32)
        W_out = jax.random.normal(ks[5], (N_LAYER, D_INNER, D_MODEL), jnp.float32) * s_out
        block_norm_w = jnp.ones((N_LAYER, D_MODEL), jnp.float32)
        final_norm_w = jnp.ones((D_MODEL,), jnp.float32)
        return dict(x=x, W_in=W_in, conv_w=conv_w, conv_b=conv_b, dt_bias=dt_bias, A_log=A_log, D=D, gate_norm_w=gate_norm_w, W_out=W_out, block_norm_w=block_norm_w, final_norm_w=final_norm_w)
    _L3_attn_in = _L3_attn_setup()

    def _L3_ffn_setup():
        import jax, jax.numpy as jnp
        import numpy as np
        E = 8
        K = 2
        S = 1
        THRESHOLD = 0.7
        NORM_TOPK = True
        H = 128
        F = 128
        B, SEQ = (2, 128)
        key = jax.random.key(seed)
        k1, k2, k3, k4, k5 = jax.random.split(key, 5)
        hidden_states = jax.random.normal(k1, (B, SEQ, H), jnp.float32)
        gate_weight = jax.random.normal(k2, (E, H), jnp.float32) * 0.02
        gate_up_proj = jax.random.normal(k3, (E, 2 * F, H), jnp.float32) * 0.02
        down_proj = jax.random.normal(k4, (E, H, F), jnp.float32) * 0.02
        sim = jax.random.uniform(k5, (E, E), jnp.float32)
        sim = (sim + sim.T) / 2.0
        sim = sim.at[jnp.arange(E), jnp.arange(E)].set(1.0)
        return {'hidden_states': hidden_states, 'gate_weight': gate_weight, 'gate_up_proj': gate_up_proj, 'down_proj': down_proj, 'similarity_matrix': sim}
    _L3_ffn_in = _L3_ffn_setup()
    _d = {'L0_attn_x': _L0_attn_in['x'], 'L0_attn_W_in': _L0_attn_in['W_in'], 'L0_attn_b_in': _L0_attn_in['b_in'], 'L0_attn_in_ln_w': _L0_attn_in['in_ln_w'], 'L0_attn_in_ln_b': _L0_attn_in['in_ln_b'], 'L0_attn_W_out': _L0_attn_in['W_out'], 'L0_attn_out_ln_w': _L0_attn_in['out_ln_w'], 'L0_attn_out_ln_b': _L0_attn_in['out_ln_b'], 'L0_attn_smear_factor': _L0_attn_in['smear_factor'], 'L0_attn_log_scale': _L0_attn_in['log_scale'], 'L0_ffn_w_gate': _L0_ffn_in['w_gate'], 'L0_ffn_w_in': _L0_ffn_in['w_in'], 'L0_ffn_w_out': _L0_ffn_in['w_out'], 'L1_attn_past_states': _L1_attn_in['past_states'], 'L1_attn_Wq': _L1_attn_in['Wq'], 'L1_attn_bq': _L1_attn_in['bq'], 'L1_attn_Wk': _L1_attn_in['Wk'], 'L1_attn_bk': _L1_attn_in['bk'], 'L1_attn_Wv': _L1_attn_in['Wv'], 'L1_attn_bv': _L1_attn_in['bv'], 'L1_attn_Wo': _L1_attn_in['Wo'], 'L1_attn_bo': _L1_attn_in['bo'], 'L1_attn_Wrq': _L1_attn_in['Wrq'], 'L1_attn_brq': _L1_attn_in['brq'], 'L1_attn_Wrk': _L1_attn_in['Wrk'], 'L1_attn_brk': _L1_attn_in['brk'], 'L1_attn_Wrv': _L1_attn_in['Wrv'], 'L1_attn_brv': _L1_attn_in['brv'], 'L1_attn_Wg': _L1_attn_in['Wg'], 'L1_attn_bg': _L1_attn_in['bg'], 'L1_ffn_centroids': _L1_ffn_in['centroids'], 'L1_ffn_expert_biases': _L1_ffn_in['expert_biases'], 'L1_ffn_Wr': _L1_ffn_in['Wr'], 'L1_ffn_br': _L1_ffn_in['br'], 'L1_ffn_Ws': _L1_ffn_in['Ws'], 'L1_ffn_bs': _L1_ffn_in['bs'], 'L2_attn_A_log': _L2_attn_in['A_log'], 'L2_attn_B_w': _L2_attn_in['B_w'], 'L2_attn_B_b': _L2_attn_in['B_b'], 'L2_attn_C_w': _L2_attn_in['C_w'], 'L2_attn_C_b': _L2_attn_in['C_b'], 'L2_attn_norm_g': _L2_attn_in['norm_g'], 'L2_attn_norm_b': _L2_attn_in['norm_b'], 'L2_attn_ff1_w': _L2_attn_in['ff1_w'], 'L2_attn_ff1_b': _L2_attn_in['ff1_b'], 'L2_attn_ff2_w': _L2_attn_in['ff2_w'], 'L2_attn_ff2_b': _L2_attn_in['ff2_b'], 'L2_attn_ta_w': _L2_attn_in['ta_w'], 'L2_attn_ta_b': _L2_attn_in['ta_b'], 'L2_attn_tb_w': _L2_attn_in['tb_w'], 'L2_attn_tb_b': _L2_attn_in['tb_b'], 'L2_attn_out_w': _L2_attn_in['out_w'], 'L2_attn_out_b': _L2_attn_in['out_b'], 'L2_ffn_fast_b': _L2_ffn_in['fast_b'], 'L2_ffn_w_fc': _L2_ffn_in['w_fc'], 'L2_ffn_w_proj': _L2_ffn_in['w_proj'], 'L2_ffn_u': _L2_ffn_in['u'], 'L2_ffn_v': _L2_ffn_in['v'], 'L2_ffn_gate': _L2_ffn_in['gate'], 'L3_attn_W_in': _L3_attn_in['W_in'], 'L3_attn_conv_w': _L3_attn_in['conv_w'], 'L3_attn_conv_b': _L3_attn_in['conv_b'], 'L3_attn_dt_bias': _L3_attn_in['dt_bias'], 'L3_attn_A_log': _L3_attn_in['A_log'], 'L3_attn_D': _L3_attn_in['D'], 'L3_attn_gate_norm_w': _L3_attn_in['gate_norm_w'], 'L3_attn_W_out': _L3_attn_in['W_out'], 'L3_attn_block_norm_w': _L3_attn_in['block_norm_w'], 'L3_attn_final_norm_w': _L3_attn_in['final_norm_w'], 'L3_ffn_gate_weight': _L3_ffn_in['gate_weight'], 'L3_ffn_gate_up_proj': _L3_ffn_in['gate_up_proj'], 'L3_ffn_down_proj': _L3_ffn_in['down_proj'], 'L3_ffn_similarity_matrix': _L3_ffn_in['similarity_matrix']}
    _x0 = _d['L0_attn_x']
    _d['L0_attn_x'] = jax.random.normal(jax.random.fold_in(jax.random.key(seed), 1), (4, 512, 128), dtype=_x0.dtype)
    del _x0
    return _d

def reference(L0_attn_x, L0_attn_W_in, L0_attn_b_in, L0_attn_in_ln_w, L0_attn_in_ln_b, L0_attn_W_out, L0_attn_out_ln_w, L0_attn_out_ln_b, L0_attn_smear_factor, L0_attn_log_scale, L0_ffn_w_gate, L0_ffn_w_in, L0_ffn_w_out, L1_attn_past_states, L1_attn_Wq, L1_attn_bq, L1_attn_Wk, L1_attn_bk, L1_attn_Wv, L1_attn_bv, L1_attn_Wo, L1_attn_bo, L1_attn_Wrq, L1_attn_brq, L1_attn_Wrk, L1_attn_brk, L1_attn_Wrv, L1_attn_brv, L1_attn_Wg, L1_attn_bg, L1_ffn_centroids, L1_ffn_expert_biases, L1_ffn_Wr, L1_ffn_br, L1_ffn_Ws, L1_ffn_bs, L2_attn_A_log, L2_attn_B_w, L2_attn_B_b, L2_attn_C_w, L2_attn_C_b, L2_attn_norm_g, L2_attn_norm_b, L2_attn_ff1_w, L2_attn_ff1_b, L2_attn_ff2_w, L2_attn_ff2_b, L2_attn_ta_w, L2_attn_ta_b, L2_attn_tb_w, L2_attn_tb_b, L2_attn_out_w, L2_attn_out_b, L2_ffn_fast_b, L2_ffn_w_fc, L2_ffn_w_proj, L2_ffn_u, L2_ffn_v, L2_ffn_gate, L3_attn_W_in, L3_attn_conv_w, L3_attn_conv_b, L3_attn_dt_bias, L3_attn_A_log, L3_attn_D, L3_attn_gate_norm_w, L3_attn_W_out, L3_attn_block_norm_w, L3_attn_final_norm_w, L3_ffn_gate_weight, L3_ffn_gate_up_proj, L3_ffn_down_proj, L3_ffn_similarity_matrix):

    def _L0_attn_ref(x, W_in, b_in, in_ln_w, in_ln_b, W_out, out_ln_w, out_ln_b, smear_factor, log_scale):
        import jax, jax.numpy as jnp
        import numpy as np
        HEADS = 16
        D_MODEL = 128
        EXPANSION = 2
        D_EXP = D_MODEL * EXPANSION
        D_HEAD = D_EXP // HEADS
        B, SEQ = (1, 256)
        LN_EPS = 1e-05
        NEG_BIG = -10000000000.0

        def layer_norm(x, w, b):
            mu = jnp.mean(x, axis=-1, keepdims=True)
            var = jnp.var(x, axis=-1, keepdims=True)
            return (x - mu) * jax.lax.rsqrt(var + LN_EPS) * w + b
        b, i, d = x.shape
        xn = layer_norm(x, in_ln_w, in_ln_b)
        proj = xn @ W_in.T + b_in
        q, k, v, p, y = jnp.split(proj, [D_EXP, 2 * D_EXP, 3 * D_EXP, 4 * D_EXP], axis=-1)
        to_heads = lambda t: t.reshape(b, i, HEADS, D_HEAD).transpose(0, 2, 1, 3)
        q, k, v = (to_heads(q), to_heads(k), to_heads(v))
        smear = jax.nn.sigmoid(smear_factor)[None, :, None, None]
        k_prev = jnp.pad(k, ((0, 0), (0, 0), (1, 0), (0, 0)))[:, :, :-1, :]
        k = (1 - smear) * k + smear * k_prev
        s = jnp.exp(log_scale)[None, :, None, None]
        pos = jnp.cumsum(jax.nn.sigmoid(y).transpose(0, 2, 1), axis=-1)
        relpos = pos[..., :, None] - pos[..., None, :]
        causal = jnp.triu(jnp.full((i, i), NEG_BIG, dtype=x.dtype), k=1)
        mask = causal - relpos
        scores = jnp.einsum('bhid,bhjd->bhij', q / s, k / s) / np.sqrt(D_HEAD) + mask
        attn = jax.nn.softmax(scores, axis=-1)
        o = jnp.einsum('bhij,bhjd->bhid', attn, v)
        o = o.transpose(0, 2, 1, 3).reshape(b, i, D_EXP)
        out = jax.nn.silu(p) * o @ W_out.T
        return layer_norm(out, out_ln_w, out_ln_b)

    def _L0_ffn_ref(x, w_gate, w_in, w_out):
        import jax, jax.numpy as jnp
        import numpy as np
        D_MODEL = 128
        HIDDEN = 512
        NUM_EXPERTS = 8
        TOP_K = 2
        B, S, D = x.shape
        E = w_in.shape[0]
        xt = x.reshape(-1, D)
        logits = (xt @ w_gate.T).astype(jnp.float32)
        top_logits, top_idx = jax.lax.top_k(logits, TOP_K)
        top_gates = jax.nn.softmax(top_logits, axis=-1).astype(x.dtype)
        gates = (jax.nn.one_hot(top_idx, E, dtype=x.dtype) * top_gates[..., None]).sum(axis=1)
        y = jnp.zeros_like(xt)
        for e in range(E):
            h = xt @ w_in[e].T
            y = y + gates[:, e:e + 1] * (h @ w_out[e].T)
        return y.reshape(B, S, D)

    def _L1_attn_ref(hidden_states, past_states, Wq, bq, Wk, bk, Wv, bv, Wo, bo, Wrq, brq, Wrk, brk, Wrv, brv, Wg, bg):
        import jax, jax.numpy as jnp
        import numpy as np
        B, S, H, NH, P = (1, 256, 128, 16, 2)
        D = H // NH
        SCALE = 1.0 / np.sqrt(D).astype(np.float32)

        def _lin(x, W, b):
            return x @ W + b

        def _split_heads(x):
            return x.reshape(*x.shape[:-2], x.shape[-2], NH, D).swapaxes(-3, -2)

        def _merge_heads(x):
            return x.swapaxes(-3, -2).reshape(*x.shape[:-3], x.shape[-2], H)
        q = _split_heads(_lin(hidden_states, Wq, bq))
        k = _split_heads(_lin(hidden_states, Wk, bk))
        v = _split_heads(_lin(hidden_states, Wv, bv))
        scores = jnp.einsum('bhsd,bhtd->bhst', q, k) * SCALE
        attn = jax.nn.softmax(scores, axis=-1)
        ctx = jnp.einsum('bhst,bhtd->bhsd', attn, v)
        output = _lin(_merge_heads(ctx), Wo, bo)
        rq = _split_heads(_lin(output, Wrq, brq))
        rk = _split_heads(_lin(past_states, Wrk, brk))
        rv = _split_heads(_lin(past_states, Wrv, brv))
        rscores = jnp.einsum('bhsd,pbhtd->pbhst', rq, rk) * SCALE
        rattn = jax.nn.softmax(rscores, axis=-1)
        rctx = jnp.einsum('pbhst,pbhtd->pbhsd', rattn, rv)
        recursive_output = _merge_heads(rctx).mean(axis=0)
        gate = jax.nn.sigmoid(_lin(jnp.concatenate([output, recursive_output], axis=-1), Wg, bg))
        output = output * (1.0 - gate) + recursive_output * gate
        return output

    def _L1_ffn_ref(u, centroids, expert_biases, Wr, br, Ws, bs):
        import jax, jax.numpy as jnp
        import numpy as np
        TOP_K = 2
        N_r = centroids.shape[0]
        N_s = Ws.shape[0]
        raw_scores = jnp.einsum('bsd,ed->bse', u, centroids)
        s = jax.nn.softmax(raw_scores + expert_biases, axis=-1)
        topk_vals, topk_idx = jax.lax.top_k(s, TOP_K)
        g_topk = jnp.sum(jax.nn.one_hot(topk_idx, N_r, dtype=s.dtype) * topk_vals[..., None], axis=-2)
        xe = jnp.einsum('bsd,eod->bseo', u, Wr) + br
        routed = jnp.einsum('bse,bseo->bso', g_topk, xe)
        shared = (jnp.einsum('bsd,eod->bso', u, Ws) + jnp.sum(bs, axis=0)) / N_s
        return u + routed + shared

    def _L2_attn_ref(x, A_log, B_w, B_b, C_w, C_b, norm_g, norm_b, ff1_w, ff1_b, ff2_w, ff2_b, ta_w, ta_b, tb_w, tb_b, out_w, out_b):
        import jax, jax.numpy as jnp
        import numpy as np
        B, S, D, N, H = (4, 512, 128, 128, 64)
        TIME_DELTA = 0.1
        LN_EPS = 1e-05

        def _reference_tuple_inner(x, A_log, B_w, B_b, C_w, C_b, norm_g, norm_b, ff1_w, ff1_b, ff2_w, ff2_b, ta_w, ta_b, tb_w, tb_b, out_w, out_b):
            mu = x.mean(-1, keepdims=True)
            var = ((x - mu) ** 2).mean(-1, keepdims=True)
            xn = (x - mu) * jax.lax.rsqrt(var + LN_EPS) * norm_g + norm_b
            A = jax.nn.sigmoid(A_log)
            B_all = jnp.einsum('bsd,nd->bsn', xn, B_w) + B_b
            powers = jnp.arange(x.shape[1], dtype=x.dtype)[:, None]
            A_pow = A[None, :] ** powers
            A_safe = jnp.maximum(A_pow, 1e-08)
            states = A_pow[None] * jnp.cumsum(B_all / A_safe[None], axis=1)
            ssm_out = jnp.einsum('bsn,dn->bsd', states, C_w) + C_b
            final_ssm_state = states[:, -1, :]

            def step(h, xt):
                cat = jnp.concatenate([xt, h], axis=-1)
                ff1 = jnp.tanh(cat @ ff1_w.T + ff1_b)
                ff2 = jnp.tanh(cat @ ff2_w.T + ff2_b)
                t_i = jax.nn.sigmoid((cat @ ta_w.T + ta_b) * TIME_DELTA + (cat @ tb_w.T + tb_b))
                h_new = ff1 * (1.0 - t_i) + t_i * ff2
                return (h_new, h_new)
            h0 = jnp.zeros((x.shape[0], ff1_w.shape[0]), x.dtype)
            h_last, cfc_seq = jax.lax.scan(step, h0, jnp.swapaxes(ssm_out, 0, 1))
            cfc_out = jnp.swapaxes(cfc_seq, 0, 1)
            layer_out = x + cfc_out @ out_w.T + out_b
            return (layer_out, final_ssm_state, h_last)
        return _reference_tuple_inner(x, A_log, B_w, B_b, C_w, C_b, norm_g, norm_b, ff1_w, ff1_b, ff2_w, ff2_b, ta_w, ta_b, tb_w, tb_b, out_w, out_b)[0]

    def _L2_ffn_ref(x, fast_b, w_fc, w_proj, u, v, gate):
        import jax, jax.numpy as jnp
        import numpy as np

        def _bitlinear(x, w_latent):
            scale = jax.lax.stop_gradient(jnp.clip(jnp.mean(jnp.abs(w_latent), axis=1, keepdims=True), 1e-05, None))
            tern = jnp.clip(jnp.round(w_latent / scale), -1.0, 1.0)
            w = w_latent + jax.lax.stop_gradient(tern - w_latent)
            return x @ (w * scale).T
        h = _bitlinear(x, w_fc) + gate * (x @ v.T @ fast_b.T @ u.T)
        r = jnp.maximum(h, 0.0)
        return _bitlinear(r * r, w_proj)

    def _L3_attn_ref(x, W_in, conv_w, conv_b, dt_bias, A_log, D, gate_norm_w, W_out, block_norm_w, final_norm_w):
        import jax, jax.numpy as jnp
        import numpy as np
        D_MODEL = 128
        N_LAYER = 4
        EXPAND = 2
        HEADDIM = 32
        D_STATE = 128
        D_CONV = 4
        NGROUPS = 1
        D_INNER = EXPAND * D_MODEL
        NHEADS = D_INNER // HEADDIM
        CONV_DIM = D_INNER + 2 * NGROUPS * D_STATE
        D_IN_PROJ = 2 * D_INNER + 2 * NGROUPS * D_STATE + NHEADS
        BATCH, SEQLEN = (4, 256)

        def _rmsnorm(x, w, eps=1e-05):
            return x * jax.lax.rsqrt(jnp.mean(x * x, axis=-1, keepdims=True) + eps) * w

        def _mamba2_layer(h, Wi, cw, cb, dtb, Alog, Dh, gw, Wo):
            B, L, _ = h.shape
            zxbcdt = h @ Wi
            z, xBC, dt = jnp.split(zxbcdt, [D_INNER, D_INNER + CONV_DIM], axis=-1)
            xp = jnp.pad(xBC, ((0, 0), (D_CONV - 1, 0), (0, 0)))
            conv = cb + sum((xp[:, k:k + L, :] * cw[:, k] for k in range(D_CONV)))
            xBC = jax.nn.silu(conv)
            xs, Bm, Cm = jnp.split(xBC, [D_INNER, D_INNER + D_STATE], axis=-1)
            xs = xs.reshape(B, L, NHEADS, HEADDIM)
            dt = jax.nn.softplus(dt + dtb)
            A = -jnp.exp(Alog)
            dA = jnp.exp(dt * A)
            dtx = dt[..., None] * xs

            def step(hs, inp):
                dA_t, dtx_t, B_t, C_t = inp
                hs = hs * dA_t[:, :, None, None] + dtx_t[..., None] * B_t[:, None, None, :]
                y = jnp.einsum('bhpn,bn->bhp', hs, C_t)
                return (hs, y)
            h0 = jnp.zeros((B, NHEADS, HEADDIM, D_STATE), h.dtype)
            _, ys = jax.lax.scan(step, h0, (dA.swapaxes(0, 1), dtx.swapaxes(0, 1), Bm.swapaxes(0, 1), Cm.swapaxes(0, 1)))
            y = ys.swapaxes(0, 1) + Dh[None, None, :, None] * xs
            y = y.reshape(B, L, D_INNER)
            y = _rmsnorm(y * jax.nn.silu(z), gw)
            return y @ Wo
        h = x
        for l in range(N_LAYER):
            h = h + _mamba2_layer(_rmsnorm(h, block_norm_w[l]), W_in[l], conv_w[l], conv_b[l], dt_bias[l], A_log[l], D[l], gate_norm_w[l], W_out[l])
        return _rmsnorm(h, final_norm_w)

    def _L3_ffn_ref(hidden_states, gate_weight, gate_up_proj, down_proj, similarity_matrix):
        import jax, jax.numpy as jnp
        import numpy as np
        E = 8
        K = 2
        S = 1
        THRESHOLD = 0.7
        NORM_TOPK = True
        H = 128
        F = 128
        B, SEQ = (2, 128)
        b, s, h = hidden_states.shape
        x = hidden_states.reshape(-1, h)
        N = x.shape[0]
        logits = x @ gate_weight.T
        probs = jax.nn.softmax(logits.astype(jnp.float32), axis=-1)
        top_w, top_i = jax.lax.top_k(probs, K)
        if NORM_TOPK:
            top_w = top_w / jnp.clip(jnp.sum(top_w, -1, keepdims=True), 1e-12)
        primary_mask = jnp.zeros((E,), bool).at[top_i[:, :S].reshape(-1)].set(True)
        sim = jnp.where(primary_mask[None, :], similarity_matrix.astype(jnp.float32), -jnp.inf)
        best_j = jnp.argmax(sim, axis=-1)
        best_sim = jnp.max(sim, axis=-1)
        ids = jnp.arange(E)
        expert_map = jnp.where(~primary_mask & (best_sim >= THRESHOLD), best_j, ids)
        rerouted = expert_map[top_i]
        rows = jnp.arange(N)[:, None]
        dense = jnp.zeros((N, E), top_w.dtype).at[rows, rerouted].add(top_w)
        fw, fi = jax.lax.top_k(dense, K)
        combine = jnp.zeros((N, E), fw.dtype).at[rows, fi].add(jnp.where(fw > 0, fw, 0.0))
        gu = jnp.einsum('nh,efh->enf', x, gate_up_proj)
        g, u = jnp.split(gu, 2, axis=-1)
        hmid = jax.nn.silu(g) * u
        y = jnp.einsum('enf,ehf->enh', hmid, down_proj)
        out = jnp.einsum('ne,enh->nh', combine, y)
        return out.reshape(b, s, h)
    x = L0_attn_x
    x = _layernorm(x + _L0_attn_ref(x, L0_attn_W_in, L0_attn_b_in, L0_attn_in_ln_w, L0_attn_in_ln_b, L0_attn_W_out, L0_attn_out_ln_w, L0_attn_out_ln_b, L0_attn_smear_factor, L0_attn_log_scale), axis=-1)
    x = _layernorm(x + _L0_ffn_ref(x, L0_ffn_w_gate, L0_ffn_w_in, L0_ffn_w_out), axis=-1)
    x = _layernorm(x + _L1_attn_ref(x, L1_attn_past_states, L1_attn_Wq, L1_attn_bq, L1_attn_Wk, L1_attn_bk, L1_attn_Wv, L1_attn_bv, L1_attn_Wo, L1_attn_bo, L1_attn_Wrq, L1_attn_brq, L1_attn_Wrk, L1_attn_brk, L1_attn_Wrv, L1_attn_brv, L1_attn_Wg, L1_attn_bg), axis=-1)
    x = _layernorm(x + _L1_ffn_ref(x, L1_ffn_centroids, L1_ffn_expert_biases, L1_ffn_Wr, L1_ffn_br, L1_ffn_Ws, L1_ffn_bs), axis=-1)
    x = _layernorm(x + _L2_attn_ref(x, L2_attn_A_log, L2_attn_B_w, L2_attn_B_b, L2_attn_C_w, L2_attn_C_b, L2_attn_norm_g, L2_attn_norm_b, L2_attn_ff1_w, L2_attn_ff1_b, L2_attn_ff2_w, L2_attn_ff2_b, L2_attn_ta_w, L2_attn_ta_b, L2_attn_tb_w, L2_attn_tb_b, L2_attn_out_w, L2_attn_out_b), axis=-1)
    x = _layernorm(x + _L2_ffn_ref(x, L2_ffn_fast_b, L2_ffn_w_fc, L2_ffn_w_proj, L2_ffn_u, L2_ffn_v, L2_ffn_gate), axis=-1)
    x = _layernorm(x + _L3_attn_ref(x, L3_attn_W_in, L3_attn_conv_w, L3_attn_conv_b, L3_attn_dt_bias, L3_attn_A_log, L3_attn_D, L3_attn_gate_norm_w, L3_attn_W_out, L3_attn_block_norm_w, L3_attn_final_norm_w), axis=-1)
    x = _layernorm(x + _L3_ffn_ref(x, L3_ffn_gate_weight, L3_ffn_gate_up_proj, L3_ffn_down_proj, L3_ffn_similarity_matrix), axis=-1)
    return x

_drawn_inputs = setup_inputs


def setup_inputs(seed=0):
    import zlib

    import numpy as np

    out = dict(_drawn_inputs(seed))
    spreads = {'L0_attn_in_ln_w': (1.0, 0.2),
     'L0_attn_in_ln_b': (0.0, 0.1),
     'L0_attn_out_ln_w': (1.0, 0.2),
     'L0_attn_out_ln_b': (0.0, 0.1),
     'L0_attn_log_scale': (0.0, 0.8),
     'L1_attn_bq': (0.0, 0.8),
     'L1_attn_bk': (0.0, 0.8),
     'L1_attn_bv': (0.0, 0.1),
     'L1_attn_bo': (0.0, 0.1),
     'L1_attn_brq': (0.0, 0.8),
     'L1_attn_brk': (0.0, 0.8),
     'L1_attn_brv': (0.0, 0.1),
     'L1_attn_bg': (0.0, 0.8),
     'L1_ffn_expert_biases': (0.0, 0.364),
     'L2_attn_B_b': (0.0, 0.8),
     'L2_attn_C_b': (0.0, 0.8),
     'L2_attn_norm_g': (1.0, 0.6),
     'L2_attn_norm_b': (0.0, 0.8),
     'L2_attn_ff1_b': (0.0, 0.8),
     'L2_attn_ff2_b': (0.0, 0.8),
     'L2_attn_ta_b': (0.0, 0.8),
     'L2_attn_tb_b': (0.0, 0.8),
     'L2_attn_out_b': (0.0, 0.1),
     'L3_attn_conv_b': (0.0, 0.1),
     'L3_attn_D': (1.0, 0.2),
     'L3_attn_gate_norm_w': (1.0, 0.2),
     'L3_attn_block_norm_w': (1.0, 0.2),
     'L3_attn_final_norm_w': (1.0, 0.2)}
    factors = {'L0_ffn_w_gate': 8.0,
     'L0_ffn_w_in': 8.0,
     'L0_ffn_w_out': 8.0,
     'L1_attn_past_states': 3.489,
     'L1_attn_Wq': 8.0,
     'L1_attn_Wk': 8.0,
     'L1_attn_Wv': 7.29,
     'L1_attn_Wrq': 8.0,
     'L1_attn_Wrk': 8.0,
     'L1_attn_Wrv': 4.796,
     'L1_attn_Wg': 8.0,
     'L1_ffn_br': 8.0,
     'L1_ffn_bs': 8.0,
     'L2_attn_A_log': 8.0,
     'L2_attn_B_w': 8.0,
     'L2_attn_C_w': 8.0,
     'L2_attn_ff1_w': 8.0,
     'L2_attn_ff2_w': 8.0,
     'L2_attn_ta_w': 8.0,
     'L2_attn_tb_w': 8.0,
     'L2_attn_out_w': 6.295,
     'L2_ffn_fast_b': 8.0,
     'L2_ffn_w_fc': 3.367,
     'L2_ffn_u': 8.0,
     'L2_ffn_v': 8.0,
     'L3_ffn_gate_weight': 8.0,
     'L3_ffn_gate_up_proj': 8.0,
     'L3_ffn_down_proj': 8.0}
    for name, (base, spread) in spreads.items():
        noise = np.random.default_rng([zlib.crc32(name.encode()), seed]).standard_normal(out[name].shape)
        drawn = base * np.exp(spread * noise) if base else spread * noise
        out[name] = jnp.asarray(drawn.astype(out[name].dtype))
    for name, factor in factors.items():
        out[name] = (out[name] * factor).astype(out[name].dtype)
    return out
```

```python
from contextlib import ExitStack

import concourse.bass as bass
from concourse import mybir

P = 128
BATCH, SEQ, D = 4, 512, 128
TOK = BATCH * SEQ
TILES = TOK // P
QT = SEQ // P
BANK = 512
EPS = 1e-5
MASKED = -1e30

HEADS = 16
L0_DH = 16
L0_EXP = HEADS * L0_DH
L1_DH = D // HEADS
PAST_SETS, PAST = 2, 256
PARTS = 3

MOE0_E, MOE0_H = 8, 512
MOE1_E, MOE1_S = 16, 2
RNN_H = 64
BIT_H, BIT_R = 512, 16
M_LAYERS, M_INNER, M_STATE, M_HEADS, M_HD, M_CONV = 4, 256, 128, 8, 32, 4
M_PROJ = 2 * M_INNER + 2 * M_STATE + M_HEADS
MOE3_E, MOE3_F = 8, 128
THRESHOLD = 0.7

F32 = mybir.dt.float32
BF16 = mybir.dt.bfloat16
ALU = mybir.AluOpType
ACT = mybir.ActivationFunctionType
AX = mybir.AxisListType

QUERY_PART = (0, 0, 1, 1, 0, 2)
KEY_PART = (0, 1, 0, 1, 2, 0)
PAIRS = len(QUERY_PART)


class Core:

    def __init__(self, nc, ctx, dram):
        self.nc, self.dram = nc, dram
        self.X = ctx.enter_context(nc.sbuf_tensor("X", [P, TILES, D], F32))
        self.XT = ctx.enter_context(nc.sbuf_tensor("XT", [P, TOK], F32))
        self.ps = ctx.enter_context(nc.psum_tensor("ps", [P, 8, BANK], F32))
        self.ident = ctx.enter_context(nc.sbuf_tensor("ident", [P, P], F32))
        self.ident_bf = ctx.enter_context(nc.sbuf_tensor("ident_bf", [P, P], BF16))
        self.mask_q = ctx.enter_context(nc.sbuf_tensor("mask_q", [P, P], BF16))
        self.mask_k = ctx.enter_context(nc.sbuf_tensor("mask_k", [P, P], BF16))
        self.w_routed = ctx.enter_context(nc.sbuf_tensor("w_routed", [P, MOE1_E * D], F32))
        self.w_routed_in = nc.alloc_semaphore(name="w_routed_in")
        self.stored = nc.alloc_semaphore(name="stored")
        self.tri = ctx.enter_context(nc.sbuf_tensor("tri", [P, P], F32))
        self.all_ones = ctx.enter_context(nc.sbuf_tensor("all_ones", [P, P], F32))
        self.half_neg = ctx.enter_context(nc.sbuf_tensor("half_neg", [P, TILES], F32))


class Scope:

    def __init__(self, core, name):
        self.nc, self.name, self.ctx, self.sems = core.nc, name, ExitStack(), []

    def __enter__(self):
        self.ctx.__enter__()
        return self

    def __exit__(self, *a):
        if self.sems:
            self.nc.clear_and_free_semaphores(self.sems)
            self.nc.all_engine_barrier()
        return self.ctx.__exit__(*a)

    def sb(self, name, shape, dt=F32):
        return self.ctx.enter_context(self.nc.sbuf_tensor(f"{self.name}_{name}", shape, dt))

    def sem(self, name):
        self.sems.append(self.nc.alloc_semaphore(name=f"{self.name}_{name}"))
        return self.sems[-1]

    def block(self):
        return self.nc.Block()


class Chain:

    def __init__(self, eng, sem):
        self.eng, self.sem, self.n = eng, sem, 0

    def __call__(self, ins):
        self.n += 1
        ins.then_inc(self.sem, 1)
        self.eng.wait_ge(self.sem, self.n)

    def mark(self, ins):
        self.n += 1
        ins.then_inc(self.sem, 1)

    def wait(self):
        self.eng.wait_ge(self.sem, self.n)


def norm_tokens(v, pool_done, ve_done, chain, src, dst, stats, mv, rstd):
    for t in range(TILES):
        chain.mark(v.bn_stats(stats[:, t, :], src[:, t, :]))
    chain.wait()
    for t in range(TILES):
        last = v.bn_aggr(mv[:, t, :], stats[:, t, :])
        if t < TILES - 1:
            chain.mark(last)
    last.then_inc(ve_done, 1)
    v.wait_ge(pool_done, 2)
    for t in range(TILES):
        v.tensor_scalar(dst[:, t, :], src[:, t, :], mv[:, t, 0:1], rstd[:, t:t + 1],
                        ALU.subtract, ALU.mult).then_inc(ve_done, 1)


def rstd_tokens(g, core, pool_done, ve_done, mv, rstd):
    g.wait_ge(ve_done, 1)
    g.tensor_scalar(rstd[:], mv[:, :, 1], EPS, None, ALU.add).then_inc(pool_done, 1)
    g.wait_ge(pool_done, 1)
    g.tensor_tensor(rstd[:], rstd[:], core.half_neg[:], ALU.pow).then_inc(pool_done, 1)


def prepare(core):
    d = core.dram
    with Scope(core, "prep") as s:
        masks = s.sb("masks", [P, 2, P])
        loaded = s.sem("loaded")
        made = s.sem("made")
        with s.block() as block:
            @block.sync
            def _(sp):
                sp.dma_start(core.X[:], d["L0_attn_x"].rearrange("b (q p) d -> p (b q) d", p=P)).then_inc(loaded, 16)
                sp.dma_start(core.ident[:], d["ident"]).then_inc(loaded, 16)
                sp.dma_start(masks[:], d["masks"].rearrange("m p n -> p m n")).then_inc(loaded, 16)
                sp.dma_start(core.w_routed[:], d["moe1_wT"]).then_inc(core.w_routed_in, 16)
                sp.wait_ge(loaded, 48)

            @block.vector
            def _(v):
                v.memset(core.half_neg[:], -0.5).then_inc(made, 1)
                v.wait_ge(loaded, 48)
                v.tensor_copy(core.ident_bf[:], core.ident[:]).then_inc(made, 1)
                v.tensor_copy(core.mask_q[:], masks[:, 0, :]).then_inc(made, 1)
                v.tensor_copy(core.mask_k[:], masks[:, 1, :]).then_inc(made, 1)


def l0_project(core, buf, scr):
    nc, d = core.nc, core.dram
    V, G = buf["V"], buf["gate"]
    with Scope(core, "l0p") as s:
        w = s.sb("w", [P, 4 * L0_EXP + HEADS])
        bias_y = s.sb("bias_y", [HEADS, 1])
        bias_vp = s.sb("bias_vp", [P, 2 * L0_EXP])
        cols = s.sb("cols", [P, 10])
        lnw, hp, bias_qk = cols[:, 0:2], cols[:, 2:6], cols[:, 6:10]
        qs = s.sb("qs", [P, 2])
        bq = s.sb("bq", [P, 2])
        sm = s.sb("sm", [P, 2])
        oms = s.sb("oms", [P, 2])
        stats = s.sb("stats", [P, TILES, 6])
        mv = s.sb("mv", [P, TILES, 2])
        rstd = s.sb("rstd", [P, TILES])
        xn = s.sb("xn", [P, TILES, D])
        xnT = s.sb("xnT", [P, TOK])
        qk = s.sb("qk", [P, 2, 4, SEQ])
        kraw = s.sb("kraw", [P, 2, SEQ])
        parts = s.sb("parts", [P, 2, PARTS, 4, SEQ], BF16)
        yv = s.sb("yv", [HEADS, TOK])
        ones = s.sb("ones", [HEADS, SEQ])
        pos = s.sb("pos", [HEADS, TOK])
        pparts = s.sb("pparts", [HEADS, PARTS, TOK], BF16)
        loaded, loaded2 = s.sem("loaded"), s.sem("loaded2")
        ve_done, pool_done, chain_s = s.sem("ve_done"), s.sem("pool_done"), s.sem("ve_chain")
        act_chain = s.sem("act_chain")
        transposed, xnT_ready = s.sem("transposed"), s.sem("xnT_ready")
        proj_done = s.sem("proj_done")
        q_ready, hi_done, rest_done = s.sem("q_ready"), s.sem("hi_done"), s.sem("rest_done")
        mid_done, lo_done = s.sem("mid_done"), s.sem("lo_done")
        y_ready, scales = s.sem("y_ready"), s.sem("scales")
        written = [s.sem(f"written{b}") for b in range(BATCH)]
        pos_written = s.sem("pos_written")
        k_ready, pos_hi, pos_rest = s.sem("k_ready"), s.sem("pos_hi"), s.sem("pos_rest")
        gates_in = s.sem("gates_in")
        pos_mid, pos_lo, v_ready = s.sem("pos_mid"), s.sem("pos_lo"), s.sem("v_ready")
        PER = 9

        def bank(n):
            return core.ps[:, 4 + n % 4, :]

        def wait_read(pe, n):
            b, j = divmod(n, PER)
            if j < 2:
                pe.wait_ge(q_ready, 2 * b + j + 1)
            elif j < 4:
                pe.wait_ge(k_ready, 2 * b + j - 1)
            elif j == 4:
                pe.wait_ge(y_ready, b + 1)
            else:
                pe.wait_ge(v_ready, QT * b + j - 4)

        with s.block() as block:
            @block.sync
            def _(sp):
                sp.dma_start(cols[:], d["l0_cols"]).then_inc(loaded, 16)
                sp.dma_start(bias_y[:], d["L0_attn_b_in"][4 * L0_EXP:].rearrange("(p c) -> p c", c=1)).then_inc(loaded, 16)
                sp.dma_start(w[:], d["l0_w_inT"]).then_inc(loaded2, 16)
                sp.dma_start(bias_vp[:], d["L0_attn_b_in"][2 * L0_EXP:4 * L0_EXP].rearrange("(a n) -> a n", a=1).broadcast_to([P, 2 * L0_EXP])).then_inc(loaded2, 16)
                for b in range(BATCH):
                    sp.wait_ge(lo_done, b + 1)
                    sp.dma_start(scr["qk"][b].rearrange("j (c p) t -> p (j c) t", p=P), parts[:, b % 2, :, :, :].rearrange("p j c t -> p (j c) t")).then_inc(written[b], 16)
                sp.wait_ge(pos_lo, 1)
                sp.dma_start(scr["pos"].rearrange("j b h t -> h (j b) t"), pparts[:].rearrange("h j (b t) -> h (j b) t", b=BATCH)).then_inc(pos_written, 16)
                sp.wait_ge(pos_written, 16)
                for b in range(BATCH):
                    sp.wait_ge(written[b], 16)

            @block.tensor
            def _(pe):
                for t in range(TILES):
                    pe.wait_ge(ve_done, t + 2)
                    m = pe.transpose(core.ps[:, t // 4, (t % 4) * P:(t % 4) * P + P], xn[:, t, :], core.ident[:])
                    if t % 4 == 3:
                        m.then_inc(transposed, 1)
                pe.wait_ge(loaded2, 32)
                for b in range(BATCH):
                    pe.wait_ge(xnT_ready, b + 1)
                    xb = xnT[:, b * SEQ:(b + 1) * SEQ]
                    for j in range(PER):
                        n = b * PER + j
                        if n >= 4:
                            wait_read(pe, n - 4)
                        out = bank(n)
                        if j < 4:
                            pe.matmul(out, w[:, j * P:(j + 1) * P], xb, start=True, stop=True).then_inc(proj_done, 1)
                        elif j == 4:
                            pe.matmul(out[0:HEADS, :], w[:, 4 * L0_EXP:], xb, start=True, stop=True).then_inc(proj_done, 1)
                        else:
                            q = j - 5
                            pe.matmul(out, xb[:, q * P:(q + 1) * P], w[:, 2 * L0_EXP:4 * L0_EXP], start=True, stop=True).then_inc(proj_done, 1)

            @block.scalar
            def _(a):
                own = Chain(a, act_chain)
                a.wait_ge(loaded, 32)
                a.activation(qs[:], hp[:, 0:2], ACT.Exp, scale=-2.0).then_inc(scales, 1)
                a.activation(sm[:], hp[:, 2:4], ACT.Sigmoid).then_inc(scales, 1)
                for g in range(4):
                    a.wait_ge(transposed, g + 1)
                    a.activation(xnT[:, g * BANK:(g + 1) * BANK], core.ps[:, g, :], ACT.Identity, scale=lnw[:, 0:1], bias=lnw[:, 1:2]).then_inc(xnT_ready, 1)
                a.wait_ge(gates_in, 1)
                for b in range(BATCH):
                    for j in (0, 1):
                        n = b * PER + j
                        a.wait_ge(proj_done, n + 1)
                        if b >= 2:
                            a.wait_ge(rest_done, b - 1)
                            a.wait_ge(hi_done, b - 1)
                        a.activation(qk[:, b % 2, j, :], bank(n), ACT.Identity, scale=qs[:, j:j + 1], bias=bq[:, j:j + 1]).then_inc(q_ready, 1)
                    n = b * PER + 4
                    a.wait_ge(proj_done, n + 1)
                    a.activation(yv[:, b * SEQ:(b + 1) * SEQ], bank(n)[0:HEADS, :], ACT.Sigmoid, bias=bias_y[:]).then_inc(y_ready, 1)
                    a.wait_ge(k_ready, 2 * b + 2)
                    a.wait_ge(q_ready, 2 * b + 2)
                    if b >= 2:
                        a.wait_ge(written[b - 2], 16)
                    a.activation(parts[:, b % 2, 0, :, :], qk[:, b % 2, :, :], ACT.Copy).then_inc(hi_done, 1)
                    a.wait_ge(rest_done, b + 1)
                    a.activation(parts[:, b % 2, 1, :, :], qk[:, b % 2, :, :], ACT.Copy).then_inc(mid_done, 1)
                a.wait_ge(pos_rest, 4)
                a.activation(pparts[:, 0, :], pos[:], ACT.Copy).then_inc(pos_hi, 1)
                a.wait_ge(pos_rest, 5)
                a.activation(pparts[:, 1, :], pos[:], ACT.Copy).then_inc(pos_mid, 1)
                a.wait_ge(v_ready, TILES)
                a.activation(G[:], G[:], ACT.Silu).then_inc(own.sem, 1)

            @block.gpsimd
            def _(g):
                rstd_tokens(g, core, pool_done, ve_done, mv, rstd)

            @block.vector
            def _(v):
                own = Chain(v, chain_s)
                own.mark(v.memset(ones[:], 1.0))
                own.mark(v.memset(V[:, :, :, L0_DH:L0_DH + 1], 1.0))
                norm_tokens(v, pool_done, ve_done, own, core.X, xn, stats, mv, rstd)
                v.wait_ge(scales, 2)
                own(v.tensor_scalar(qs[:], qs[:], float(L0_DH) ** -0.5, None, ALU.mult))
                own(v.tensor_scalar(oms[:], sm[:], -1.0, 1.0, ALU.mult, ALU.add))
                v.tensor_tensor(bq[:], qs[:], bias_qk[:, 0:2], ALU.mult).then_inc(gates_in, 1)
                v.wait_ge(loaded2, 32)
                for b in range(BATCH):
                    for j in (2, 3):
                        n = b * PER + j
                        c = j - 2
                        v.wait_ge(proj_done, n + 1)
                        own(v.tensor_scalar(kraw[:, c, :], bank(n), bias_qk[:, j:j + 1], None, ALU.add))
                        own(v.tensor_scalar(qk[:, b % 2, j, :], kraw[:, c, :], oms[:, c:c + 1], None, ALU.mult))
                        v.scalar_tensor_tensor(out=qk[:, b % 2, j, 1:], in0=kraw[:, c, 0:SEQ - 1], scalar=sm[:, c:c + 1], in1=qk[:, b % 2, j, 1:], op0=ALU.mult, op1=ALU.add).then_inc(k_ready, 1)
                    for j in range(5, PER):
                        n = b * PER + j
                        t = b * QT + j - 5
                        v.wait_ge(proj_done, n + 1)
                        out = bank(n)
                        own.mark(v.tensor_tensor(V[:, t, :, 0:L0_DH], out[:, 0:L0_EXP].rearrange("p (h e) -> p h e", h=HEADS), bias_vp[:, 0:L0_EXP].rearrange("p (h e) -> p h e", h=HEADS), ALU.add))
                        v.tensor_tensor(G[:, t, :], out[:, L0_EXP:], bias_vp[:, L0_EXP:], ALU.add).then_inc(v_ready, 1)
                    v.wait_ge(hi_done, b + 1)
                    v.tensor_tensor(qk[:, b % 2, :, :], qk[:, b % 2, :, :], parts[:, b % 2, 0, :, :], ALU.subtract).then_inc(rest_done, 1)
                    v.wait_ge(mid_done, b + 1)
                    v.wait_ge(rest_done, b + 1)
                    v.tensor_tensor(parts[:, b % 2, 2, :, :], qk[:, b % 2, :, :], parts[:, b % 2, 1, :, :], ALU.subtract).then_inc(lo_done, 1)
                v.wait_ge(y_ready, BATCH)
                for b in range(BATCH):
                    v.tensor_tensor_scan(pos[:, b * SEQ:(b + 1) * SEQ], ones[:], yv[:, b * SEQ:(b + 1) * SEQ], 0.0, ALU.mult, ALU.add).then_inc(pos_rest, 1)
                v.wait_ge(pos_rest, 4)
                v.wait_ge(pos_hi, 1)
                v.tensor_tensor(pos[:], pos[:], pparts[:, 0, :], ALU.subtract).then_inc(pos_rest, 1)
                v.wait_ge(pos_rest, 5)
                v.wait_ge(pos_mid, 1)
                v.tensor_tensor(pparts[:, 2, :], pos[:], pparts[:, 1, :], ALU.subtract).then_inc(pos_lo, 1)


class Plan:
    pass


def causal_plan():
    p = Plan()
    p.dh, p.kinds, p.keys = L0_DH, 1, SEQ
    p.rows = [(q, 0, (q + 1) * P, True, 0) for q in range(QT)]
    p.cols = [[(0, 0, 0, 0, 512, True), (1, 0, 1, 128, 384, True), (1, 384, 3, 384, 128, True)],
              [(2, 0, 2, 256, 256, True)]]
    p.exps = [(0, 1024, 0), (2, 256, 1024)]
    p.accs = 1
    return p


def full_plan():
    p = Plan()
    p.dh, p.kinds, p.keys = L1_DH, 1, SEQ
    p.rows = [(q, 0, SEQ, False, 0) for q in range(QT)]
    p.cols = [[(0, 0, 0, 0, 512, False), (1, 0, 1, 0, 512, False)],
              [(2, 0, 2, 0, 512, False), (3, 0, 3, 0, 512, False)]]
    p.exps = [(0, 1024, 0), (2, 1024, 1024)]
    p.accs = 1
    return p


def recursive_plan():
    p = full_plan()
    p.kinds = PAST_SETS
    p.rows = [(q, 0, SEQ, False, None) for q in range(QT)]
    p.accs = PAST_SETS
    return p


def attention(core, name, plan, scr, V, O):
    nc = core.nc
    DH = plan.dh
    W = DH + 1
    SETS = plan.kinds
    NR = len(plan.rows)
    base = PAIRS * DH
    POS = PARTS if name == "l0a" else 0
    RA = base + POS
    RB = RA + PARTS * SETS
    COLS = 1280 if name == "l0a" else 2048
    NMX = QT * SETS
    U = 4 // SETS
    shared = SETS == 2
    with Scope(core, name) as s:
        QS = s.sb("QS", [RB, 2, HEADS, SEQ], BF16)
        NK = 1 if shared else 2
        KS = s.sb("KS", [RB, NK, HEADS, SEQ], BF16)
        set_rows = s.sb("set_rows", [SETS, SEQ], BF16) if shared else None
        set_rows32 = s.sb("set_rows32", [SETS, SEQ]) if shared else None
        sets_in, sets_made = s.sem("sets_in"), s.sem("sets_made")
        table_in = s.sem("table_in")
        warm = s.sb("warm", [1, 1])
        mx = s.sb("mx", [P, NMX, HEADS])
        nm = s.sb("nm", [HEADS, NMX * P])
        mparts = s.sb("mparts", [HEADS, PARTS, NMX * P], BF16)
        PT = s.sb("PT", [P, 2, COLS])
        VS = s.sb("VS", [P, 2, QT, 32])
        ST = s.sb("ST", [P, SEQ])
        den = s.sb("den", [P, QT, 4])
        tmp = s.sb("tmp", [P, QT, U, SETS, DH]) if shared else None
        loaded_q = [s.sem(f"queries_in{i}") for i in range(2)]
        loaded_k = [s.sem(f"keys_in{i}") for i in range(2)]
        filled = s.sem("filled")
        maxima_in = s.sem("maxima_in")
        row_scores, row_max = s.sem("row_scores"), s.sem("row_max")
        turned, negated = s.sem("maxima_turned"), s.sem("maxima_negated")
        m_hi, m_rest, m_mid, m_split = s.sem("m_hi"), s.sem("m_rest"), s.sem("m_mid"), s.sem("m_split")
        scored, weighed = s.sem("scored"), s.sem("weighed")
        staged, valued, taken, turned_out = s.sem("values_staged"), s.sem("valued"), s.sem("sums_taken"), s.sem("sums_turned")
        padded, normed, recips, halves = s.sem("padded"), s.sem("normed"), s.sem("recips"), s.sem("halves")
        row_banks = [0, 1]

        def queries(sp, b):
            for g, part in enumerate(QUERY_PART):
                sp.dma_start(QS[g * DH:(g + 1) * DH, b % 2, :, :], scr["qk"][b, part, 0:HEADS * DH].rearrange("(h e) t -> e h t", e=DH)).then_inc(loaded_q[b % 2], 16)

        def keys(sp, b):
            for g, part in enumerate(KEY_PART):
                sp.dma_start(KS[g * DH:(g + 1) * DH, b % NK, :, :], scr["qk"][b if not shared else 0, part, HEADS * DH:].rearrange("(h e) t -> e h t", e=DH)).then_inc(loaded_k[b % 2], 16)
            for j in range(POS):
                sp.dma_start(KS[base + j:base + j + 1, b % NK, :, :], scr["pos"][j:j + 1, b]).then_inc(loaded_k[b % 2], 16)

        K_DMAS = PAIRS + POS
        with s.block() as block:
            @block.sync
            def _(sp):
                ones = core.dram["ones"].unsqueeze(1)
                for i in range(2):
                    sp.dma_start(QS[base:RB, i, :, :], ones.broadcast_to([RB - base, HEADS, SEQ])).then_inc(filled, 16)
                for i in range(NK):
                    sp.dma_start(KS[base:RB, i, :, :], ones.broadcast_to([RB - base, HEADS, SEQ])).then_inc(filled, 16)
                sp.wait_ge(filled, 16 * (2 + NK))
                if shared:
                    sp.dma_start(set_rows32[:], core.dram["set_rows"]).then_inc(sets_in, 16)

                def loads(b):
                    if b >= 2:
                        sp.wait_ge(scored, (b - 1) * HEADS * 2)
                    queries(sp, b)
                    if not shared or b == 0:
                        keys(sp, b)
                    if shared and b == 0:
                        sp.wait_ge(sets_made, 1)
                        for k in range(SETS):
                            for j in range(PARTS):
                                r = RA + PARTS * k + j
                                sp.dma_start(KS[r:r + 1, 0, :, :], set_rows[k:k + 1, :].unsqueeze(1).broadcast_to([1, HEADS, SEQ])).then_inc(loaded_k[0], 16)

                loads(0)
                for b in range(BATCH):
                    if b < 1:
                        loads(b + 1)
                    sp.wait_ge(m_split, b + 1)
                    for k in range(SETS):
                        for j in range(PARTS):
                            r = RA + PARTS * k + j
                            sp.dma_start(QS[r:r + 1, b % 2, :, :], mparts[:, j, k * SEQ:(k + 1) * SEQ]).then_inc(maxima_in, 16)
                    if 1 <= b < BATCH - 1:
                        loads(b + 1)

            @block.tensor
            def _(pe):
                pe.wait_ge(filled, 16 * (2 + NK))

                def rows(b, h, n):
                    for i, (q, k0, kn, masked, _) in enumerate(plan.rows):
                        if i >= 2 or not (isinstance(n, int) and n == 0):
                            pe.wait_ge(row_max, n * NR + i - 1)
                        out = core.ps[:, row_banks[i % 2], 0:kn]
                        m = pe.matmul(out, QS[0:RA, b % 2, h, q * P:(q + 1) * P], KS[0:RA, b % NK, h, k0:k0 + kn], start=True, stop=not masked)
                        if masked:
                            m = pe.matmul(out[:, kn - P:kn], core.ident_bf[:], core.mask_q[:], start=False, stop=True)
                        m.then_inc(row_scores, 1)

                def turn(b):
                    pe.wait_ge(row_max, (b + 1) * HEADS * NR)
                    for i in range(NMX):
                        m = pe.transpose(core.ps[0:HEADS, i // 4, (i % 4) * P:(i % 4 + 1) * P], mx[:, i, :], core.ident[:])
                    m.then_inc(turned, 1)

                def weigh(b, h, par, n):
                    for g, group in enumerate(plan.cols):
                        if not (isinstance(n, int) and n == 0):
                            pe.wait_ge(weighed, 2 * n + (g - 1))
                        for slot, col, kt, q0, qn, masked in group:
                            out = core.ps[:, 2 + slot, col:col + qn]
                            m = pe.matmul(out, KS[0:RB, b % NK, h, kt * P:(kt + 1) * P], QS[0:RB, b % 2, h, q0:q0 + qn], start=True, stop=not masked)
                            if masked:
                                m = pe.matmul(out[:, 0:P], core.ident_bf[:], core.mask_k[:], start=False, stop=True)
                        m.then_inc(scored, 1)

                def values(j, par, n, m):
                    if j == 0 and not (isinstance(m, int) and m == 0):
                        pe.wait_ge(taken, m)
                    pe.wait_ge(staged, n + 1)
                    for g, group in enumerate(plan.cols):
                        pe.wait_ge(weighed, 2 * n + (g + 1))
                        for slot, col, kt, q0, qn, masked in group:
                            off = plan.exps[g][2] + (slot - plan.exps[g][0]) * BANK + col
                            kset = kt // 2 if shared else 0
                            r = 32 * (j * SETS + kset)
                            lead = kt % 2 == 0 if shared else kt == 0
                            tail = kt % 2 == 1 if shared else (g == 1 and (slot, col, kt, q0, qn, masked) == group[-1])
                            mm = pe.matmul(core.ps[r:r + 32, 6, q0:q0 + qn], VS[:, par, kt, :], PT[:, par, off:off + qn], start=lead, stop=tail, skip_group_check=True)
                    mm.then_inc(valued, 1)

                def turn_out(m):
                    pe.wait_ge(taken, m + 1)
                    if not (isinstance(m, int) and m == 0):
                        pe.wait_ge(normed, m)
                    for q in range(QT):
                        mm = pe.transpose(core.ps[:, 7, q * P:(q + 1) * P], ST[:, q * P:(q + 1) * P], core.ident[:])
                    mm.then_inc(turned_out, 1)

                def turn_in(b):
                    pe.wait_ge(maxima_in, 16 * PARTS * SETS * (b + 1))

                KW = 16 * K_DMAS + (16 * PARTS * SETS if shared else 0)
                pe.wait_ge(loaded_q[0], 16 * PAIRS)
                pe.wait_ge(loaded_k[0], KW)
                rows(0, 0, 0)
                with pe.Fori(1, HEADS) as h:
                    rows(0, h, h)
                turn(0)
                for b in range(BATCH):
                    turn_in(b)
                    last = b == BATCH - 1
                    if not last:
                        pe.wait_ge(loaded_q[(b + 1) % 2], 16 * PAIRS * ((b + 1) // 2 + 1))
                        if not shared:
                            pe.wait_ge(loaded_k[(b + 1) % 2], 16 * K_DMAS * ((b + 1) // 2 + 1))
                        pe.wait_ge(negated, b + 1)

                    def quad(i):
                        for j in range(U):
                            h = U * i + j
                            n = h + b * HEADS
                            m = i + b * HEADS // U
                            weigh(b, h, j % 2, n)
                            if not last:
                                rows(b + 1, h, n + HEADS)
                            if j == 1 and not (isinstance(m, int) and m == 0):
                                turn_out(m - 1)
                            if j > 0:
                                values(j - 1, (j - 1) % 2, n - 1, m)
                            elif not (isinstance(n, int) and n == 0):
                                values(U - 1, 1, n - 1, m - 1)

                    if b == 0:
                        quad(0)
                    with pe.Fori(1 if b == 0 else 0, HEADS // U) as i:
                        quad(i)
                    if last:
                        values(U - 1, 1, BATCH * HEADS - 1, BATCH * HEADS // U - 1)
                        turn_out(BATCH * HEADS // U - 1)
                    if not last:
                        turn(b + 1)

            @block.scalar
            def _(a):
                def exps(par, n):
                    for g, (slot, cols, at) in enumerate(plan.exps):
                        a.wait_ge(scored, 2 * n + (g + 1))
                        if not (isinstance(n, int) and n < 2):
                            a.wait_ge(valued, n - 1)
                        if cols > BANK:
                            a.activation(PT[:, par, at:at + cols].rearrange("p (s n) -> p s n", s=2), core.ps[:, 2 + slot:4 + slot, :], ACT.Exp).then_inc(weighed, 1)
                        else:
                            a.activation(PT[:, par, at:at + cols], core.ps[:, 2 + slot, 0:cols], ACT.Exp).then_inc(weighed, 1)

                def take(m):
                    a.wait_ge(valued, U * m + U)
                    if not (isinstance(m, int) and m == 0):
                        a.wait_ge(turned_out, m)
                    a.activation(ST[:], core.ps[:, 6, :], ACT.Copy).then_inc(taken, 1)

                def negate(b):
                    a.wait_ge(turned, b + 1)
                    if b >= 1:
                        a.wait_ge(m_split, b)
                    a.activation(nm[:].rearrange("p (s n) -> p s n", s=SETS), core.ps[0:HEADS, 0:SETS, :], ACT.Copy, scale=-1.0).then_inc(negated, 1)
                    a.wait_ge(negated, b + 1)
                    if b >= 1:
                        a.wait_ge(maxima_in, 16 * PARTS * SETS * b)
                    a.activation(mparts[:, 0, :], nm[:], ACT.Copy).then_inc(m_hi, 1)
                    a.wait_ge(m_rest, b + 1)
                    a.activation(mparts[:, 1, :], nm[:], ACT.Copy).then_inc(m_mid, 1)

                a.activation(warm[:], core.half_neg[0:1, 0:1], ACT.Exp).then_inc(table_in, 1)
                negate(0)
                for b in range(BATCH):
                    def quad(i):
                        for j in range(U):
                            n = U * i + (j + b * HEADS)
                            m = i + b * HEADS // U
                            exps(j % 2, n)
                            if j == 0 and not (isinstance(m, int) and m == 0):
                                take(m - 1)

                    if b == 0:
                        quad(0)
                    with a.Fori(1 if b == 0 else 0, HEADS // U) as i:
                        quad(i)
                    if b == BATCH - 1:
                        take(BATCH * HEADS // U - 1)
                    if b < BATCH - 1:
                        negate(b + 1)

            @block.gpsimd
            def _(g):
                g.memset(VS[:], 0.0).then_inc(padded, 1)
                g.wait_ge(padded, 1)

                def stage(b, h, par, n):
                    if not (isinstance(n, int) and n < 2):
                        g.wait_ge(valued, n - 1)
                    g.tensor_copy(VS[:, par, :, 0:W], V[:, 0 if shared else b * QT:QT if shared else (b + 1) * QT, h, :]).then_inc(staged, 1)

                stage(0, 0, 0, 0)
                stage(0, 1, 1, 1)
                for b in range(BATCH):
                    with g.Fori(1 if b == 0 else 0, HEADS // 2) as i:
                        for par in range(2):
                            stage(b, 2 * i + par, par, 2 * i + (par + b * HEADS))

            @block.vector
            def _(v):
                if shared:
                    v.wait_ge(sets_in, 16)
                    v.tensor_copy(set_rows[:], set_rows32[:]).then_inc(sets_made, 1)

                def maxima(h, n):
                    for i, (q, k0, kn, _, _) in enumerate(plan.rows):
                        v.wait_ge(row_scores, n * NR + i + 1)
                        src = core.ps[:, row_banks[i % 2], 0:kn]
                        if shared:
                            out = mx[:, :, bass.ds(h, 1)].rearrange("p (k q) o -> p k q o", k=SETS)[:, :, q, 0]
                            v.tensor_reduce(out, src.rearrange("p (k n) -> p k n", k=SETS), AX.X, ALU.max).then_inc(row_max, 1)
                        else:
                            v.tensor_reduce(mx[:, i, bass.ds(h, 1)], src, AX.X, ALU.max).then_inc(row_max, 1)

                def norm(b, i, m):
                    v.wait_ge(turned_out, m + 1)
                    acc = core.ps[:, 7, :].rearrange("p (q j c) -> p q j c", q=QT, j=4)
                    v.reciprocal(den[:], acc[:, :, :, DH]).then_inc(recips, 1)
                    v.wait_ge(recips, m + 1)
                    out = O[:, b * QT:(b + 1) * QT, bass.ds(i * (U * DH), U * DH)].rearrange("p q (j e) -> p q j e", j=U)
                    over = den[:].unsqueeze(3).broadcast_to([P, QT, 4, DH])
                    if not shared:
                        v.tensor_tensor(out, acc[:, :, :, 0:DH], over, ALU.mult).then_inc(normed, 1)
                    else:
                        v.tensor_tensor(tmp[:].rearrange("p q j k e -> p q (j k) e"), acc[:, :, :, 0:DH], over, ALU.mult).then_inc(normed, 1)
                        v.wait_ge(normed, m + 1)
                        v.tensor_tensor(out, tmp[:, :, :, 0], tmp[:, :, :, 1], ALU.add).then_inc(halves, 1)

                def split(b):
                    v.wait_ge(m_hi, b + 1)
                    v.tensor_tensor(nm[:], nm[:], mparts[:, 0, :], ALU.subtract).then_inc(m_rest, 1)
                    v.wait_ge(m_rest, b + 1)
                    v.wait_ge(m_mid, b + 1)
                    v.tensor_tensor(mparts[:, 2, :], nm[:], mparts[:, 1, :], ALU.subtract).then_inc(m_split, 1)

                with v.Fori(0, HEADS) as h:
                    maxima(h, h)
                split(0)
                for b in range(BATCH):
                    last = b == BATCH - 1

                    def quad(i):
                        for j in range(U):
                            m = i + b * HEADS // U
                            if not last:
                                h = U * i + j
                                maxima(h, h + (b + 1) * HEADS)
                            if j == 1 and not (isinstance(m, int) and m == 0):
                                if isinstance(i, int):
                                    norm(b if i else b - 1, (i - 1) % (HEADS // U), m - 1)
                                else:
                                    norm(b, i - 1, m - 1)

                    quad(0)
                    with v.Fori(1, HEADS // U) as i:
                        quad(i)
                    if last:
                        norm(b, HEADS // U - 1, BATCH * HEADS // U - 1)
                    if not last:
                        split(b + 1)


def l0_finish(core, buf):
    d = core.dram
    V, G, O = buf["V"], buf["gate"], buf["O"]
    with Scope(core, "l0f") as s:
        wo = s.sb("wo", [P, 2, D])
        ln = s.sb("ln", [P, 2, D])
        gT = s.sb("gT", [P, 4, 2, P])
        y = s.sb("y", [P, TILES, D])
        stats = s.sb("stats", [P, TILES, 6])
        mv = s.sb("mv", [P, TILES, 2])
        rstd = s.sb("rstd", [P, TILES])
        loaded, gated, turned, copied = s.sem("loaded"), s.sem("gated"), s.sem("turned"), s.sem("copied")
        made, taken = s.sem("made"), s.sem("taken")
        ve_done, pool_done, chain_s = s.sem("ve_done"), s.sem("pool_done"), s.sem("ve_chain")
        ve_done2, pool_done2 = s.sem("ve_done2"), s.sem("pool_done2")
        with s.block() as block:
            @block.sync
            def _(sp):
                sp.dma_start(wo[:], d["l0_w_outT"].rearrange("(c p) n -> p c n", p=P)).then_inc(loaded, 16)
                sp.dma_start(ln[:], d["l0_out_ln"].rearrange("(a c) n -> a c n", a=1).broadcast_to([P, 2, D])).then_inc(loaded, 16)

            @block.tensor
            def _(pe):
                pe.wait_ge(loaded, 32)

                def project(t):
                    pe.wait_ge(copied, t + 1)
                    if t >= 4:
                        pe.wait_ge(taken, t - 3)
                    for c in range(2):
                        m = pe.matmul(core.ps[:, 4 + t % 4, 0:D], gT[:, t % 4, c, :], wo[:, c, :], start=(c == 0), stop=(c == 1))
                    m.then_inc(made, 1)

                for t in range(TILES):
                    pe.wait_ge(gated, t // 4 + 1)
                    if t >= 4:
                        pe.wait_ge(copied, t - 3)
                    for c in range(2):
                        m = pe.transpose(core.ps[:, t % 4, c * P:(c + 1) * P], G[:, t, c * P:(c + 1) * P], core.ident[:])
                    m.then_inc(turned, 1)
                    if t >= 1:
                        project(t - 1)
                project(TILES - 1)

            @block.scalar
            def _(a):
                for t in range(TILES):
                    a.wait_ge(turned, t + 1)
                    if t >= 4:
                        a.wait_ge(made, t - 3)
                    a.activation(gT[:, t % 4, :, :], core.ps[:, t % 4, 0:2 * P].rearrange("p (c n) -> p c n", c=2), ACT.Copy).then_inc(copied, 1)

            @block.gpsimd
            def _(g):
                rstd_tokens(g, core, pool_done, ve_done, mv, rstd)
                rstd_tokens(g, core, pool_done2, ve_done2, mv, rstd)

            @block.vector
            def _(v):
                own = Chain(v, chain_s)
                for b in range(BATCH):
                    v.tensor_tensor(G[:, b * QT:(b + 1) * QT, :], G[:, b * QT:(b + 1) * QT, :], O[:, b * QT:(b + 1) * QT, :], ALU.mult).then_inc(gated, 1)
                for t in range(TILES):
                    v.wait_ge(made, t + 1)
                    v.tensor_copy(y[:, t, :], core.ps[:, 4 + t % 4, 0:D]).then_inc(taken, 1)
                v.wait_ge(taken, TILES)
                norm_tokens(v, pool_done, ve_done, own, y, y, stats, mv, rstd)
                v.wait_ge(loaded, 32)
                v.wait_ge(ve_done, TILES + 1)
                own(v.tensor_tensor(y[:], y[:], ln[:, 0, :].unsqueeze(1).broadcast_to([P, TILES, D]), ALU.mult))
                own(v.tensor_tensor(y[:], y[:], ln[:, 1, :].unsqueeze(1).broadcast_to([P, TILES, D]), ALU.add))
                own(v.tensor_tensor(y[:], y[:], core.X[:], ALU.add))
                norm_tokens(v, pool_done2, ve_done2, own, y, core.X, stats, mv, rstd)


def store(core, out):
    with core.nc.Block() as block:
        @block.sync
        def _(sp):
            sp.dma_start(out.rearrange("b (q p) d -> p (b q) d", p=P), core.X[:]).then_inc(core.stored, 16)
            sp.wait_ge(core.stored, 16)


def turn_tokens(pe, core, turned, src, free=None):
    for t in range(TILES):
        m = pe.transpose(core.ps[:, t // 4, (t % 4) * P:(t % 4 + 1) * P], src[:, t, :], core.ident[:])
        if t % 4 == 3:
            m.then_inc(turned, 1)


def keep_turned(a, core, turned, kept):
    for g in range(4):
        a.wait_ge(turned, g + 1)
        a.activation(core.XT[:, g * BANK:(g + 1) * BANK], core.ps[:, g, :], ACT.Copy).then_inc(kept, 1)


def pick_two(v, own, rank, vals, work, hots, tops, E):
    key, best = work
    for k in range(2):
        own(v.tensor_reduce(tops[k][:], vals, AX.X, ALU.max))
        own(v.tensor_tensor(key[:], vals, tops[k][:].unsqueeze(2).broadcast_to([P, TILES, E]), ALU.is_equal))
        own(v.tensor_tensor(key[:], key[:], rank[:, 0:E].unsqueeze(1).broadcast_to([P, TILES, E]), ALU.mult))
        own(v.tensor_reduce(best[:], key[:], AX.X, ALU.max))
        own(v.tensor_tensor(hots[k][:], key[:], best[:].unsqueeze(2).broadcast_to([P, TILES, E]), ALU.is_equal))
        if k == 0:
            own(v.scalar_tensor_tensor(out=hots[1][:], in0=hots[0][:], scalar=MASKED, in1=vals, op0=ALU.mult, op1=ALU.add))
            vals = hots[1][:]


def mixture(core, name, E, ws, routed):
    d = core.dram
    H = E // 8
    UNITS = TILES * H
    with Scope(core, name) as s:
        gate_w = s.sb("gate_w", [P, E])
        rank = s.sb("rank", [P, 16])
        L = s.sb("L", [P, TILES, E])
        gates = s.sb("gates", [P, TILES, E])
        hots = [s.sb(f"hot{k}", [P, TILES, E]) for k in range(2)]
        key = s.sb("key", [P, TILES, E])
        best = s.sb("best", [P, TILES])
        tops = [s.sb(f"top{k}", [P, TILES]) for k in range(2)]
        e2 = s.sb("e2", [P, TILES])
        Z = s.sb("Z", [P, 2, 4, D])
        Z2 = s.sb("Z2", [P, 2, 2, D])
        R = s.sb("R", [P, UNITS, D])
        Y = s.sb("Y", [P, TILES, D])
        stats = s.sb("stats", [P, TILES, 6])
        mv = s.sb("mv", [P, TILES, 2])
        rstd = s.sb("rstd", [P, TILES])
        if routed:
            bias = s.sb("bias", [P, E])
            shared_w = s.sb("shared_w", [P, MOE1_S, D])
            shared_b = s.sb("shared_b", [MOE1_S, D])
            expert_b = s.sb("expert_b", [E, D])
            gT = s.sb("gT", [E, TOK])
            two = s.sb("two", [MOE1_S, P])
        loaded = s.sem("loaded")
        turned, kept, scored = s.sem("turned"), s.sem("kept"), s.sem("scored")
        made, weighed_v, weighed_a, added = s.sem("made"), s.sem("weighed_by_v"), s.sem("weighed_by_a"), s.sem("added")
        differ, exped, gated = s.sem("differences"), s.sem("exponentials"), s.sem("gated")
        gates_turned, gates_kept, extra, extra_read = s.sem("gates_turned"), s.sem("gates_kept"), s.sem("extra"), s.sem("extra_read")
        ve_done, pool_done, chain_s, pool_chain, twos = s.sem("ve_done"), s.sem("pool_done"), s.sem("ve_chain"), s.sem("pool_chain"), s.sem("twos")
        LOADS = 6 if routed else 2
        with s.block() as block:
            @block.sync
            def _(sp):
                sp.dma_start(gate_w[:], d["moe1_gateT" if routed else "moe0_gateT"]).then_inc(loaded, 16)
                sp.dma_start(rank[:], d["rank"].broadcast_to([P, 16])).then_inc(loaded, 16)
                if routed:
                    sp.dma_start(bias[:], d["L1_ffn_expert_biases"].rearrange("(a n) -> a n", a=1).broadcast_to([P, E])).then_inc(loaded, 16)
                    sp.dma_start(shared_w[:], d["moe1_sharedT"].rearrange("e i o -> i e o")).then_inc(loaded, 16)
                    sp.dma_start(shared_b[:], d["L1_ffn_bs"]).then_inc(loaded, 16)
                    sp.dma_start(expert_b[:], d["L1_ffn_br"]).then_inc(loaded, 16)

            @block.tensor
            def _(pe):
                turn_tokens(pe, core, turned, core.X)
                pe.wait_ge(loaded, 16 * LOADS)
                for t in range(TILES):
                    pe.wait_ge(kept, t // 4 + 1)
                    m = pe.matmul(core.ps[:, 7, t * E:(t + 1) * E], core.XT[:, t * P:(t + 1) * P], gate_w[:], start=True, stop=True)
                m.then_inc(scored, 1)
                if routed:
                    pe.wait_ge(twos, 1)
                    pe.wait_ge(core.w_routed_in, 16)

                def extras(t):
                    pe.wait_ge(gates_kept, t // 4 + 1)
                    if t >= 1:
                        pe.wait_ge(extra_read, t)
                    x = core.XT[:, t * P:(t + 1) * P]
                    for k in range(MOE1_S):
                        pe.matmul(core.ps[:, 6, 0:D], x, shared_w[:, k, :], start=(k == 0), stop=False)
                    pe.matmul(core.ps[:, 6, 0:D], two[:], shared_b[:], start=False, stop=True)
                    pe.matmul(core.ps[:, 6, D:2 * D], gT[:, t * P:(t + 1) * P], expert_b[:], start=True, stop=True).then_inc(extra, 1)

                for u in range(UNITS):
                    t, h = divmod(u, H)
                    if u >= 3:
                        pe.wait_ge(weighed_v, u - 2)
                        pe.wait_ge(weighed_a, u - 2)
                    for k in range(2):
                        c = (h * 8 + k * 4) * D
                        m = pe.matmul(core.ps[:, 2 * (u % 3) + k, :], core.XT[:, t * P:(t + 1) * P], ws[:, c:c + BANK], start=True, stop=True)
                    m.then_inc(made, 1)
                    if routed and u == 2:
                        pe.wait_ge(gated, 1)
                        for g in range(4):
                            if g:
                                pe.wait_ge(gates_kept, g)
                            for i in range(4):
                                m = pe.transpose(core.ps[0:E, 7, i * P:(i + 1) * P], gates[:, 4 * g + i, :], core.ident[:])
                            m.then_inc(gates_turned, 1)
                    if routed and t >= 2 and h == 1:
                        extras(t - 2)
                if routed:
                    extras(TILES - 2)
                    extras(TILES - 1)

            @block.scalar
            def _(a):
                keep_turned(a, core, turned, kept)
                a.wait_ge(differ, 1)
                if routed:
                    a.activation(L[:], L[:], ACT.Exp).then_inc(exped, 1)
                else:
                    a.activation(e2[:], e2[:], ACT.Exp).then_inc(exped, 1)
                a.wait_ge(gated, 1)
                for u in range(UNITS):
                    t, h = divmod(u, H)
                    if routed and u == 3:
                        for g in range(4):
                            a.wait_ge(gates_turned, g + 1)
                            a.activation(gT[:, g * BANK:(g + 1) * BANK], core.ps[0:E, 7, :], ACT.Copy).then_inc(gates_kept, 1)
                    a.wait_ge(made, u + 1)
                    if u >= 2:
                        a.wait_ge(added, u - 1)
                    for k in range(4):
                        e = h * 8 + 4 + k
                        m = a.activation(Z[:, u % 2, k, :], core.ps[:, 2 * (u % 3) + 1, k * D:(k + 1) * D], ACT.Copy, scale=gates[:, t, e:e + 1])
                    m.then_inc(weighed_a, 1)

            @block.gpsimd
            def _(g):
                own = Chain(g, pool_chain)
                if routed:
                    g.memset(two[:], 1.0).then_inc(twos, 1)
                for u in range(UNITS):
                    g.wait_ge(weighed_a, u + 1)
                    own(g.tensor_tensor(Z2[:, u % 2], Z[:, u % 2, 0:2], Z[:, u % 2, 2:4], ALU.add))
                    g.tensor_tensor(R[:, u, :], Z2[:, u % 2, 0], Z2[:, u % 2, 1], ALU.add).then_inc(added, 1)
                rstd_tokens(g, core, pool_done, ve_done, mv, rstd)

            @block.vector
            def _(v):
                own = Chain(v, chain_s)
                v.wait_ge(loaded, 16 * LOADS)
                v.wait_ge(scored, 1)
                scores = core.ps[:, 7, 0:TILES * E].rearrange("p (t e) -> p t e", e=E)

                def each(x):
                    return x[:].unsqueeze(2).broadcast_to([P, TILES, E])

                if routed:
                    own(v.tensor_tensor(L[:], scores, bias[:].unsqueeze(1).broadcast_to([P, TILES, E]), ALU.add))
                    own(v.tensor_reduce(best[:], L[:], AX.X, ALU.max))
                    v.tensor_tensor(L[:], L[:], each(best), ALU.subtract).then_inc(differ, 1)
                    v.wait_ge(exped, 1)
                    own(v.tensor_reduce(best[:], L[:], AX.X, ALU.add))
                    own(v.reciprocal(best[:], best[:]))
                    own(v.tensor_tensor(L[:], L[:], each(best), ALU.mult))
                    pick_two(v, own, rank, L[:], (key, best), hots, tops, E)
                    own(v.tensor_tensor(hots[0][:], hots[0][:], hots[1][:], ALU.add))
                    v.tensor_tensor(gates[:], hots[0][:], L[:], ALU.mult).then_inc(gated, 1)
                else:
                    own(v.tensor_copy(L[:], scores))
                    pick_two(v, own, rank, L[:], (key, best), hots, tops, E)
                    v.tensor_tensor(e2[:], tops[1][:], tops[0][:], ALU.subtract).then_inc(differ, 1)
                    v.wait_ge(exped, 1)
                    own(v.tensor_scalar(best[:], e2[:], 1.0, None, ALU.add))
                    own(v.reciprocal(tops[0][:], best[:]))
                    own(v.tensor_tensor(tops[1][:], e2[:], tops[0][:], ALU.mult))
                    own(v.tensor_tensor(hots[0][:], hots[0][:], each(tops[0]), ALU.mult))
                    own(v.tensor_tensor(hots[1][:], hots[1][:], each(tops[1]), ALU.mult))
                    v.tensor_tensor(gates[:], hots[0][:], hots[1][:], ALU.add).then_inc(gated, 1)
                v.wait_ge(gated, 1)

                def finish(t):
                    for h in range(H):
                        u = t * H + h
                        v.wait_ge(added, u + 1)
                        own(v.tensor_tensor(Y[:, t, :], Y[:, t, :], R[:, u, :], ALU.add))
                    if routed:
                        v.wait_ge(extra, t + 1)
                        own(v.scalar_tensor_tensor(out=Y[:, t, :], in0=core.ps[:, 6, 0:D], scalar=1.0 / MOE1_S, in1=Y[:, t, :], op0=ALU.mult, op1=ALU.add))
                        v.tensor_tensor(Y[:, t, :], core.ps[:, 6, D:2 * D], Y[:, t, :], ALU.add).then_inc(extra_read, 1)

                if routed:
                    own(v.tensor_scalar(Y[:], core.X[:], 2.0, None, ALU.mult))
                for u in range(UNITS):
                    t, h = divmod(u, H)
                    v.wait_ge(made, u + 1)
                    for k in range(4):
                        e = h * 8 + k
                        into = core.X[:, t, :] if (k == 0 and h == 0 and not routed) else Y[:, t, :]
                        m = v.scalar_tensor_tensor(out=Y[:, t, :], in0=core.ps[:, 2 * (u % 3), k * D:(k + 1) * D], scalar=gates[:, t, e:e + 1], in1=into, op0=ALU.mult, op1=ALU.add)
                        if k < 3:
                            own(m)
                    m.then_inc(weighed_v, 1)
                    v.wait_ge(weighed_v, u + 1)
                    if h == H - 1 and t >= 2:
                        finish(t - 2)
                finish(TILES - 2)
                finish(TILES - 1)
                if routed:
                    v.wait_ge(extra_read, TILES)
                norm_tokens(v, pool_done, ve_done, own, Y, core.X, stats, mv, rstd)


def experts0(core, M):
    d = core.dram
    with Scope(core, "ex0") as s:
        w_in = s.sb("w_in", [P, MOE0_E, 4, D])
        w_out = s.sb("w_out", [P, MOE0_E, 4, D])
        loaded = [s.sem(f"loaded{e}") for e in range(4)]
        made, kept = s.sem("made"), s.sem("kept")
        with s.block() as block:
            @block.sync
            def _(sp):
                for g in range(4):
                    es = slice(2 * g, 2 * g + 2)
                    sp.dma_start(w_in[:, es].rearrange("p e c i -> p (e c) i"), d["L0_ffn_w_in"][es].rearrange("e (c p) i -> p (e c) i", p=P)).then_inc(loaded[g], 16)
                    sp.dma_start(w_out[:, es].rearrange("p e c i -> p (e c) i"), d["moe0_w_outT"][es].rearrange("e (c p) o -> p (e c) o", p=P)).then_inc(loaded[g], 16)

            @block.tensor
            def _(pe):
                for e in range(MOE0_E):
                    pe.wait_ge(loaded[e // 2], 32)
                    for c in range(4):
                        m = pe.matmul(core.ps[:, e // 4, (e % 4) * D:(e % 4 + 1) * D], w_in[:, e, c, :], w_out[:, e, c, :], start=(c == 0), stop=(c == 3))
                    if e % 4 == 3:
                        m.then_inc(made, 1)

            @block.scalar
            def _(a):
                for g in range(2):
                    a.wait_ge(made, g + 1)
                    a.activation(M[:, g * BANK:(g + 1) * BANK], core.ps[:, g, :], ACT.Copy).then_inc(kept, 1)


class Split:

    def __init__(self, s, chunks, batches=BATCH):
        self.src = s.sb("split_src", [P, 2, chunks, SEQ])
        self.parts = s.sb("split_parts", [P, 2, PARTS, chunks, SEQ], BF16)
        self.hi, self.rest, self.mid, self.low = (s.sem(f"split_{n}") for n in ("hi", "rest", "mid", "low"))
        self.written = [s.sem(f"split_written{b}") for b in range(batches)]

    def may_fill(self, eng, b):
        if b >= 2:
            eng.wait_ge(self.low, b - 1)

    def scalar(self, a, b):
        if b >= 2:
            a.wait_ge(self.written[b - 2], 16)
        a.activation(self.parts[:, b % 2, 0], self.src[:, b % 2], ACT.Copy).then_inc(self.hi, 1)
        a.wait_ge(self.rest, b + 1)
        a.activation(self.parts[:, b % 2, 1], self.src[:, b % 2], ACT.Copy).then_inc(self.mid, 1)

    def vector(self, v, b):
        v.wait_ge(self.hi, b + 1)
        v.tensor_tensor(self.src[:, b % 2], self.src[:, b % 2], self.parts[:, b % 2, 0], ALU.subtract).then_inc(self.rest, 1)
        v.wait_ge(self.rest, b + 1)
        v.wait_ge(self.mid, b + 1)
        v.tensor_tensor(self.parts[:, b % 2, 2], self.src[:, b % 2], self.parts[:, b % 2, 1], ALU.subtract).then_inc(self.low, 1)

    def store(self, sp, b, dst):
        sp.wait_ge(self.low, b + 1)
        sp.dma_start(dst.rearrange("j (c p) t -> p (j c) t", p=P), self.parts[:, b % 2].rearrange("p j c t -> p (j c) t")).then_inc(self.written[b], 16)

    def stored(self, sp):
        for w in self.written:
            sp.wait_ge(w, 16)


L1_SCALE = float(L1_DH) ** -0.5


def l1_project(core, V, RV, scr, rscr):
    d = core.dram
    JOBS = BATCH + 1
    with Scope(core, "l1p") as s:
        w = s.sb("w", [P, 5, D])
        cols = s.sb("cols", [P, 3])
        rows = s.sb("rows", [P, 2, D])
        pastT = s.sb("pastT", [P, PAST_SETS * PAST])
        bq = s.sb("bq", [P, 1])
        sp_ = Split(s, 2, JOBS)
        loaded, turned, kept, scaled = s.sem("loaded"), s.sem("turned"), s.sem("kept"), s.sem("scaled")
        made, filled, vals, chain_s = s.sem("made"), s.sem("filled"), s.sem("values"), s.sem("ve_chain")
        with s.block() as block:
            @block.sync
            def _(sp):
                sp.dma_start(w[:], d["l1_w"].rearrange("k p n -> p k n")).then_inc(loaded, 16)
                sp.dma_start(cols[:], d["l1_cols"]).then_inc(loaded, 16)
                sp.dma_start(rows[:], d["l1_rows"].rearrange("(a c) n -> a c n", a=1).broadcast_to([P, 2, D])).then_inc(loaded, 16)
                sp.dma_start(pastT[:], d["pastT"]).then_inc(loaded, 16)
                for b in range(JOBS):
                    sp_.store(sp, b, scr[b] if b < BATCH else rscr[0])
                sp_.stored(sp)

            @block.tensor
            def _(pe):
                turn_tokens(pe, core, turned, core.X)
                pe.wait_ge(loaded, 64)
                for b in range(JOBS):
                    if b < BATCH:
                        pe.wait_ge(kept, b + 1)
                        x, wk, wv, which = core.XT[:, b * SEQ:(b + 1) * SEQ], w[:, 1], w[:, 2], (0, 1)
                    else:
                        x, wk, wv, which = pastT[:], w[:, 3], w[:, 4], (3,)
                    if b >= 1:
                        pe.wait_ge(filled, 2 * b)
                        pe.wait_ge(vals, b)
                    for k in which:
                        pe.matmul(core.ps[:, 4 + min(k, 1), :], w[:, k, :], x, start=True, stop=True).then_inc(made, 1)
                    for q in range(QT):
                        m = pe.matmul(core.ps[:, 6, q * P:(q + 1) * P], x[:, q * P:(q + 1) * P], wv, start=True, stop=True)
                    m.then_inc(made, 1)

            @block.scalar
            def _(a):
                a.wait_ge(loaded, 64)
                a.activation(bq[:], cols[:, 0:1], ACT.Copy, scale=L1_SCALE).then_inc(scaled, 1)
                keep_turned(a, core, turned, kept)
                a.wait_ge(scaled, 1)
                for b in range(BATCH):
                    sp_.may_fill(a, b)
                    a.wait_ge(made, 3 * b + 1)
                    a.activation(sp_.src[:, b % 2, 0], core.ps[:, 4, :], ACT.Identity, scale=L1_SCALE, bias=bq[:]).then_inc(filled, 1)
                    a.wait_ge(made, 3 * b + 2)
                    a.activation(sp_.src[:, b % 2, 1], core.ps[:, 5, :], ACT.Identity, bias=cols[:, 1:2]).then_inc(filled, 1)
                    a.wait_ge(filled, 2 * b + 2)
                    sp_.scalar(a, b)
                b = BATCH
                sp_.may_fill(a, b)
                a.wait_ge(made, 3 * b + 1)
                for c in range(2):
                    a.activation(sp_.src[:, b % 2, c], core.ps[:, 5, :], ACT.Identity, bias=cols[:, 2:3]).then_inc(filled, 1)
                a.wait_ge(filled, 2 * b + 2)
                sp_.scalar(a, b)

            @block.vector
            def _(v):
                own = Chain(v, chain_s)
                own.mark(v.memset(V[:, :, :, L1_DH:], 1.0))
                own.mark(v.memset(RV[:, :, :, L1_DH:], 1.0))
                v.wait_ge(loaded, 64)
                for b in range(JOBS):
                    v.wait_ge(made, 3 * b + 3 if b < BATCH else 3 * b + 2)
                    out = V[:, b * QT:(b + 1) * QT] if b < BATCH else RV[:]
                    bias = rows[:, 0 if b < BATCH else 1, :].rearrange("p (h e) -> p h e", h=HEADS)
                    for q in range(QT):
                        m = v.tensor_tensor(out[:, q, :, 0:L1_DH], core.ps[:, 6, q * P:(q + 1) * P].rearrange("p (h e) -> p h e", h=HEADS), bias, ALU.add)
                    m.then_inc(vals, 1)
                    sp_.vector(v, b)


def l1_between(core, O, OT, rscr):
    d = core.dram
    with Scope(core, "l1m") as s:
        w = s.sb("w", [P, 2, D])
        cols = s.sb("cols", [P, 2])
        bq = s.sb("bq", [P, 1])
        cT = s.sb("cT", [P, 2, SEQ])
        sp_ = Split(s, 1)
        loaded, scaled, turned, kept = s.sem("loaded"), s.sem("scaled"), s.sem("turned"), s.sem("kept")
        made, outed, made2, filled = s.sem("made"), s.sem("outed"), s.sem("queried"), s.sem("filled")
        with s.block() as block:
            @block.sync
            def _(sp):
                sp.dma_start(w[:], d["l1_w2"].rearrange("k p n -> p k n")).then_inc(loaded, 16)
                sp.dma_start(cols[:], d["l1_cols2"]).then_inc(loaded, 16)
                for b in range(BATCH):
                    sp_.store(sp, b, rscr[b][:, 0:P])
                sp_.stored(sp)

            @block.tensor
            def _(pe):
                pe.wait_ge(loaded, 32)

                def turn(b):
                    if b >= 2:
                        pe.wait_ge(kept, b - 1)
                    for q in range(QT):
                        m = pe.transpose(core.ps[:, b % 2, q * P:(q + 1) * P], O[:, b * QT + q, :], core.ident[:])
                    m.then_inc(turned, 1)

                turn(0)
                for b in range(BATCH):
                    if b < BATCH - 1:
                        turn(b + 1)
                    pe.wait_ge(kept, b + 1)
                    if b >= 2:
                        pe.wait_ge(outed, b - 1)
                    pe.matmul(core.ps[:, 2 + b % 2, :], w[:, 0, :], cT[:, b % 2, :], start=True, stop=True).then_inc(made, 1)
                    pe.wait_ge(outed, b + 1)
                    if b >= 2:
                        pe.wait_ge(filled, b - 1)
                    pe.matmul(core.ps[:, 4 + b % 2, :], w[:, 1, :], OT[:, b * SEQ:(b + 1) * SEQ], start=True, stop=True).then_inc(made2, 1)

            @block.scalar
            def _(a):
                a.wait_ge(loaded, 32)
                a.activation(bq[:], cols[:, 1:2], ACT.Copy, scale=L1_SCALE).then_inc(scaled, 1)
                a.wait_ge(scaled, 1)
                for b in range(BATCH):
                    a.wait_ge(turned, b + 1)
                    if b >= 2:
                        a.wait_ge(made, b - 1)
                    a.activation(cT[:, b % 2, :], core.ps[:, b % 2, :], ACT.Copy).then_inc(kept, 1)
                    a.wait_ge(made, b + 1)
                    a.activation(OT[:, b * SEQ:(b + 1) * SEQ], core.ps[:, 2 + b % 2, :], ACT.Identity, bias=cols[:, 0:1]).then_inc(outed, 1)
                    a.wait_ge(made2, b + 1)
                    sp_.may_fill(a, b)
                    a.activation(sp_.src[:, b % 2, 0], core.ps[:, 4 + b % 2, :], ACT.Identity, scale=L1_SCALE, bias=bq[:]).then_inc(filled, 1)
                    a.wait_ge(filled, b + 1)
                    sp_.scalar(a, b)

            @block.vector
            def _(v):
                for b in range(BATCH):
                    sp_.vector(v, b)


def l1_finish(core, O, OT):
    d = core.dram
    with Scope(core, "l1f") as s:
        w = s.sb("w", [P, 2, D])
        bg = s.sb("bg", [P, 1])
        rT = s.sb("rT", [P, 2, SEQ])
        gate = s.sb("gate", [P, 2, SEQ])
        diff = s.sb("diff", [P, 2, SEQ])
        Y = s.sb("Y", [P, TILES, D])
        stats = s.sb("stats", [P, TILES, 6])
        mv = s.sb("mv", [P, TILES, 2])
        rstd = s.sb("rstd", [P, TILES])
        loaded, turned, kept, made, gated = s.sem("loaded"), s.sem("turned"), s.sem("kept"), s.sem("made"), s.sem("gated")
        mixed, back, chain_s, summed = s.sem("mixed"), s.sem("back"), s.sem("ve_chain"), s.sem("summed")
        ve_done, pool_done = s.sem("ve_done"), s.sem("pool_done")
        with s.block() as block:
            @block.sync
            def _(sp):
                sp.dma_start(w[:], d["L1_attn_Wg"].rearrange("(k p) n -> p k n", p=P)).then_inc(loaded, 16)
                sp.dma_start(bg[:], d["L1_attn_bg"].rearrange("(p a) -> p a", a=1)).then_inc(loaded, 16)

            @block.tensor
            def _(pe):
                pe.wait_ge(loaded, 32)

                def turn(b):
                    if b >= 2:
                        pe.wait_ge(kept, b - 1)
                    for q in range(QT):
                        m = pe.transpose(core.ps[:, b % 2, q * P:(q + 1) * P], O[:, b * QT + q, :], core.ident[:])
                    m.then_inc(turned, 1)

                turn(0)
                for b in range(BATCH):
                    if b < BATCH - 1:
                        turn(b + 1)
                    pe.wait_ge(kept, b + 1)
                    if b >= 2:
                        pe.wait_ge(gated, b - 1)
                    pe.matmul(core.ps[:, 2 + b % 2, :], w[:, 0, :], OT[:, b * SEQ:(b + 1) * SEQ], start=True, stop=False)
                    pe.matmul(core.ps[:, 2 + b % 2, :], w[:, 1, :], rT[:, b % 2, :], start=False, stop=True).then_inc(made, 1)
                    pe.wait_ge(mixed, b + 1)
                    if b >= 2:
                        pe.wait_ge(summed, b - 1)
                    for q in range(QT):
                        m = pe.transpose(core.ps[:, 4 + b % 2, q * P:(q + 1) * P], diff[:, b % 2, q * P:(q + 1) * P], core.ident[:])
                    m.then_inc(back, 1)

            @block.scalar
            def _(a):
                a.wait_ge(loaded, 32)
                for b in range(BATCH):
                    a.wait_ge(turned, b + 1)
                    if b >= 2:
                        a.wait_ge(mixed, b - 1)
                    a.activation(rT[:, b % 2, :], core.ps[:, b % 2, :], ACT.Copy, scale=1.0 / PAST_SETS).then_inc(kept, 1)
                    a.wait_ge(made, b + 1)
                    a.activation(gate[:, b % 2, :], core.ps[:, 2 + b % 2, :], ACT.Sigmoid, bias=bg[:]).then_inc(gated, 1)

            @block.gpsimd
            def _(g):
                rstd_tokens(g, core, pool_done, ve_done, mv, rstd)

            @block.vector
            def _(v):
                own = Chain(v, chain_s)
                for b in range(BATCH):
                    out = OT[:, b * SEQ:(b + 1) * SEQ]
                    v.wait_ge(kept, b + 1)
                    if b >= 2:
                        v.wait_ge(back, b - 1)
                    own(v.tensor_tensor(diff[:, b % 2], rT[:, b % 2], out, ALU.subtract))
                    v.wait_ge(gated, b + 1)
                    own(v.tensor_tensor(diff[:, b % 2], diff[:, b % 2], gate[:, b % 2], ALU.mult))
                    v.tensor_tensor(diff[:, b % 2], diff[:, b % 2], out, ALU.add).then_inc(mixed, 1)
                    v.wait_ge(back, b + 1)
                    v.tensor_tensor(Y[:, b * QT:(b + 1) * QT], core.ps[:, 4 + b % 2, :].rearrange("p (q d) -> p q d", q=QT), core.X[:, b * QT:(b + 1) * QT], ALU.add).then_inc(summed, 1)
                v.wait_ge(summed, BATCH)
                norm_tokens(v, pool_done, ve_done, own, Y, core.X, stats, mv, rstd)


STEPS = 64
COLS = 2 * BATCH


def l2_ssm(core, cat, sign):
    d = core.dram
    with Scope(core, "ssm") as s:
        cols = s.sb("cols", [P, 5])
        bw = s.sb("bw", [P, 2, P])
        A = s.sb("A", [P, 1])
        apow = s.sb("apow", [P, SEQ])
        inv = s.sb("inv", [P, SEQ])
        ones = s.sb("ones", [P, SEQ])
        zeros = s.sb("zeros", [P, SEQ])
        xn = s.sb("xn", [P, TILES, D])
        u = s.sb("u", [P, 2, SEQ])
        cum = s.sb("cum", [P, 2, SEQ])
        states = s.sb("states", [P, 2, SEQ])
        stats = s.sb("stats", [P, TILES, 6])
        mv = s.sb("mv", [P, TILES, 2])
        rstd = s.sb("rstd", [P, TILES])
        loaded, decay, turned, kept, made = s.sem("loaded"), s.sem("decay"), s.sem("turned"), s.sem("kept"), s.sem("made")
        scaled, stated, projected, out_kept = s.sem("scaled"), s.sem("stated"), s.sem("projected"), s.sem("out_kept")
        ve_done, pool_done, chain_s = s.sem("ve_done"), s.sem("pool_done"), s.sem("ve_chain")
        with s.block() as block:
            @block.sync
            def _(sp):
                sp.dma_start(cols[:], d["ssm_cols"]).then_inc(loaded, 16)
                sp.dma_start(bw[:], d["ssm_w"].rearrange("k p n -> p k n")).then_inc(loaded, 16)
                sp.dma_start(sign[:], d["sign"]).then_inc(loaded, 16)

            @block.tensor
            def _(pe):
                for t in range(TILES):
                    pe.wait_ge(ve_done, t + 2)
                    m = pe.transpose(core.ps[:, t // 4, (t % 4) * P:(t % 4 + 1) * P], xn[:, t, :], core.ident[:])
                    if t % 4 == 3:
                        m.then_inc(turned, 1)
                def project(b):
                    pe.wait_ge(stated, b + 1)
                    if b >= 2:
                        pe.wait_ge(out_kept, b - 1)
                    pe.matmul(core.ps[:, 6 + b % 2, :], bw[:, 1, :], states[:, b % 2, :], start=True, stop=True).then_inc(projected, 1)

                pe.wait_ge(loaded, 48)
                for b in range(BATCH):
                    pe.wait_ge(kept, b + 1)
                    if b >= 2:
                        pe.wait_ge(scaled, b - 1)
                    pe.matmul(core.ps[:, 4 + b % 2, :], bw[:, 0, :], core.XT[:, b * SEQ:(b + 1) * SEQ], start=True, stop=True).then_inc(made, 1)
                    if b >= 1:
                        project(b - 1)
                project(BATCH - 1)

            @block.scalar
            def _(a):
                a.wait_ge(loaded, 48)
                a.activation(A[:], cols[:, 4:5], ACT.Sigmoid).then_inc(decay, 1)
                for g in range(4):
                    a.wait_ge(turned, g + 1)
                    a.activation(core.XT[:, g * BANK:(g + 1) * BANK], core.ps[:, g, :], ACT.Identity, scale=cols[:, 0:1], bias=cols[:, 1:2]).then_inc(kept, 1)
                for b in range(BATCH):
                    a.wait_ge(projected, b + 1)
                    a.activation(cat[:, b, 0:SEQ], core.ps[:, 6 + b % 2, :], ACT.Identity, bias=cols[:, 3:4]).then_inc(out_kept, 1)

            @block.gpsimd
            def _(g):
                rstd_tokens(g, core, pool_done, ve_done, mv, rstd)

            @block.vector
            def _(v):
                own = Chain(v, chain_s)
                norm_tokens(v, pool_done, ve_done, own, core.X, xn, stats, mv, rstd)
                own.mark(v.memset(ones[:], 1.0))
                own.mark(v.memset(zeros[:], 0.0))
                own.mark(v.memset(cat[:, :, SEQ:], 0.0))
                own(v.memset(apow[:, 0:1], 1.0))
                v.wait_ge(decay, 1)
                own(v.tensor_tensor_scan(apow[:, 1:], A[:].broadcast_to([P, SEQ - 1]), zeros[:, 1:], 1.0, ALU.mult, ALU.add))
                own(v.tensor_scalar(inv[:], apow[:], 1e-8, None, ALU.max))
                own(v.reciprocal(inv[:], inv[:]))
                for b in range(BATCH):
                    v.wait_ge(made, b + 1)
                    v.scalar_tensor_tensor(out=u[:, b % 2], in0=core.ps[:, 4 + b % 2, :], scalar=cols[:, 2:3], in1=inv[:], op0=ALU.add, op1=ALU.mult).then_inc(scaled, 1)
                    v.wait_ge(scaled, b + 1)
                    own(v.tensor_tensor_scan(cum[:, b % 2], ones[:], u[:, b % 2], 0.0, ALU.mult, ALU.add))
                    if b >= 2:
                        v.wait_ge(projected, b - 1)
                    v.tensor_tensor(states[:, b % 2], cum[:, b % 2], apow[:], ALU.mult).then_inc(stated, 1)


def l2_scan(core, cat, history, rows_sign):
    d = core.dram
    RING = 2 * STEPS
    with Scope(core, "rnn") as s:
        wx = s.sb("wx", [P, 3, P])
        wh = s.sb("wh", [P, 3, P])
        bias = s.sb("bias", [1, 3, P])
        ones = s.sb("ones", [1, STEPS])
        half = s.sb("half", [P, 1])
        ring = s.sb("ring", [P, RING, BATCH])
        act = s.sb("act", [P, 2, COLS])
        warm = s.sb("warm", [P, 1])
        loaded, weights, chain_s = s.sem("loaded"), s.sem("weights"), s.sem("ve_chain")
        summed, bent, stepped, copied, primed = s.sem("summed"), s.sem("bent"), s.sem("stepped"), s.sem("copied"), s.sem("primed")
        with s.block() as block:
            @block.sync
            def _(sp):
                sp.dma_start(wx[:], d["rnn_wx"].rearrange("k p n -> p k n")).then_inc(loaded, 16)
                sp.dma_start(wh[:], d["rnn_wh"].rearrange("k p n -> p k n")).then_inc(loaded, 16)
                sp.dma_start(bias[:], d["rnn_b"].rearrange("(a k) n -> a k n", a=1)).then_inc(loaded, 16)

            @block.tensor
            def _(pe):
                pe.wait_ge(weights, 1)
                pe.wait_ge(copied, 2)

                def inputs(bank, chunk, piece, kind):
                    n = STEPS // 4
                    out = core.ps[:, bank, :].rearrange("p (t c) -> p t c", c=COLS)[:, piece * n:(piece + 1) * n, (kind // 2) * BATCH:(kind // 2 + 1) * BATCH]
                    if kind % 2 == 0:
                        src = cat[:, 0:BATCH, bass.ds(chunk * STEPS + piece * n, n)].rearrange("p b t -> p t b")
                        pe.matmul(out, wx[:, kind // 2, :], src, start=(kind == 0 and piece == 0), stop=False, skip_group_check=True)
                    else:
                        pe.matmul(out, bias[:, kind // 2, :], ones[:, 0:n].unsqueeze(2).broadcast_to([1, n, BATCH]), start=False, stop=False, skip_group_check=True)

                for piece in range(4):
                    for kind in range(4):
                        inputs(0, 0, piece, kind)
                with pe.Fori(0, SEQ // RING) as i:
                    for k in range(RING):
                        bank, t = divmod(k, STEPS)
                        pe.wait_ge(stepped, RING * i + (k + 1))
                        prev = ring[:, (k - 1) % RING, :]
                        pe.matmul(core.ps[:, bank, t * COLS:t * COLS + BATCH], wh[:, 0, :], prev, start=False, stop=True, skip_group_check=True)
                        pe.matmul(core.ps[:, bank, t * COLS + BATCH:(t + 1) * COLS], wh[:, 1, :], prev, start=False, stop=True, skip_group_check=True).then_inc(summed, 1)
                        if 4 <= t < 20:
                            inputs(1 - bank, 2 * i + (bank + 1), (t - 4) // 4, (t - 4) % 4)

            @block.scalar
            def _(a):
                a.wait_ge(weights, 1)
                a.activation(warm[:], half[:], ACT.Tanh).then_inc(primed, 1)
                with a.Fori(0, SEQ // RING) as i:
                    for k in range(RING):
                        bank, t = divmod(k, STEPS)
                        a.wait_ge(summed, RING * i + (k + 1))
                        a.activation(act[:, k % 2, :], core.ps[:, bank, t * COLS:(t + 1) * COLS], ACT.Tanh).then_inc(bent, 1)

            @block.gpsimd
            def _(g):
                g.memset(ones[:], 1.0).then_inc(copied, 2)
                with g.Fori(0, SEQ // RING) as i:
                    for hf in range(2):
                        g.wait_ge(stepped, RING * i + (hf + 1) * STEPS + 1)
                        g.tensor_copy(history[:, bass.ds((2 * i + hf) * (STEPS * BATCH), STEPS * BATCH)], ring[:, hf * STEPS:(hf + 1) * STEPS, :].rearrange("p t b -> p (t b)")).then_inc(copied, 1)

            @block.vector
            def _(v):
                own = Chain(v, chain_s)
                v.wait_ge(loaded, 48)
                own(v.tensor_scalar(half[:], rows_sign[:], 0.5, None, ALU.mult))
                for w in (wx, wh, bias):
                    own(v.tensor_scalar(w[:, 1, :], w[:, 1, :], 0.05, None, ALU.mult))
                    own(v.scalar_tensor_tensor(out=w[:, 1, :], in0=w[:, 2, :], scalar=0.5, in1=w[:, 1, :], op0=ALU.mult, op1=ALU.add))
                v.tensor_scalar(wh[:, 0:2, :], wh[:, 0:2, :], half[:], None, ALU.mult).then_inc(weights, 1)
                v.memset(ring[:, RING - 1, :], 0.0).then_inc(stepped, 1)
                with v.Fori(0, SEQ // RING) as i:
                    for k in range(RING):
                        if k % STEPS == 0:
                            v.wait_ge(copied, 2 * i + (k // STEPS + 1))
                        v.wait_ge(bent, RING * i + (k + 1))
                        v.scalar_tensor_tensor(out=ring[:, k, :], in0=act[:, k % 2, BATCH:COLS], scalar=rows_sign[:], in1=act[:, k % 2, 0:BATCH], op0=ALU.add, op1=ALU.mult).then_inc(stepped, 1)


def l2_finish(core, history, rows_sign):
    d = core.dram
    with Scope(core, "l2f") as s:
        w = s.sb("w", [P, D])
        half = s.sb("half", [P, 1])
        ob = s.sb("ob", [P, D])
        Y = s.sb("Y", [P, TILES, D])
        stats = s.sb("stats", [P, TILES, 6])
        mv = s.sb("mv", [P, TILES, 2])
        rstd = s.sb("rstd", [P, TILES])
        loaded, weights, made, chain_s = s.sem("loaded"), s.sem("weights"), s.sem("made"), s.sem("ve_chain")
        ve_done, pool_done = s.sem("ve_done"), s.sem("pool_done")
        with s.block() as block:
            @block.sync
            def _(sp):
                sp.dma_start(w[:], d["rnn_out"]).then_inc(loaded, 16)
                sp.dma_start(ob[:], d["L2_attn_out_b"].rearrange("(a n) -> a n", a=1).broadcast_to([P, D])).then_inc(loaded, 16)

            @block.tensor
            def _(pe):
                pe.wait_ge(weights, 1)
                for t in range(TILES):
                    b, q = divmod(t, QT)
                    src = history[:].rearrange("p (t b) -> p b t", b=BATCH)[:, b, q * P:(q + 1) * P]
                    m = pe.matmul(core.ps[:, t // 4, (t % 4) * D:(t % 4 + 1) * D], src, w[:], start=True, stop=True)
                    if t % 4 == 3:
                        m.then_inc(made, 1)

            @block.gpsimd
            def _(g):
                rstd_tokens(g, core, pool_done, ve_done, mv, rstd)

            @block.vector
            def _(v):
                own = Chain(v, chain_s)
                v.wait_ge(loaded, 32)
                own(v.tensor_scalar(half[:], rows_sign[:], 0.5, None, ALU.mult))
                v.tensor_scalar(w[:], w[:], half[:], None, ALU.mult).then_inc(weights, 1)
                own(v.scalar_tensor_tensor(out=Y[:], in0=core.X[:], scalar=2.0, in1=ob[:].unsqueeze(1).broadcast_to([P, TILES, D]), op0=ALU.mult, op1=ALU.add))
                for g in range(4):
                    v.wait_ge(made, g + 1)
                    m = v.tensor_tensor(Y[:, 4 * g:4 * g + 4], core.ps[:, g, :].rearrange("p (q d) -> p q d", q=4), Y[:, 4 * g:4 * g + 4], ALU.add)
                    own.mark(m)
                own.wait()
                norm_tokens(v, pool_done, ve_done, own, Y, core.X, stats, mv, rstd)


def bit_mlp(core):
    d = core.dram
    C = BIT_H // P
    with Scope(core, "bit") as s:
        wf = s.sb("wf", [P, C, P])
        wp = s.sb("wp", [P, BIT_H])
        mag = s.sb("mag", [P, BIT_H])
        neg = s.sb("neg", [P, BIT_H])
        scale = s.sb("scale", [P, C + 1])
        up = s.sb("up", [P, C + 1])
        down = s.sb("down", [P, C + 1])
        fastT = s.sb("fastT", [BIT_R, BIT_R])
        vw = s.sb("vw", [BIT_R, P])
        uT = s.sb("uT", [BIT_R, BIT_H])
        fv = s.sb("fv", [BIT_R, P])
        gate = s.sb("gate", [P, 1])
        w1 = s.sb("w1", [P, BIT_H])
        w2 = s.sb("w2", [P, C, P])
        r0 = s.sb("r0", [P, 2, SEQ])
        r = s.sb("r", [P, 2, C, SEQ])
        Y = s.sb("Y", [P, TILES, D])
        stats = s.sb("stats", [P, TILES, 6])
        mv = s.sb("mv", [P, TILES, 2])
        rstd = s.sb("rstd", [P, TILES])
        loaded, turned, kept, ternary = s.sem("loaded"), s.sem("turned"), s.sem("kept"), s.sem("ternary")
        turned_w, low1, low1_kept, low2, w_kept, w_ready = (s.sem(n) for n in ("turned_w", "low1", "low1_kept", "low2", "w_kept", "w_ready"))
        hidden, relu, squared, out, summed = (s.sem(n) for n in ("hidden", "relu", "squared", "out", "summed"))
        ve_done, pool_done, chain_s = s.sem("ve_done"), s.sem("pool_done"), s.sem("ve_chain")
        with s.block() as block:
            @block.sync
            def _(sp):
                sp.dma_start(wf[:], d["L2_ffn_w_fc"].rearrange("(c p) n -> p c n", p=P)).then_inc(loaded, 16)
                sp.dma_start(wp[:], d["L2_ffn_w_proj"]).then_inc(loaded, 16)
                sp.dma_start(fastT[:], d["bit_fastT"]).then_inc(loaded, 16)
                sp.dma_start(vw[:], d["L2_ffn_v"]).then_inc(loaded, 16)
                sp.dma_start(uT[:], d["bit_uT"]).then_inc(loaded, 16)
                sp.dma_start(gate[:], d["bit_gate"].broadcast_to([P, 1])).then_inc(loaded, 16)

            @block.tensor
            def _(pe):
                turn_tokens(pe, core, turned, core.X)
                pe.wait_ge(loaded, 96)
                pe.matmul(core.ps[0:BIT_R, 4, 0:P], fastT[:], vw[:], start=True, stop=True).then_inc(low1, 1)
                pe.wait_ge(ternary, 1)
                for c in range(C):
                    m = pe.transpose(core.ps[:, 5, c * P:(c + 1) * P], wf[:, c, :], core.ident[:])
                m.then_inc(turned_w, 1)
                for c in range(C):
                    m = pe.transpose(core.ps[:, 6, c * P:(c + 1) * P], wp[:, c * P:(c + 1) * P], core.ident[:])
                m.then_inc(turned_w, 1)
                pe.wait_ge(low1_kept, 1)
                pe.matmul(core.ps[:, 7, :], fv[:], uT[:], start=True, stop=True).then_inc(low2, 1)
                pe.wait_ge(w_ready, 1)

                def project(b):
                    if b >= 2:
                        pe.wait_ge(summed, b - 1)
                    pe.wait_ge(squared, C * b + C)
                    for q in range(QT):
                        for c in range(C):
                            m = pe.matmul(core.ps[:, 6 + b % 2, q * P:(q + 1) * P], r[:, b % 2, c, q * P:(q + 1) * P], w2[:, c, :], start=(c == 0), stop=(c == C - 1))
                    m.then_inc(out, 1)

                for b in range(BATCH):
                    pe.wait_ge(kept, b + 1)
                    for c in range(C):
                        n = b * C + c
                        if n >= 6:
                            pe.wait_ge(squared, n - 5)
                        else:
                            pe.wait_ge(kept, 4)
                        pe.matmul(core.ps[:, n % 6, :], w1[:, c * P:(c + 1) * P], core.XT[:, b * SEQ:(b + 1) * SEQ], start=True, stop=True).then_inc(hidden, 1)
                    if b >= 1:
                        project(b - 1)
                project(BATCH - 1)

            @block.scalar
            def _(a):
                keep_turned(a, core, turned, kept)
                a.wait_ge(low1, 1)
                a.activation(fv[:], core.ps[0:BIT_R, 4, 0:P], ACT.Copy).then_inc(low1_kept, 1)
                a.wait_ge(turned_w, 1)
                a.activation(w1[:], core.ps[:, 5, :], ACT.Copy).then_inc(w_kept, 1)
                a.wait_ge(turned_w, 2)
                a.activation(w2[:], core.ps[:, 6, :].rearrange("p (c n) -> p c n", c=C), ACT.Copy).then_inc(w_kept, 1)
                for n in range(BATCH * C):
                    a.wait_ge(hidden, n + 1)
                    if n >= 2:
                        a.wait_ge(squared, n - 1)
                    a.activation(r0[:, n % 2], core.ps[:, n % 6, :], ACT.Relu).then_inc(relu, 1)

            @block.gpsimd
            def _(g):
                rstd_tokens(g, core, pool_done, ve_done, mv, rstd)

            @block.vector
            def _(v):
                own = Chain(v, chain_s)
                v.wait_ge(loaded, 96)
                own(v.scalar_tensor_tensor(out=mag[:], in0=wp[:], scalar=-1.0, in1=wp[:], op0=ALU.mult, op1=ALU.max))
                own(v.tensor_reduce(scale[:, C:C + 1], mag[:], AX.X, ALU.add))
                own(v.tensor_scalar(scale[:, C:C + 1], scale[:, C:C + 1], 1.0 / BIT_H, 1e-5, ALU.mult, ALU.max))
                own(v.scalar_tensor_tensor(out=mag[:], in0=wf[:].rearrange("p c n -> p (c n)"), scalar=-1.0, in1=wf[:].rearrange("p c n -> p (c n)"), op0=ALU.mult, op1=ALU.max))
                own(v.tensor_reduce(scale[:, 0:C], mag[:].rearrange("p (c n) -> p c n", c=C), AX.X, ALU.add))
                own(v.tensor_scalar(scale[:, 0:C], scale[:, 0:C], 1.0 / D, 1e-5, ALU.mult, ALU.max))
                own(v.tensor_scalar(up[:], scale[:], 0.5, None, ALU.mult))
                own(v.tensor_scalar(down[:], scale[:], -0.5, None, ALU.mult))
                for c in range(C):
                    own(v.tensor_scalar(neg[:, c * P:(c + 1) * P], wf[:, c, :], down[:, c:c + 1], scale[:, c:c + 1], ALU.is_lt, ALU.mult))
                    own(v.tensor_scalar(wf[:, c, :], wf[:, c, :], up[:, c:c + 1], scale[:, c:c + 1], ALU.is_gt, ALU.mult))
                own(v.tensor_tensor(wf[:].rearrange("p c n -> p (c n)"), wf[:].rearrange("p c n -> p (c n)"), neg[:], ALU.subtract))
                own(v.tensor_scalar(neg[:], wp[:], down[:, C:C + 1], scale[:, C:C + 1], ALU.is_lt, ALU.mult))
                own(v.tensor_scalar(wp[:], wp[:], up[:, C:C + 1], scale[:, C:C + 1], ALU.is_gt, ALU.mult))
                v.tensor_tensor(wp[:], wp[:], neg[:], ALU.subtract).then_inc(ternary, 1)
                v.wait_ge(low2, 1)
                v.wait_ge(w_kept, 2)
                v.scalar_tensor_tensor(out=w1[:], in0=core.ps[:, 7, :], scalar=gate[:], in1=w1[:], op0=ALU.mult, op1=ALU.add).then_inc(w_ready, 1)

                def residual(b):
                    v.wait_ge(out, b + 1)
                    v.tensor_tensor(Y[:, b * QT:(b + 1) * QT], core.ps[:, 6 + b % 2, :].rearrange("p (q d) -> p q d", q=QT), core.X[:, b * QT:(b + 1) * QT], ALU.add).then_inc(summed, 1)

                for n in range(BATCH * C):
                    b, c = divmod(n, C)
                    v.wait_ge(relu, n + 1)
                    if c == 0 and b >= 2:
                        v.wait_ge(out, b - 1)
                    v.scalar_tensor_tensor(out=r[:, b % 2, c, :], in0=core.ps[:, n % 6, :], scalar=0.0, in1=r0[:, n % 2], op0=ALU.max, op1=ALU.mult).then_inc(squared, 1)
                    if c == C - 1 and b >= 1:
                        residual(b - 1)
                residual(BATCH - 1)
                v.wait_ge(summed, BATCH)
                norm_tokens(v, pool_done, ve_done, own, Y, core.X, stats, mv, rstd)


def rms_tokens(v, pool_done, ve_done, chain, src, stats, mv, ms):
    for t in range(TILES):
        chain.mark(v.bn_stats(stats[:, t, :], src[:, t, :]))
    chain.wait()
    for t in range(TILES):
        chain.mark(v.bn_aggr(mv[:, t, :], stats[:, t, :]))
    chain.wait()
    chain(v.tensor_tensor(ms[:], mv[:, :, 0], mv[:, :, 0], ALU.mult))
    v.tensor_tensor(ms[:], ms[:], mv[:, :, 1], ALU.add).then_inc(ve_done, 1)
    v.wait_ge(pool_done, 2)


def rstd_ms(g, core, pool_done, ve_done, ms, rstd):
    g.wait_ge(ve_done, 1)
    g.tensor_scalar(rstd[:], ms[:], EPS, None, ALU.add).then_inc(pool_done, 1)
    g.wait_ge(pool_done, 1)
    g.tensor_tensor(rstd[:], rstd[:], core.half_neg[:], ALU.pow).then_inc(pool_done, 1)


DA_W = 40
CH = 4


def mamba_layer(core, l, H, m):
    d = core.dram
    ms = m
    with Scope(core, "ma") as s:
        w = s.sb("w", [P, M_PROJ])
        stats = s.sb("stats", [P, TILES, 6])
        mv = s.sb("mv", [P, TILES, 2])
        msq = s.sb("msq", [P, TILES])
        rstd = s.sb("rstd", [P, TILES])
        xn = s.sb("xn", [P, TILES, D])
        cv = s.sb("cv", [P, 4, SEQ])
        dt0 = s.sb("dt0", [P, TILES, M_HEADS])
        dt1 = s.sb("dt1", [P, TILES, M_HEADS])
        da = s.sb("da", [P, TILES, DA_W])
        Arow = s.sb("Arow", [P, M_HEADS])
        loaded, loaded_w = s.sem("loaded"), s.sem("loaded_w")
        turned, kept, made, zmade = s.sem("turned"), s.sem("kept"), s.sem("made"), s.sem("zmade")
        tap, conv, silued, zsilued, dts = s.sem("tap"), s.sem("conv"), s.sem("silued"), s.sem("zsilued"), s.sem("dts")
        ve_done, pool_done, chain_s, padded = s.sem("ve_done"), s.sem("pool_done"), s.sem("ve_chain"), s.sem("padded")
        neg_abs, exp_dt, plus_one, lned, da_ready, a_ready = (s.sem(n) for n in ("neg_abs", "exp_dt", "plus_one", "lned", "da_ready", "a_ready"))
        sums, diffs, exps, rows_sum, rows_kept, factors = (s.sem(n) for n in ("sums", "diffs", "exps", "rows_sum", "rows_kept", "factors"))
        with s.block() as block:
            @block.sync
            def _(sp):
                sp.dma_start(ms.cols[:], d["m_cols"][bass.ds(l, 1)].rearrange("a p n -> p (a n)")).then_inc(loaded, 16)
                sp.dma_start(ms.rows[:], d["m_rows"][bass.ds(l, 1)].broadcast_to([P, 3 * M_HEADS])).then_inc(loaded, 16)
                sp.dma_start(w[:], d["L3_attn_W_in"][bass.ds(l, 1)].rearrange("a p n -> p (a n)")).then_inc(loaded_w, 16)
                sp.dma_start(ms.wo[:], d["L3_attn_W_out"][bass.ds(l, 1)].rearrange("a (c p) n -> p (a c) n", p=P)).then_inc(loaded_w, 16)

            @block.tensor
            def _(pe):
                for t in range(TILES):
                    pe.wait_ge(ve_done, t + 2)
                    mm = pe.transpose(core.ps[:, t // 4, (t % 4) * P:(t % 4 + 1) * P], xn[:, t, :], core.ident[:])
                    if t % 4 == 3:
                        mm.then_inc(turned, 1)
                pe.wait_ge(loaded_w, 32)
                for b in range(BATCH):
                    pe.wait_ge(kept, BATCH)
                    for j in range(CH):
                        n = b * CH + j
                        if n >= 4:
                            pe.wait_ge(conv, n - 3)
                        pe.matmul(core.ps[:, 4 + n % 4, :], w[:, M_INNER + j * P:M_INNER + (j + 1) * P], core.XT[:, b * SEQ:(b + 1) * SEQ], start=True, stop=True).then_inc(made, 1)
                    for q in range(QT):
                        t = b * QT + q
                        if t >= 4:
                            pe.wait_ge(dts, t - 3)
                        x = core.XT[:, t * P:(t + 1) * P]
                        pe.matmul(core.ps[:, t % 4, 0:M_INNER], x, w[:, 0:M_INNER], start=True, stop=True)
                        pe.matmul(core.ps[:, t % 4, M_INNER:M_INNER + M_HEADS], x, w[:, M_PROJ - M_HEADS:], start=True, stop=True).then_inc(zmade, 1)
                pe.wait_ge(da_ready, 1)
                dense = da[:, :, 0:M_HEADS]
                pe.matmul(core.ps[:, 0, 0:TILES * M_HEADS], core.tri[:], dense, start=True, stop=True)
                pe.matmul(core.ps[:, 0, P:P + TILES * M_HEADS], core.all_ones[:], dense, start=True, stop=True).then_inc(sums, 1)
                for t in range(TILES):
                    mm = pe.matmul(core.ps[0:DA_W, 4 + t // 4, (t % 4) * P:(t % 4 + 1) * P], da[:, t, :], core.tri[:], start=True, stop=True)
                    if t % 4 == 3:
                        mm.then_inc(rows_sum, 1)

            @block.scalar
            def _(a):
                a.wait_ge(loaded, 32)
                a.activation(Arow[:], ms.rows[:, M_HEADS:2 * M_HEADS], ACT.Exp).then_inc(a_ready, 1)
                for g in range(4):
                    a.wait_ge(turned, g + 1)
                    a.activation(core.XT[:, g * BANK:(g + 1) * BANK], core.ps[:, g, :], ACT.Copy, scale=ms.cols[:, 0:1]).then_inc(kept, 1)

                def silu(n):
                    b, j = divmod(n, CH)
                    a.wait_ge(conv, n + 1)
                    a.activation(ms.xs[:, j, b * SEQ:(b + 1) * SEQ], cv[:, n % 4, :], ACT.Silu).then_inc(silued, 1)

                for b in range(BATCH):
                    for j in range(CH):
                        n = b * CH + j
                        a.wait_ge(made, n + 1)
                        if n >= 4:
                            a.wait_ge(silued, n - 3)
                        a.activation(cv[:, n % 4, :], core.ps[:, 4 + n % 4, :], ACT.Identity, scale=ms.cols[:, 1 + j * 4 + 3:1 + j * 4 + 4], bias=ms.cols[:, 17 + j:18 + j]).then_inc(tap, 1)
                        if n >= 2:
                            silu(n - 2)
                    for q in range(QT):
                        t = b * QT + q
                        a.wait_ge(zmade, t + 1)
                        a.activation(ms.zs[:, t, :], core.ps[:, t % 4, 0:M_INNER], ACT.Silu).then_inc(zsilued, 1)
                silu(BATCH * CH - 2)
                silu(BATCH * CH - 1)
                a.wait_ge(neg_abs, 1)
                a.activation(dt1[:], dt1[:], ACT.Exp).then_inc(exp_dt, 1)
                a.wait_ge(plus_one, 1)
                a.activation(dt1[:], dt1[:], ACT.Ln).then_inc(lned, 1)
                a.wait_ge(diffs, 1)
                a.activation(ms.fac[:], ms.fac[:], ACT.Exp).then_inc(exps, 1)
                for g in range(4):
                    a.wait_ge(rows_sum, g + 1)
                    a.activation(ms.csT[0:DA_W, g * BANK:(g + 1) * BANK], core.ps[0:DA_W, 4 + g, :], ACT.Copy).then_inc(rows_kept, 1)

            @block.gpsimd
            def _(g):
                g.memset(da[:], 0.0).then_inc(padded, 1)
                rstd_ms(g, core, pool_done, ve_done, msq, rstd)
                g.wait_ge(rows_kept, 4)
                g.tensor_copy(ms.lh[0:32, :], ms.csT[0:32, :]).then_inc(factors, 1)

            @block.vector
            def _(v):
                own = Chain(v, chain_s)
                rms_tokens(v, pool_done, ve_done, own, H, stats, mv, msq)
                for t in range(TILES):
                    v.tensor_scalar(xn[:, t, :], H[:, t, :], rstd[:, t:t + 1], None, ALU.mult).then_inc(ve_done, 1)
                v.wait_ge(loaded, 32)
                for b in range(BATCH):
                    for j in range(CH):
                        n = b * CH + j
                        v.wait_ge(tap, n + 1)
                        for k in (2, 1, 0):
                            lag = 3 - k
                            mm = v.scalar_tensor_tensor(out=cv[:, n % 4, lag:], in0=core.ps[:, 4 + n % 4, 0:SEQ - lag], scalar=ms.cols[:, 1 + j * 4 + k:2 + j * 4 + k], in1=cv[:, n % 4, lag:], op0=ALU.mult, op1=ALU.add)
                            if k:
                                own(mm)
                        mm.then_inc(conv, 1)
                    for q in range(QT):
                        t = b * QT + q
                        v.wait_ge(zsilued, t + 1)
                        v.tensor_tensor(dt0[:, t, :], core.ps[:, t % 4, M_INNER:M_INNER + M_HEADS], ms.rows[:, 0:M_HEADS], ALU.add).then_inc(dts, 1)
                v.wait_ge(dts, TILES)
                v.scalar_tensor_tensor(out=dt1[:], in0=dt0[:], scalar=-1.0, in1=dt0[:], op0=ALU.mult, op1=ALU.min).then_inc(neg_abs, 1)
                v.wait_ge(exp_dt, 1)
                v.tensor_scalar(dt1[:], dt1[:], 1.0, None, ALU.add).then_inc(plus_one, 1)
                v.wait_ge(lned, 1)
                own(v.scalar_tensor_tensor(out=ms.dt[:], in0=dt0[:], scalar=0.0, in1=dt1[:], op0=ALU.max, op1=ALU.add))
                v.wait_ge(a_ready, 1)
                v.wait_ge(padded, 1)
                arow = Arow[:].unsqueeze(1).broadcast_to([P, TILES, M_HEADS])
                own(v.scalar_tensor_tensor(out=da[:, :, 0:M_HEADS], in0=ms.dt[:], scalar=-1.0, in1=arow, op0=ALU.mult, op1=ALU.mult))
                v.tensor_copy(da[:, :, 32:40], da[:, :, 0:M_HEADS]).then_inc(da_ready, 1)
                v.wait_ge(sums, 1)
                n = TILES * M_HEADS
                own(v.tensor_copy(ms.fac[:, 0:2, :].rearrange("p k n -> p (k n)"), core.ps[:, 0, 0:2 * n]))
                v.tensor_tensor(ms.fac[:, 2, :], ms.fac[:, 1, :], ms.fac[:, 0, :], ALU.subtract).then_inc(diffs, 1)
                v.wait_ge(exps, 1)
                own(v.tensor_tensor(ms.fac[:, 2, :], ms.fac[:, 2, :], ms.dt[:].rearrange("p t h -> p (t h)"), ALU.mult))

    mamba_chunks(core, H, m)
    mamba_output(core, H, m)


class MambaBuffers:

    def __init__(self, s):
        self.cols = s.sb("cols", [P, 23])
        self.rows = s.sb("rows", [P, 3 * M_HEADS])
        self.wo = s.sb("wo", [P, 2, D])
        self.xs = s.sb("xs", [P, CH, TOK])
        self.zs = s.sb("zs", [P, TILES, M_INNER])
        self.dt = s.sb("dt", [P, TILES, M_HEADS])
        self.fac = s.sb("fac", [P, 3, TILES * M_HEADS])
        self.csT = s.sb("csT", [DA_W, TOK])
        self.lh = s.sb("lh", [DA_W, TOK])
        self.rh = s.sb("rh", [DA_W, 2, M_HEADS, P])
        self.delta = s.sb("delta", [DA_W, M_HEADS, P])
        self.yz = s.sb("yz", [P, TILES, M_INNER])
        self.ss = s.sb("ss", [P, TILES])
        self.state = s.sb("state", [P, 2, M_INNER])


def mamba_constants(core, m):
    with Scope(core, "mc") as s:
        loaded, set_ = s.sem("loaded"), s.sem("set")
        with s.block() as block:
            @block.sync
            def _(sp):
                sp.dma_start(m.delta[:], core.dram["m_delta"]).then_inc(loaded, 16)
                sp.dma_start(core.tri[:], core.dram["tri"]).then_inc(loaded, 16)
                sp.wait_ge(loaded, 32)

            @block.gpsimd
            def _(g):
                own = Chain(g, set_)
                own(g.memset(core.all_ones[:], 1.0))
                own(g.memset(m.lh[32:DA_W, :], 1.0))
                own(g.memset(m.lh[0:32, :], 0.0))
                g.wait_ge(loaded, 32)
                for i in range(2):
                    own(g.tensor_copy(m.rh[:, i], m.delta[:]))


def mamba_chunks(core, H, m):
    with Scope(core, "mb") as s:
        L = s.sb("L", [P, 2, M_HEADS, P])
        M = s.sb("M", [P, 2, M_HEADS, P])
        Bt = s.sb("Bt", [P, 2, P])
        xt = s.sb("xt", [P, 2, M_INNER])
        dtx = s.sb("dtx", [P, 2, M_INNER])
        wx = s.sb("wx", [P, 2, M_INNER])
        xd = s.sb("xd", [P, 2, M_INNER])
        off = s.sb("off", [P, 2, M_INNER])
        y = s.sb("y", [P, 2, M_INNER])
        sq = s.sb("sq", [P, 2, M_INNER])
        names = ("rows_in", "args", "decays", "inner", "turned", "x_kept", "b_kept", "dtx_made", "wx_made", "mixed", "xd_made",
                 "inside", "outside", "state_in", "off_made", "y_made", "y_sum", "gated", "squares", "shrunk", "state_made")
        sem = {n: s.sem(n) for n in names}
        NT = TILES

        def heads(x):
            return x.rearrange("p (h e) -> p h e", h=M_HEADS)

        def each(row):
            return row.unsqueeze(2).broadcast_to([P, M_HEADS, M_HD])

        def fac(k, t):
            return each(m.fac[:, k, t * M_HEADS:(t + 1) * M_HEADS])

        with s.block() as block:
            @block.tensor
            def _(pe):
                def first(t):
                    pe.wait_ge(sem["rows_in"], t + 1)
                    if t >= 1:
                        pe.wait_ge(sem["decays"], t)
                    for k in range(2):
                        pe.matmul(core.ps[:, k, :], m.lh[:, t * P:(t + 1) * P], m.rh[:, t % 2, 4 * k:4 * k + 4, :], start=True, stop=False)
                        mm = pe.matmul(core.ps[:, k, :], core.ident_bf[:], core.mask_k[:].unsqueeze(1).broadcast_to([P, 4, P]), start=False, stop=True)
                    mm.then_inc(sem["args"], 1)
                    if t >= 1:
                        pe.wait_ge(sem["x_kept"], t)
                        pe.wait_ge(sem["dtx_made"], t)
                        pe.wait_ge(sem["b_kept"], t)
                    cols = slice(t * P, (t + 1) * P)
                    for k in range(2):
                        pe.transpose(core.ps[:, 3, k * P:(k + 1) * P], m.xs[:, k, cols], core.ident[:])
                    pe.transpose(core.ps[:, 4, 0:P], m.xs[:, 2, cols], core.ident[:]).then_inc(sem["turned"], 1)
                    if t >= 1:
                        pe.wait_ge(sem["mixed"], t)
                    pe.matmul(core.ps[:, 2, 0:P], m.xs[:, 2, cols], m.xs[:, 3, cols], start=True, stop=True).then_inc(sem["inner"], 1)

                def second(t):
                    b, c = divmod(t, QT)
                    if c > 0:
                        pe.wait_ge(sem["state_made"], t)
                        if t >= 2:
                            pe.wait_ge(sem["off_made"], t - 1 - b)
                        pe.matmul(core.ps[:, 6, 0:M_INNER], m.xs[:, 3, t * P:(t + 1) * P], m.state[:, (t - 1) % 2, :], start=True, stop=True).then_inc(sem["outside"], 1)
                    if t >= 1:
                        pe.wait_ge(sem["y_made"], t)
                    pe.wait_ge(sem["mixed"], t + 1)
                    for h in range(M_HEADS):
                        mm = pe.matmul(core.ps[:, 5, h * M_HD:(h + 1) * M_HD], M[:, t % 2, h, :], dtx[:, t % 2, h * M_HD:(h + 1) * M_HD], start=True, stop=True)
                    mm.then_inc(sem["inside"], 1)
                    pe.wait_ge(sem["wx_made"], t + 1)
                    if t >= 1:
                        pe.wait_ge(sem["state_made"], t)
                    pe.wait_ge(sem["b_kept"], t + 1)
                    pe.matmul(core.ps[:, 7, 0:M_INNER], Bt[:, t % 2, :], wx[:, t % 2, :], start=True, stop=True).then_inc(sem["state_in"], 1)

                first(0)
                for t in range(NT):
                    if t + 1 < NT:
                        first(t + 1)
                    second(t)

            @block.scalar
            def _(a):
                def square(t):
                    a.wait_ge(sem["gated"], t + 1)
                    if t >= 2:
                        a.wait_ge(sem["squares"], t - 1)
                    a.activation(sq[:, t % 2], m.yz[:, t, :], ACT.Square, accum_out=m.ss[:, t:t + 1]).then_inc(sem["squares"], 1)

                for t in range(NT):
                    a.wait_ge(sem["args"], t + 1)
                    if t >= 2:
                        a.wait_ge(sem["mixed"], t - 1)
                    a.activation(L[:, t % 2].rearrange("p (k h) q -> p k (h q)", k=2), core.ps[:, 0:2, :], ACT.Exp).then_inc(sem["decays"], 1)
                    a.wait_ge(sem["turned"], t + 1)
                    if t >= 2:
                        a.wait_ge(sem["xd_made"], t - 1)
                        a.wait_ge(sem["wx_made"], t - 1)
                        a.wait_ge(sem["state_in"], t - 1)
                    a.activation(xt[:, t % 2], core.ps[:, 3, 0:M_INNER], ACT.Copy).then_inc(sem["x_kept"], 1)
                    a.activation(Bt[:, t % 2], core.ps[:, 4, 0:P], ACT.Copy).then_inc(sem["b_kept"], 1)
                    if t >= 2:
                        square(t - 2)
                square(NT - 2)
                square(NT - 1)

            @block.gpsimd
            def _(g):
                def rows(t):
                    if t >= 2:
                        g.wait_ge(sem["args"], t - 1)
                    if t == 1:
                        g.wait_ge(sem["rows_in"], 1)
                    g.tensor_tensor(m.rh[32:DA_W, t % 2], m.csT[32:DA_W, t * P:(t + 1) * P].unsqueeze(1).broadcast_to([M_HEADS, M_HEADS, P]), m.delta[32:DA_W], ALU.mult).then_inc(sem["rows_in"], 1)

                rows(0)
                for t in range(NT):
                    b, c = divmod(t, QT)
                    if t + 1 < NT:
                        if t >= 1:
                            g.wait_ge(sem["y_sum"], t)
                        rows(t + 1)
                    g.wait_ge(sem["rows_in"], min(t + 2, NT))
                    g.wait_ge(sem["x_kept"], t + 1)
                    if t >= 2:
                        g.wait_ge(sem["gated"], t - 1)
                    g.tensor_tensor(heads(xd[:, t % 2]), heads(xt[:, t % 2]), each(m.rows[:, 2 * M_HEADS:]), ALU.mult).then_inc(sem["xd_made"], 1)
                    if 0 < c:
                        g.wait_ge(sem["state_made"], t)
                        g.wait_ge(sem["outside"], t - b)
                        if t >= 2:
                            g.wait_ge(sem["state_made"], t)
                        g.tensor_tensor(heads(m.state[:, t % 2, :]), heads(m.state[:, (t - 1) % 2, :]), fac(1, t), ALU.mult).then_inc(sem["shrunk"], 1)
                    g.wait_ge(sem["y_made"], t + 1)
                    g.wait_ge(sem["xd_made"], t + 1)
                    g.tensor_tensor(xd[:, t % 2], y[:, t % 2], xd[:, t % 2], ALU.add).then_inc(sem["y_sum"], 1)

            @block.vector
            def _(v):
                def gate(t):
                    v.wait_ge(sem["y_sum"], t + 1)
                    v.tensor_tensor(m.yz[:, t, :], xd[:, t % 2], m.zs[:, t, :], ALU.mult).then_inc(sem["gated"], 1)

                for t in range(NT):
                    b, c = divmod(t, QT)
                    v.wait_ge(sem["x_kept"], t + 1)
                    if t >= 2:
                        v.wait_ge(sem["inside"], t - 1)
                    v.tensor_tensor(heads(dtx[:, t % 2]), heads(core.ps[:, 3, 0:M_INNER]), each(m.dt[:, t, :]), ALU.mult).then_inc(sem["dtx_made"], 1)
                    if t >= 2:
                        v.wait_ge(sem["state_in"], t - 1)
                    v.tensor_tensor(heads(wx[:, t % 2]), heads(xt[:, t % 2]), fac(2, t), ALU.mult).then_inc(sem["wx_made"], 1)
                    v.wait_ge(sem["decays"], t + 1)
                    v.wait_ge(sem["inner"], t + 1)
                    v.tensor_tensor(M[:, t % 2], core.ps[:, 2, 0:P].unsqueeze(1).broadcast_to([P, M_HEADS, P]), L[:, t % 2], ALU.mult).then_inc(sem["mixed"], 1)
                    if c > 0:
                        v.wait_ge(sem["outside"], t - b)
                        v.tensor_tensor(heads(off[:, t % 2]), heads(core.ps[:, 6, 0:M_INNER]), fac(0, t), ALU.mult).then_inc(sem["off_made"], 1)
                        v.wait_ge(sem["off_made"], t - b)
                    v.wait_ge(sem["inside"], t + 1)
                    if t >= 2:
                        v.wait_ge(sem["y_sum"], t - 1)
                    if c > 0:
                        v.tensor_tensor(y[:, t % 2], core.ps[:, 5, 0:M_INNER], off[:, t % 2], ALU.add).then_inc(sem["y_made"], 1)
                    else:
                        v.tensor_copy(y[:, t % 2], core.ps[:, 5, 0:M_INNER]).then_inc(sem["y_made"], 1)
                    v.wait_ge(sem["state_in"], t + 1)
                    if c > 0:
                        v.wait_ge(sem["shrunk"], t - b)
                        v.tensor_tensor(m.state[:, t % 2, :], core.ps[:, 7, 0:M_INNER], m.state[:, t % 2, :], ALU.add).then_inc(sem["state_made"], 1)
                    else:
                        v.tensor_copy(m.state[:, t % 2, :], core.ps[:, 7, 0:M_INNER]).then_inc(sem["state_made"], 1)
                    if t >= 1:
                        gate(t - 1)
                gate(NT - 1)


def mamba_output(core, H, m):
    with Scope(core, "mo") as s:
        yT = s.sb("yT", [P, 4, 2, P])
        rstd = s.sb("rstd", [P, TILES])
        turned, kept, made, added, pool_done, first = (s.sem(n) for n in ("turned", "kept", "made", "added", "pool_done", "first"))
        with s.block() as block:
            @block.tensor
            def _(pe):
                def project(t):
                    pe.wait_ge(kept, 2 * t + 2)
                    if t >= 4:
                        pe.wait_ge(added, t - 3)
                    for c in range(2):
                        mm = pe.matmul(core.ps[:, 4 + t % 4, 0:D], yT[:, t % 4, c, :], m.wo[:, c, :], start=(c == 0), stop=(c == 1))
                    mm.then_inc(made, 1)

                for t in range(TILES):
                    if t >= 4:
                        pe.wait_ge(kept, 2 * (t - 3))
                    for c in range(2):
                        mm = pe.transpose(core.ps[:, t % 4, c * P:(c + 1) * P], m.yz[:, t, c * P:(c + 1) * P], core.ident[:])
                    mm.then_inc(turned, 1)
                    if t >= 1:
                        project(t - 1)
                project(TILES - 1)

            @block.scalar
            def _(a):
                for t in range(TILES):
                    a.wait_ge(turned, t + 1)
                    if t >= 4:
                        a.wait_ge(made, t - 3)
                    for c in range(2):
                        a.activation(yT[:, t % 4, c, :], core.ps[:, t % 4, c * P:(c + 1) * P], ACT.Copy, scale=m.cols[:, 21 + c:22 + c]).then_inc(kept, 1)

            @block.gpsimd
            def _(g):
                g.tensor_scalar(rstd[:], m.ss[:], 1.0 / M_INNER, EPS, ALU.mult, ALU.add).then_inc(first, 1)
                g.wait_ge(first, 1)
                g.tensor_tensor(rstd[:], rstd[:], core.half_neg[:], ALU.pow).then_inc(pool_done, 1)

            @block.vector
            def _(v):
                v.wait_ge(pool_done, 1)
                for t in range(TILES):
                    v.wait_ge(made, t + 1)
                    v.scalar_tensor_tensor(out=H[:, t, :], in0=core.ps[:, 4 + t % 4, 0:D], scalar=rstd[:, t:t + 1], in1=H[:, t, :], op0=ALU.mult, op1=ALU.add).then_inc(added, 1)


def mamba_begin(core, H):
    with Scope(core, "m0") as s:
        copied = s.sem("copied")
        with s.block() as block:
            @block.vector
            def _(v):
                v.tensor_copy(H[:], core.X[:]).then_inc(copied, 1)


def mamba_end(core, H):
    with Scope(core, "me") as s:
        fw = s.sb("fw", [P, D])
        Y = s.sb("Y", [P, TILES, D])
        stats = s.sb("stats", [P, TILES, 6])
        mv = s.sb("mv", [P, TILES, 2])
        msq = s.sb("msq", [P, TILES])
        rstd = s.sb("rstd", [P, TILES])
        loaded, chain_s = s.sem("loaded"), s.sem("ve_chain")
        ve_done, pool_done, ve_done2, pool_done2 = s.sem("ve_done"), s.sem("pool_done"), s.sem("ve_done2"), s.sem("pool_done2")
        with s.block() as block:
            @block.sync
            def _(sp):
                sp.dma_start(fw[:], core.dram["L3_attn_final_norm_w"].rearrange("(a n) -> a n", a=1).broadcast_to([P, D])).then_inc(loaded, 16)

            @block.gpsimd
            def _(g):
                rstd_ms(g, core, pool_done, ve_done, msq, rstd)
                rstd_tokens(g, core, pool_done2, ve_done2, mv, rstd)

            @block.vector
            def _(v):
                own = Chain(v, chain_s)
                rms_tokens(v, pool_done, ve_done, own, H, stats, mv, msq)
                v.wait_ge(loaded, 16)
                for t in range(TILES):
                    own.mark(v.scalar_tensor_tensor(out=Y[:, t, :], in0=H[:, t, :], scalar=rstd[:, t:t + 1], in1=fw[:], op0=ALU.mult, op1=ALU.mult))
                own.wait()
                own(v.tensor_tensor(Y[:], Y[:], core.X[:], ALU.add))
                norm_tokens(v, pool_done2, ve_done2, own, Y, core.X, stats, mv, rstd)


def gated_mixture(core):
    d = core.dram
    E = MOE3_E
    W = TILES * E
    UNITS = E * BATCH
    with Scope(core, "moe3") as s:
        gate_w = s.sb("gate_w", [P, E])
        rank = s.sb("rank", [P, 16])
        sim = s.sb("sim", [E, E])
        rep = s.sb("rep", [E, W])
        blocks = s.sb("blocks", [W, TILES, E])
        w_gu = s.sb("w_gu", [P, E, 2 * MOE3_F])
        w_down = s.sb("w_down", [P, E, D])
        ones = s.sb("ones", [P, E])
        L = s.sb("L", [P, TILES, E])
        key = s.sb("key", [P, TILES, E])
        hots = [s.sb(f"hot{k}", [P, TILES, E]) for k in range(2)]
        tops = [s.sb(f"top{k}", [P, TILES]) for k in range(2)]
        best = s.sb("best", [P, TILES])
        gates = s.sb("gates", [P, TILES, E])
        gatesT = s.sb("gatesT", [W, P])
        count = s.sb("count", [P, E])
        used = s.sb("used", [E, E])
        unused = s.sb("unused", [E, E])
        own_use = s.sb("own_use", [E, 1])
        sim_key = s.sb("sim_key", [E, E])
        sim_top = s.sb("sim_top", [E, 2])
        moved = s.sb("moved", [E, 1])
        R = s.sb("R", [E, E])
        R2 = s.sb("R2", [E, E])
        Rrep = s.sb("Rrep", [W, TILES, E])
        dense = s.sb("dense", [P, TILES, E])
        sg = s.sb("sg", [P, 2, SEQ])
        hm = s.sb("hm", [P, 2, SEQ])
        stats = s.sb("stats", [P, TILES, 6])
        mv = s.sb("mv", [P, TILES, 2])
        rstd = s.sb("rstd", [P, TILES])
        names = ("loaded", "loaded_w", "turned", "kept", "scored", "differ", "exped", "first_two", "counted", "gated",
                 "weights_turned", "weights_kept", "rerouted", "spread", "spread_kept", "summed", "weights",
                 "made", "silued", "hidden", "down", "added", "ve_done", "pool_done", "chain", "ones_set")
        sem = {n: s.sem(n) for n in names}
        with s.block() as block:
            @block.sync
            def _(sp):
                sp.dma_start(gate_w[:], d["moe3_gateT"]).then_inc(sem["loaded"], 16)
                sp.dma_start(rank[:], d["rank"].broadcast_to([P, 16])).then_inc(sem["loaded"], 16)
                sp.dma_start(sim[:], d["L3_ffn_similarity_matrix"]).then_inc(sem["loaded"], 16)
                sp.dma_start(rep[:], d["moe3_rep"]).then_inc(sem["loaded"], 16)
                sp.dma_start(blocks[:].rearrange("p t e -> p (t e)"), d["moe3_blocks"]).then_inc(sem["loaded"], 16)
                sp.dma_start(w_gu[:], d["moe3_gate_upT"]).then_inc(sem["loaded_w"], 16)
                sp.dma_start(w_down[:], d["moe3_downT"]).then_inc(sem["loaded_w"], 16)

            @block.tensor
            def _(pe):
                turn_tokens(pe, core, sem["turned"], core.X)
                pe.wait_ge(sem["loaded"], 80)
                for t in range(TILES):
                    pe.wait_ge(sem["kept"], t // 4 + 1)
                    m = pe.matmul(core.ps[:, 7, t * E:(t + 1) * E], core.XT[:, t * P:(t + 1) * P], gate_w[:], start=True, stop=True)
                m.then_inc(sem["scored"], 1)

                def route():
                    pe.wait_ge(sem["ones_set"], 1)
                    pe.wait_ge(sem["first_two"], 1)
                    pe.matmul(core.ps[0:E, 7, 0:E], ones[:], count[:], start=True, stop=True)
                    pe.matmul(core.ps[0:E, 7, E:E + 1], count[:], ones[:, 0:1], start=True, stop=True).then_inc(sem["counted"], 1)
                    pe.wait_ge(sem["gated"], 1)
                    pe.wait_ge(sem["rerouted"], 1)
                    pe.transpose(core.ps[:, 7, P:2 * P], gates[:].rearrange("p t e -> p (t e)"), core.ident[:]).then_inc(sem["weights_turned"], 1)
                    pe.matmul(core.ps[:, 7, 2 * P:2 * P + E], rep[:], R[:], start=True, stop=True).then_inc(sem["spread"], 1)
                    pe.wait_ge(sem["weights_kept"], 1)
                    pe.wait_ge(sem["spread_kept"], 1)
                    pe.matmul(core.ps[:, 7, 3 * P:3 * P + W], gatesT[:], Rrep[:].rearrange("p t e -> p (t e)"), start=True, stop=True).then_inc(sem["summed"], 1)

                def down(u):
                    b, e = divmod(u, E)
                    pe.wait_ge(sem["hidden"], u + 1)
                    if u >= 2:
                        pe.wait_ge(sem["added"], QT * (u - 1))
                    for q in range(QT):
                        m = pe.matmul(core.ps[:, 4 + u % 2, q * D:(q + 1) * D], hm[:, u % 2, q * P:(q + 1) * P], w_down[:, e, :], start=True, stop=True)
                    m.then_inc(sem["down"], 1)

                pe.wait_ge(sem["loaded_w"], 32)
                for u in range(UNITS):
                    b, e = divmod(u, E)
                    x = core.XT[:, b * SEQ:(b + 1) * SEQ]
                    pe.wait_ge(sem["kept"], 4)
                    if u >= 2:
                        pe.wait_ge(sem["hidden"], u - 1)
                    for k in range(2):
                        m = pe.matmul(core.ps[:, 2 * (u % 2) + k, :], w_gu[:, e, k * P:(k + 1) * P], x, start=True, stop=True)
                    m.then_inc(sem["made"], 1)
                    if u == 1:
                        route()
                    if u >= 1:
                        down(u - 1)
                down(UNITS - 1)

            @block.scalar
            def _(a):
                keep_turned(a, core, sem["turned"], sem["kept"])
                a.wait_ge(sem["differ"], 1)
                a.activation(L[:], L[:], ACT.Exp).then_inc(sem["exped"], 1)

                def silu(u):
                    a.wait_ge(sem["made"], u + 1)
                    if u >= 2:
                        a.wait_ge(sem["hidden"], u - 1)
                    a.activation(sg[:, u % 2], core.ps[:, 2 * (u % 2), :], ACT.Silu).then_inc(sem["silued"], 1)

                silu(0)
                silu(1)
                a.wait_ge(sem["weights_turned"], 1)
                a.wait_ge(sem["spread"], 1)
                a.activation(gatesT[:], core.ps[:, 7, P:2 * P], ACT.Copy).then_inc(sem["weights_kept"], 1)
                for u in range(2, UNITS):
                    silu(u)

            @block.gpsimd
            def _(g):
                g.memset(ones[:], 1.0).then_inc(sem["ones_set"], 1)
                rstd_tokens(g, core, sem["pool_done"], sem["ve_done"], mv, rstd)

            @block.vector
            def _(v):
                own = Chain(v, sem["chain"])

                def each(x):
                    return x[:].unsqueeze(2).broadcast_to([P, TILES, E])

                v.wait_ge(sem["loaded"], 80)
                v.wait_ge(sem["scored"], 1)
                own(v.tensor_copy(L[:], core.ps[:, 7, 0:W].rearrange("p (t e) -> p t e", e=E)))
                own(v.tensor_reduce(best[:], L[:], AX.X, ALU.max))
                v.tensor_tensor(L[:], L[:], each(best), ALU.subtract).then_inc(sem["differ"], 1)
                v.wait_ge(sem["exped"], 1)
                own(v.tensor_reduce(best[:], L[:], AX.X, ALU.add))
                own(v.reciprocal(best[:], best[:]))
                own(v.tensor_tensor(L[:], L[:], each(best), ALU.mult))
                pick_two(v, own, rank, L[:], (key, best), hots, tops, E)
                v.tensor_reduce(count[:], hots[0][:].rearrange("p t e -> p e t"), AX.X, ALU.add).then_inc(sem["first_two"], 1)
                own(v.tensor_tensor(best[:], tops[0][:], tops[1][:], ALU.add))
                own(v.tensor_scalar(best[:], best[:], 1e-12, None, ALU.max))
                own(v.reciprocal(best[:], best[:]))
                for k in range(2):
                    own(v.tensor_tensor(tops[k][:], tops[k][:], best[:], ALU.mult))
                    own(v.tensor_tensor(hots[k][:], hots[k][:], each(tops[k]), ALU.mult))
                v.tensor_tensor(gates[:], hots[0][:], hots[1][:], ALU.add).then_inc(sem["gated"], 1)
                v.wait_ge(sem["counted"], 1)
                own(v.tensor_scalar(used[:], core.ps[0:E, 7, 0:E], 0.5, None, ALU.is_gt))
                own(v.tensor_scalar(own_use[:], core.ps[0:E, 7, E:E + 1], 0.5, None, ALU.is_lt))
                own(v.tensor_scalar(unused[:], used[:], -1.0, 1.0, ALU.mult, ALU.add))
                own(v.tensor_tensor(sim_key[:], sim[:], used[:], ALU.mult))
                own(v.scalar_tensor_tensor(out=sim_key[:], in0=unused[:], scalar=MASKED, in1=sim_key[:], op0=ALU.mult, op1=ALU.add))
                own(v.tensor_reduce(sim_top[:, 0:1], sim_key[:], AX.X, ALU.max))
                own(v.tensor_tensor(sim_key[:], sim_key[:], sim_top[:, 0:1].broadcast_to([E, E]), ALU.is_equal))
                own(v.tensor_tensor(sim_key[:], sim_key[:], rank[0:E, 0:E], ALU.mult))
                own(v.tensor_reduce(sim_top[:, 1:2], sim_key[:], AX.X, ALU.max))
                own(v.tensor_tensor(R2[:], sim_key[:], sim_top[:, 1:2].broadcast_to([E, E]), ALU.is_equal))
                own(v.tensor_scalar(moved[:], sim_top[:, 0:1], THRESHOLD, None, ALU.is_ge))
                own(v.tensor_tensor(moved[:], moved[:], own_use[:], ALU.mult))
                own(v.tensor_tensor(R2[:], R2[:], core.ident[0:E, 0:E], ALU.subtract))
                v.scalar_tensor_tensor(out=R[:], in0=R2[:], scalar=moved[:], in1=core.ident[0:E, 0:E], op0=ALU.mult, op1=ALU.add).then_inc(sem["rerouted"], 1)
                v.wait_ge(sem["spread"], 1)
                v.wait_ge(sem["weights_kept"], 1)
                v.tensor_tensor(Rrep[:], blocks[:], core.ps[:, 7, 2 * P:2 * P + E].unsqueeze(1).broadcast_to([W, TILES, E]), ALU.mult).then_inc(sem["spread_kept"], 1)
                v.wait_ge(sem["summed"], 1)
                v.tensor_copy(dense[:], core.ps[:, 7, 3 * P:3 * P + W].rearrange("p (t e) -> p t e", e=E)).then_inc(sem["weights"], 1)

                v.wait_ge(sem["weights"], 1)

                def weigh(u):
                    b, e = divmod(u, E)
                    v.wait_ge(sem["down"], u + 1)
                    if u:
                        v.wait_ge(sem["added"], QT * u)
                    for q in range(QT):
                        t = b * QT + q
                        v.scalar_tensor_tensor(out=core.X[:, t, :], in0=core.ps[:, 4 + u % 2, q * D:(q + 1) * D], scalar=dense[:, t, e:e + 1], in1=core.X[:, t, :], op0=ALU.mult, op1=ALU.add).then_inc(sem["added"], 1)

                for u in range(UNITS):
                    v.wait_ge(sem["silued"], u + 1)
                    if u >= 2:
                        v.wait_ge(sem["down"], u - 1)
                    v.tensor_tensor(hm[:, u % 2], core.ps[:, 2 * (u % 2) + 1, :], sg[:, u % 2], ALU.mult).then_inc(sem["hidden"], 1)
                    if u >= 1:
                        weigh(u - 1)
                weigh(UNITS - 1)
                v.wait_ge(sem["added"], QT * UNITS)
                norm_tokens(v, sem["pool_done"], sem["ve_done"], own, core.X, core.X, stats, mv, rstd)


def program(nc, dram, out):
    with ExitStack() as ctx:
        core = Core(nc, ctx, dram)
        scratch = {
            "qk": nc.dram_tensor("scratch_qk", (BATCH, PARTS, 2 * L0_EXP, SEQ), BF16, kind="Internal").ap(),
            "pos": nc.dram_tensor("scratch_pos", (PARTS, BATCH, HEADS, SEQ), BF16, kind="Internal").ap(),
        }
        prepare(core)
        M = ctx.enter_context(nc.sbuf_tensor("expert_products", [P, MOE0_E * D], F32))
        experts0(core, M)
        with Scope(core, "l0") as s:
            buf = {
                "V": s.sb("V", [P, TILES, HEADS, L0_DH + 1]),
                "gate": s.sb("gate", [P, TILES, L0_EXP]),
            }
            l0_project(core, buf, scratch)
            buf["O"] = s.sb("O", [P, TILES, L0_EXP])
            attention(core, "l0a", causal_plan(), scratch, buf["V"], buf["O"])
            l0_finish(core, buf)
        mixture(core, "moe0", MOE0_E, M, routed=False)
        with Scope(core, "l1") as s:
            scr = {"qk": nc.dram_tensor("scratch_qk1", (BATCH, PARTS, 2 * D, SEQ), BF16, kind="Internal").ap()}
            rscr = {"qk": nc.dram_tensor("scratch_rqk", (BATCH, PARTS, 2 * D, SEQ), BF16, kind="Internal").ap()}
            V = s.sb("V", [P, TILES, HEADS, L1_DH + 1])
            RV = s.sb("RV", [P, QT, HEADS, L1_DH + 1])
            O = s.sb("O", [P, TILES, D])
            OT = s.sb("OT", [P, TOK])
            l1_project(core, V, RV, scr["qk"], rscr["qk"])
            attention(core, "l1a", full_plan(), scr, V, O)
            l1_between(core, O, OT, rscr["qk"])
            attention(core, "l1r", recursive_plan(), rscr, RV, O)
            l1_finish(core, O, OT)
        mixture(core, "moe1", MOE1_E, core.w_routed, routed=True)
        with Scope(core, "l2") as s:
            cat = s.sb("cat", [P, BATCH, SEQ + STEPS])
            history = s.sb("history", [P, TOK])
            sign = s.sb("sign", [P, 1])
            l2_ssm(core, cat, sign)
            l2_scan(core, cat, history, sign)
            l2_finish(core, history, sign)
        bit_mlp(core)
        with Scope(core, "l3") as s:
            H = s.sb("H", [P, TILES, D])
            buffers = MambaBuffers(s)
            mamba_constants(core, buffers)
            mamba_begin(core, H)
            with nc.Fori(0, M_LAYERS) as l:
                mamba_layer(core, l, H, buffers)
            mamba_end(core, H)
        gated_mixture(core)
        store(core, out)


_USED = [
    "L0_attn_x", "L0_attn_b_in", "L0_ffn_w_in", "L1_attn_Wg", "L1_attn_bg",
    "L1_ffn_expert_biases", "L1_ffn_bs", "L1_ffn_br", "L2_attn_out_b", "L2_ffn_w_fc", "L2_ffn_w_proj", "L2_ffn_v",
    "L3_attn_W_in", "L3_attn_W_out", "L3_attn_final_norm_w",
    "L3_ffn_similarity_matrix",
]


def kernel(**inputs):
    import numpy as _np
    import concourse.bacc as _bacc
    from concourse import mybir as _mybir
    from concourse.bass_utils import run_bass_kernel_spmd as _run

    i = {k: _np.asarray(v) for k, v in inputs.items()}
    f = _np.float32
    arrays = {name: i[name] for name in _USED}
    k_, q_ = _np.meshgrid(_np.arange(128), _np.arange(128))
    arrays["ident"] = _np.eye(128, dtype=f)
    arrays["masks"] = _np.stack([_np.where(k_ > q_, f(-1e30), f(0)), _np.where(q_ > k_, f(-1e30), f(0))]).astype(f)
    sets = _np.zeros((2, 512), f)
    sets[0, :256] = 1
    sets[1, 256:] = 1
    arrays["set_rows"] = sets
    arrays["ones"] = _np.ones((1, 512), _mybir.dt.np(_mybir.dt.bfloat16))
    arrays["l0_out_ln"] = _np.stack([i["L0_attn_out_ln_w"], i["L0_attn_out_ln_b"]])
    arrays["l0_w_inT"] = i["L0_attn_W_in"].T
    arrays["l0_w_outT"] = i["L0_attn_W_out"].T
    arrays["l0_cols"] = _np.concatenate([
        i["L0_attn_in_ln_w"][None], i["L0_attn_in_ln_b"][None],
        _np.repeat(i["L0_attn_log_scale"], 16).reshape(2, 128),
        _np.repeat(i["L0_attn_smear_factor"], 16).reshape(2, 128),
        i["L0_attn_b_in"][:512].reshape(4, 128)]).T
    arrays["rank"] = _np.arange(16, 0, -1, dtype=f)[None]
    arrays["moe0_gateT"] = i["L0_ffn_w_gate"].T
    arrays["moe0_w_outT"] = i["L0_ffn_w_out"].transpose(0, 2, 1)
    arrays["l1_w"] = _np.stack([i[f"L1_attn_W{k}"] for k in ("q", "k", "v", "rk", "rv")])
    arrays["l1_cols"] = _np.stack([i[f"L1_attn_b{k}"] for k in ("q", "k", "rk")]).T
    arrays["l1_rows"] = _np.stack([i[f"L1_attn_b{k}"] for k in ("v", "rv")])
    arrays["l1_w2"] = _np.stack([i[f"L1_attn_W{k}"] for k in ("o", "rq")])
    arrays["l1_cols2"] = _np.stack([i[f"L1_attn_b{k}"] for k in ("o", "rq")]).T
    arrays["pastT"] = i["L1_attn_past_states"].reshape(512, 128).T
    arrays["moe1_gateT"] = i["L1_ffn_centroids"].T
    arrays["moe1_sharedT"] = i["L1_ffn_Ws"].transpose(0, 2, 1)
    arrays["moe1_wT"] = i["L1_ffn_Wr"].transpose(2, 0, 1).reshape(128, -1)
    arrays["ssm_cols"] = _np.stack([i[f"L2_attn_{k}"] for k in ("norm_g", "norm_b", "B_b", "C_b", "A_log")]).T
    arrays["ssm_w"] = _np.stack([i["L2_attn_B_w"].T, i["L2_attn_C_w"].T])
    ff1, ff2, ta, tb = (i[f"L2_attn_{k}_w"].T for k in ("ff1", "ff2", "ta", "tb"))
    rnn = _np.stack([_np.concatenate(p, axis=1) for p in ((ff1, ff2), (ta, ta), (tb, tb))])
    arrays["rnn_wx"] = rnn[:, :128]
    arrays["rnn_wh"] = _np.concatenate([rnn[:, 128:], rnn[:, 128:]], axis=1)
    arrays["rnn_b"] = _np.stack([_np.concatenate([i[f"L2_attn_{p}_b"], i[f"L2_attn_{q}_b"]]) for p, q in (("ff1", "ff2"), ("ta", "ta"), ("tb", "tb"))])
    arrays["rnn_out"] = _np.concatenate([i["L2_attn_out_w"].T] * 2)
    arrays["sign"] = _np.concatenate([-_np.ones((64, 1), f), _np.ones((64, 1), f)])
    arrays["bit_fastT"] = i["L2_ffn_fast_b"].T
    arrays["bit_uT"] = i["L2_ffn_u"].T
    arrays["bit_gate"] = i["L2_ffn_gate"].reshape(1, 1)
    arrays["m_cols"] = _np.concatenate([
        i["L3_attn_block_norm_w"][:, :, None],
        i["L3_attn_conv_w"].reshape(4, 4, 128, 4).transpose(0, 2, 1, 3).reshape(4, 128, 16),
        i["L3_attn_conv_b"].reshape(4, 4, 128).transpose(0, 2, 1),
        i["L3_attn_gate_norm_w"].reshape(4, 2, 128).transpose(0, 2, 1)], axis=2)
    arrays["m_rows"] = _np.concatenate([i["L3_attn_dt_bias"], i["L3_attn_A_log"], i["L3_attn_D"]], axis=1)
    delta = _np.zeros((40, 8, 128), f)
    delta[0:8] = -_np.eye(8, dtype=f)[:, :, None]
    delta[32:40] = _np.eye(8, dtype=f)[:, :, None]
    arrays["m_delta"] = delta
    arrays["tri"] = _np.triu(_np.ones((128, 128), f))
    arrays["moe3_gateT"] = i["L3_ffn_gate_weight"].T
    arrays["moe3_gate_upT"] = i["L3_ffn_gate_up_proj"].transpose(2, 0, 1)
    arrays["moe3_downT"] = i["L3_ffn_down_proj"].transpose(2, 0, 1)
    arrays["moe3_rep"] = _np.tile(_np.eye(8, dtype=f), (1, 16))
    arrays["moe3_blocks"] = _np.kron(_np.eye(16, dtype=f), _np.ones((8, 8), f))

    nc = _bacc.Bacc("TRN2", target_bir_lowering=False, num_devices=1)
    feed, dram = {}, {}
    for name, a in arrays.items():
        a = _np.ascontiguousarray(a)
        feed[f"in_{name}"] = a
        dram[name] = nc.dram_tensor(f"in_{name}", a.shape, _mybir.dt.from_np(a.dtype), kind="ExternalInput").ap()
    out = nc.dram_tensor("out_x", (4, 512, 128), _mybir.dt.float32, kind="ExternalOutput").ap()
    program(nc, dram, out)
    r = _run(nc, [feed], core_ids=[0])
    return r.results[0]["out_x"]
```

```python
from contextlib import ExitStack

import concourse.bass as bass
from concourse import mybir

P = 128
BATCH, SEQ, D = 4, 512, 128
TOK = BATCH * SEQ
TILES = TOK // P
QT = SEQ // P
BANK = 512
EPS = 1e-5
MASKED = -1e30

HEADS = 16
L0_DH = 16
L0_EXP = HEADS * L0_DH
L1_DH = D // HEADS
PAST_SETS, PAST = 2, 256
PARTS = 3

MOE0_E, MOE0_H = 8, 512
MOE1_E, MOE1_S = 16, 2
RNN_H = 64
BIT_H, BIT_R = 512, 16
M_LAYERS, M_INNER, M_STATE, M_HEADS, M_HD, M_CONV = 4, 256, 128, 8, 32, 4
M_PROJ = 2 * M_INNER + 2 * M_STATE + M_HEADS
MOE3_E, MOE3_F = 8, 128
THRESHOLD = 0.7

F32 = mybir.dt.float32
BF16 = mybir.dt.bfloat16
ALU = mybir.AluOpType
ACT = mybir.ActivationFunctionType
AX = mybir.AxisListType

QUERY_PART = (0, 0, 1, 1, 0, 2)
KEY_PART = (0, 1, 0, 1, 2, 0)
PAIRS = len(QUERY_PART)


class Core:

    def __init__(self, nc, ctx, dram):
        self.nc, self.dram = nc, dram
        self.X = ctx.enter_context(nc.sbuf_tensor("X", [P, TILES, D], F32))
        self.XT = ctx.enter_context(nc.sbuf_tensor("XT", [P, TOK], F32))
        self.ps = ctx.enter_context(nc.psum_tensor("ps", [P, 8, BANK], F32))
        self.ident = ctx.enter_context(nc.sbuf_tensor("ident", [P, P], F32))
        self.ident_bf = ctx.enter_context(nc.sbuf_tensor("ident_bf", [P, P], BF16))
        self.mask_q = ctx.enter_context(nc.sbuf_tensor("mask_q", [P, P], BF16))
        self.mask_k = ctx.enter_context(nc.sbuf_tensor("mask_k", [P, P], BF16))
        self.w_routed = ctx.enter_context(nc.sbuf_tensor("w_routed", [P, MOE1_E * D], F32))
        self.w_routed_in = nc.alloc_semaphore(name="w_routed_in")
        self.stored = nc.alloc_semaphore(name="stored")
        self.tri = ctx.enter_context(nc.sbuf_tensor("tri", [P, P], F32))
        self.all_ones = ctx.enter_context(nc.sbuf_tensor("all_ones", [P, P], F32))
        self.half_neg = ctx.enter_context(nc.sbuf_tensor("half_neg", [P, TILES], F32))


class Scope:

    def __init__(self, core, name):
        self.nc, self.name, self.ctx, self.sems = core.nc, name, ExitStack(), []

    def __enter__(self):
        self.ctx.__enter__()
        return self

    def __exit__(self, *a):
        if self.sems:
            self.nc.clear_and_free_semaphores(self.sems)
            self.nc.all_engine_barrier()
        return self.ctx.__exit__(*a)

    def sb(self, name, shape, dt=F32):
        return self.ctx.enter_context(self.nc.sbuf_tensor(f"{self.name}_{name}", shape, dt))

    def sem(self, name):
        self.sems.append(self.nc.alloc_semaphore(name=f"{self.name}_{name}"))
        return self.sems[-1]

    def block(self):
        return self.nc.Block()


class Chain:

    def __init__(self, eng, sem):
        self.eng, self.sem, self.n = eng, sem, 0

    def __call__(self, ins):
        self.n += 1
        ins.then_inc(self.sem, 1)
        self.eng.wait_ge(self.sem, self.n)

    def mark(self, ins):
        self.n += 1
        ins.then_inc(self.sem, 1)

    def wait(self):
        self.eng.wait_ge(self.sem, self.n)


GROUP = TILES // 4


def norm_stats(v, ve_done, chain, src, stats, mv, g):
    for t in range(g * GROUP, (g + 1) * GROUP):
        chain.mark(v.bn_stats(stats[:, t, :], src[:, t, :]))
    chain.wait()
    for t in range(g * GROUP, (g + 1) * GROUP):
        last = v.bn_aggr(mv[:, t, :], stats[:, t, :])
        if t < (g + 1) * GROUP - 1:
            chain.mark(last)
    last.then_inc(ve_done, 1)


def norm_apply(v, pool_done, done, src, dst, mv, rstd, g):
    v.wait_ge(pool_done, 2 * g + 2)
    for t in range(g * GROUP, (g + 1) * GROUP):
        ins = v.tensor_scalar(dst[:, t, :], src[:, t, :], mv[:, t, 0:1], rstd[:, t:t + 1], ALU.subtract, ALU.mult)
        if isinstance(done, Chain):
            done.mark(ins)
        else:
            ins.then_inc(done, 1)


def norm_tokens(v, pool_done, ve_done, chain, src, dst, stats, mv, rstd):
    for g in range(4):
        norm_stats(v, ve_done, chain, src, stats, mv, g)
    for g in range(4):
        norm_apply(v, pool_done, ve_done, src, dst, mv, rstd, g)


def rstd_group(g, core, pool_done, ve_done, mv, rstd, n):
    cols = slice(n * GROUP, (n + 1) * GROUP)
    g.wait_ge(ve_done, n + 1)
    g.tensor_scalar(rstd[:, cols], mv[:, cols, 1], EPS, None, ALU.add).then_inc(pool_done, 1)
    g.wait_ge(pool_done, 2 * n + 1)
    g.tensor_tensor(rstd[:, cols], rstd[:, cols], core.half_neg[:, cols], ALU.pow).then_inc(pool_done, 1)


def rstd_tokens(g, core, pool_done, ve_done, mv, rstd):
    for n in range(4):
        rstd_group(g, core, pool_done, ve_done, mv, rstd, n)


def prepare(core):
    d = core.dram
    with Scope(core, "prep") as s:
        masks = s.sb("masks", [P, 2, P])
        loaded = s.sem("loaded")
        made = s.sem("made")
        with s.block() as block:
            @block.sync
            def _(sp):
                sp.dma_start(core.X[:], d["L0_attn_x"].rearrange("b (q p) d -> p (b q) d", p=P)).then_inc(loaded, 16)
                sp.dma_start(core.ident[:], d["ident"]).then_inc(loaded, 16)
                sp.dma_start(masks[:], d["masks"].rearrange("m p n -> p m n")).then_inc(loaded, 16)
                sp.dma_start(core.w_routed[:], d["moe1_wT"]).then_inc(core.w_routed_in, 16)
                sp.wait_ge(loaded, 48)

            @block.vector
            def _(v):
                v.memset(core.half_neg[:], -0.5).then_inc(made, 1)
                v.wait_ge(loaded, 48)
                v.tensor_copy(core.ident_bf[:], core.ident[:]).then_inc(made, 1)
                v.tensor_copy(core.mask_q[:], masks[:, 0, :]).then_inc(made, 1)
                v.tensor_copy(core.mask_k[:], masks[:, 1, :]).then_inc(made, 1)


def l0_project(core, buf, scr):
    nc, d = core.nc, core.dram
    V, G = buf["V"], buf["gate"]
    with Scope(core, "l0p") as s:
        w = s.sb("w", [P, 4 * L0_EXP + HEADS])
        bias_y = s.sb("bias_y", [HEADS, 1])
        bias_vp = s.sb("bias_vp", [P, 2 * L0_EXP])
        cols = s.sb("cols", [P, 10])
        lnw, hp, bias_qk = cols[:, 0:2], cols[:, 2:6], cols[:, 6:10]
        qs = s.sb("qs", [P, 2])
        bq = s.sb("bq", [P, 2])
        sm = s.sb("sm", [P, 2])
        oms = s.sb("oms", [P, 2])
        stats = s.sb("stats", [P, TILES, 6])
        mv = s.sb("mv", [P, TILES, 2])
        rstd = s.sb("rstd", [P, TILES])
        xn = s.sb("xn", [P, TILES, D])
        xnT = s.sb("xnT", [P, TOK])
        qk = s.sb("qk", [P, 2, 4, SEQ])
        kraw = s.sb("kraw", [P, 2, SEQ])
        parts = s.sb("parts", [P, 2, PARTS, 4, SEQ], BF16)
        yv = s.sb("yv", [HEADS, TOK])
        ones = s.sb("ones", [HEADS, SEQ])
        pos = s.sb("pos", [HEADS, TOK])
        pparts = s.sb("pparts", [HEADS, PARTS, TOK], BF16)
        loaded, loaded2 = s.sem("loaded"), s.sem("loaded2")
        ve_done, pool_done, chain_s = s.sem("ve_done"), s.sem("pool_done"), s.sem("ve_chain")
        act_chain = s.sem("act_chain")
        transposed, xnT_ready = s.sem("transposed"), s.sem("xnT_ready")
        proj_done = s.sem("proj_done")
        q_ready, hi_done, rest_done = s.sem("q_ready"), s.sem("hi_done"), s.sem("rest_done")
        mid_done, lo_done = s.sem("mid_done"), s.sem("lo_done")
        y_ready, scales = s.sem("y_ready"), s.sem("scales")
        written = [s.sem(f"written{b}") for b in range(BATCH)]
        pos_written = s.sem("pos_written")
        k_ready, pos_hi, pos_rest = s.sem("k_ready"), s.sem("pos_hi"), s.sem("pos_rest")
        gates_in = s.sem("gates_in")
        pos_mid, pos_lo, v_ready = s.sem("pos_mid"), s.sem("pos_lo"), s.sem("v_ready")
        PER = 9

        def bank(n):
            return core.ps[:, 4 + n % 4, :]

        def wait_read(pe, n):
            b, j = divmod(n, PER)
            if j < 2:
                pe.wait_ge(q_ready, 2 * b + j + 1)
            elif j < 4:
                pe.wait_ge(k_ready, 2 * b + j - 1)
            elif j == 4:
                pe.wait_ge(y_ready, b + 1)
            else:
                pe.wait_ge(v_ready, QT * b + j - 4)

        with s.block() as block:
            @block.sync
            def _(sp):
                sp.dma_start(cols[:], d["l0_cols"]).then_inc(loaded, 16)
                sp.dma_start(bias_y[:], d["L0_attn_b_in"][4 * L0_EXP:].rearrange("(p c) -> p c", c=1)).then_inc(loaded, 16)
                sp.dma_start(w[:], d["l0_w_inT"]).then_inc(loaded2, 16)
                sp.dma_start(bias_vp[:], d["L0_attn_b_in"][2 * L0_EXP:4 * L0_EXP].rearrange("(a n) -> a n", a=1).broadcast_to([P, 2 * L0_EXP])).then_inc(loaded2, 16)
                for b in range(BATCH):
                    sp.wait_ge(lo_done, b + 1)
                    sp.dma_start(scr["qk"][b].rearrange("j (c p) t -> p (j c) t", p=P), parts[:, b % 2, :, :, :].rearrange("p j c t -> p (j c) t")).then_inc(written[b], 16)
                sp.wait_ge(pos_lo, BATCH)
                sp.dma_start(scr["pos"].rearrange("j b h t -> h (j b) t"), pparts[:].rearrange("h j (b t) -> h (j b) t", b=BATCH)).then_inc(pos_written, 16)
                sp.wait_ge(pos_written, 16)
                for b in range(BATCH):
                    sp.wait_ge(written[b], 16)

            @block.tensor
            def _(pe):
                for t in range(TILES):
                    pe.wait_ge(ve_done, t + 5)
                    m = pe.transpose(core.ps[:, t // 4, (t % 4) * P:(t % 4) * P + P], xn[:, t, :], core.ident[:])
                    if t % 4 == 3:
                        m.then_inc(transposed, 1)
                pe.wait_ge(loaded2, 32)
                for b in range(BATCH):
                    pe.wait_ge(xnT_ready, b + 1)
                    xb = xnT[:, b * SEQ:(b + 1) * SEQ]
                    for j in range(PER):
                        n = b * PER + j
                        if n >= 4:
                            wait_read(pe, n - 4)
                        out = bank(n)
                        if j < 4:
                            pe.matmul(out, w[:, j * P:(j + 1) * P], xb, start=True, stop=True).then_inc(proj_done, 1)
                        elif j == 4:
                            pe.matmul(out[0:HEADS, :], w[:, 4 * L0_EXP:], xb, start=True, stop=True).then_inc(proj_done, 1)
                        else:
                            q = j - 5
                            pe.matmul(out, xb[:, q * P:(q + 1) * P], w[:, 2 * L0_EXP:4 * L0_EXP], start=True, stop=True).then_inc(proj_done, 1)

            @block.scalar
            def _(a):
                own = Chain(a, act_chain)
                a.wait_ge(loaded, 32)
                a.activation(qs[:], hp[:, 0:2], ACT.Exp, scale=-2.0).then_inc(scales, 1)
                a.activation(sm[:], hp[:, 2:4], ACT.Sigmoid).then_inc(scales, 1)
                for g in range(4):
                    a.wait_ge(transposed, g + 1)
                    a.activation(xnT[:, g * BANK:(g + 1) * BANK], core.ps[:, g, :], ACT.Identity, scale=lnw[:, 0:1], bias=lnw[:, 1:2]).then_inc(xnT_ready, 1)

                def high_middle(b):
                    cols = slice(b * SEQ, (b + 1) * SEQ)
                    a.wait_ge(pos_rest, 2 * b + 1)
                    a.activation(pparts[:, 0, cols], pos[:, cols], ACT.Copy).then_inc(pos_hi, 1)
                    a.wait_ge(pos_rest, 2 * b + 2)
                    a.activation(pparts[:, 1, cols], pos[:, cols], ACT.Copy).then_inc(pos_mid, 1)

                a.wait_ge(gates_in, 1)
                for b in range(BATCH):
                    for j in (0, 1):
                        n = b * PER + j
                        a.wait_ge(proj_done, n + 1)
                        if b >= 2:
                            a.wait_ge(rest_done, b - 1)
                            a.wait_ge(hi_done, b - 1)
                        a.activation(qk[:, b % 2, j, :], bank(n), ACT.Identity, scale=qs[:, j:j + 1], bias=bq[:, j:j + 1]).then_inc(q_ready, 1)
                    n = b * PER + 4
                    a.wait_ge(proj_done, n + 1)
                    a.activation(yv[:, b * SEQ:(b + 1) * SEQ], bank(n)[0:HEADS, :], ACT.Sigmoid, bias=bias_y[:]).then_inc(y_ready, 1)
                    a.wait_ge(k_ready, 2 * b + 2)
                    a.wait_ge(q_ready, 2 * b + 2)
                    if b >= 2:
                        a.wait_ge(written[b - 2], 16)
                    a.activation(parts[:, b % 2, 0, :, :], qk[:, b % 2, :, :], ACT.Copy).then_inc(hi_done, 1)
                    if b >= 1:
                        high_middle(b - 1)
                    a.wait_ge(rest_done, b + 1)
                    a.activation(parts[:, b % 2, 1, :, :], qk[:, b % 2, :, :], ACT.Copy).then_inc(mid_done, 1)
                high_middle(BATCH - 1)
                a.wait_ge(v_ready, TILES)
                a.activation(G[:], G[:], ACT.Silu).then_inc(own.sem, 1)

            @block.gpsimd
            def _(g):
                rstd_tokens(g, core, pool_done, ve_done, mv, rstd)

            @block.vector
            def _(v):
                own = Chain(v, chain_s)
                own.mark(v.memset(ones[:], 1.0))
                own.mark(v.memset(V[:, :, :, L0_DH:L0_DH + 1], 1.0))
                norm_tokens(v, pool_done, ve_done, own, core.X, xn, stats, mv, rstd)
                v.wait_ge(scales, 2)
                own(v.tensor_scalar(qs[:], qs[:], float(L0_DH) ** -0.5, None, ALU.mult))
                own(v.tensor_scalar(oms[:], sm[:], -1.0, 1.0, ALU.mult, ALU.add))
                v.tensor_tensor(bq[:], qs[:], bias_qk[:, 0:2], ALU.mult).then_inc(gates_in, 1)
                v.wait_ge(loaded2, 32)

                def pos_less_high(b):
                    cols = slice(b * SEQ, (b + 1) * SEQ)
                    v.wait_ge(pos_rest, 2 * b + 1)
                    v.wait_ge(pos_hi, b + 1)
                    v.tensor_tensor(pos[:, cols], pos[:, cols], pparts[:, 0, cols], ALU.subtract).then_inc(pos_rest, 1)

                def pos_low(b):
                    cols = slice(b * SEQ, (b + 1) * SEQ)
                    v.wait_ge(pos_rest, 2 * b + 2)
                    v.wait_ge(pos_mid, b + 1)
                    v.tensor_tensor(pparts[:, 2, cols], pos[:, cols], pparts[:, 1, cols], ALU.subtract).then_inc(pos_lo, 1)

                for b in range(BATCH):
                    for j in (2, 3):
                        n = b * PER + j
                        c = j - 2
                        v.wait_ge(proj_done, n + 1)
                        own(v.tensor_scalar(kraw[:, c, :], bank(n), bias_qk[:, j:j + 1], None, ALU.add))
                        own(v.tensor_scalar(qk[:, b % 2, j, :], kraw[:, c, :], oms[:, c:c + 1], None, ALU.mult))
                        v.scalar_tensor_tensor(out=qk[:, b % 2, j, 1:], in0=kraw[:, c, 0:SEQ - 1], scalar=sm[:, c:c + 1], in1=qk[:, b % 2, j, 1:], op0=ALU.mult, op1=ALU.add).then_inc(k_ready, 1)
                    for j in range(5, PER):
                        n = b * PER + j
                        t = b * QT + j - 5
                        v.wait_ge(proj_done, n + 1)
                        out = bank(n)
                        own.mark(v.tensor_tensor(V[:, t, :, 0:L0_DH], out[:, 0:L0_EXP].rearrange("p (h e) -> p h e", h=HEADS), bias_vp[:, 0:L0_EXP].rearrange("p (h e) -> p h e", h=HEADS), ALU.add))
                        v.tensor_tensor(G[:, t, :], out[:, L0_EXP:], bias_vp[:, L0_EXP:], ALU.add).then_inc(v_ready, 1)
                    if b >= 1:
                        pos_less_high(b - 1)
                    v.wait_ge(hi_done, b + 1)
                    v.tensor_tensor(qk[:, b % 2, :, :], qk[:, b % 2, :, :], parts[:, b % 2, 0, :, :], ALU.subtract).then_inc(rest_done, 1)
                    v.wait_ge(mid_done, b + 1)
                    v.wait_ge(rest_done, b + 1)
                    v.tensor_tensor(parts[:, b % 2, 2, :, :], qk[:, b % 2, :, :], parts[:, b % 2, 1, :, :], ALU.subtract).then_inc(lo_done, 1)
                    if b >= 1:
                        pos_low(b - 1)
                    v.wait_ge(y_ready, b + 1)
                    v.tensor_tensor_scan(pos[:, b * SEQ:(b + 1) * SEQ], ones[:], yv[:, b * SEQ:(b + 1) * SEQ], 0.0, ALU.mult, ALU.add).then_inc(pos_rest, 1)
                pos_less_high(BATCH - 1)
                pos_low(BATCH - 1)


class Plan:
    pass


def causal_plan():
    p = Plan()
    p.dh, p.kinds, p.keys = L0_DH, 1, SEQ
    p.rows = [(q, 0, (q + 1) * P, True, 0) for q in range(QT)]
    p.cols = [[(0, 0, 0, 0, 512, True), (1, 0, 1, 128, 384, True), (1, 384, 3, 384, 128, True)],
              [(2, 0, 2, 256, 256, True)]]
    p.exps = [(0, 1024, 0), (2, 256, 1024)]
    p.accs = 1
    return p


def full_plan():
    p = Plan()
    p.dh, p.kinds, p.keys = L1_DH, 1, SEQ
    p.rows = [(q, 0, SEQ, False, 0) for q in range(QT)]
    p.cols = [[(0, 0, 0, 0, 512, False), (1, 0, 1, 0, 512, False)],
              [(2, 0, 2, 0, 512, False), (3, 0, 3, 0, 512, False)]]
    p.exps = [(0, 1024, 0), (2, 1024, 1024)]
    p.accs = 1
    return p


def recursive_plan():
    p = full_plan()
    p.kinds = PAST_SETS
    p.rows = [(q, 0, SEQ, False, None) for q in range(QT)]
    p.accs = PAST_SETS
    return p


UNIT = 4
UNITS = HEADS // UNIT


def attention(core, name, plan, scr, V, O):
    DH = plan.dh
    W = DH + 1
    SETS = plan.kinds
    NR = len(plan.rows)
    base = PAIRS * DH
    POS = PARTS if name == "l0a" else 0
    RA = base + POS
    RB = RA + PARTS * SETS
    COLS = 1280 if name == "l0a" else 2048
    U = 4 // SETS
    G = UNIT // U
    GROUPS = HEADS // U
    shared = SETS == 2
    with Scope(core, name) as s:
        QS = s.sb("QS", [RB, 2, HEADS, SEQ], BF16)
        NK = 1 if shared else 2
        KS = s.sb("KS", [RB, NK, HEADS, SEQ], BF16)
        set_rows = s.sb("set_rows", [SETS, SEQ], BF16) if shared else None
        set_rows32 = s.sb("set_rows32", [SETS, SEQ]) if shared else None
        sets_in, sets_made = s.sem("sets_in"), s.sem("sets_made")
        table_in = s.sem("table_in")
        warm = s.sb("warm", [1, 1])
        MXR = SETS * UNIT * QT
        mx = s.sb("mx", [P, SETS, UNIT, QT])
        mxs = s.sb("mxs", [P, MXR])
        nm = s.sb("nm", [MXR, P])
        mparts = s.sb("mparts", [MXR, PARTS, P], BF16)
        mx_copied = s.sem("mx_copied")
        PT = s.sb("PT", [P, 2, COLS])
        VS = s.sb("VS", [P, 2, QT, 32])
        ST = s.sb("ST", [P, SEQ])
        den = s.sb("den", [P, QT, 4])
        tmp = s.sb("tmp", [P, QT, U, SETS, DH]) if shared else None
        loaded_q = [s.sem(f"queries_in{i}") for i in range(2)]
        loaded_k = [s.sem(f"keys_in{i}") for i in range(2)]
        filled, sets_written = s.sem("filled"), s.sem("sets_written")
        maxima_in = s.sem("maxima_in")
        row_scores, row_max = s.sem("row_scores"), s.sem("row_max")
        turned, negated = s.sem("maxima_turned"), s.sem("maxima_negated")
        m_hi, m_rest, m_mid, m_split = s.sem("m_hi"), s.sem("m_rest"), s.sem("m_mid"), s.sem("m_split")
        scored, weighed = s.sem("scored"), s.sem("weighed")
        staged, valued, taken, turned_out = s.sem("values_staged"), s.sem("valued"), s.sem("sums_taken"), s.sem("sums_turned")
        padded, normed, recips, halves = s.sem("padded"), s.sem("normed"), s.sem("recips"), s.sem("halves")
        row_banks = [0, 1]

        def fill(sp):
            ones = core.dram["ones"].unsqueeze(1)
            for i in range(2):
                sp.dma_start(QS[base:RB, i, :, :], ones.broadcast_to([RB - base, HEADS, SEQ])).then_inc(filled, 16)
            for i in range(NK):
                sp.dma_start(KS[base:RB, i, :, :], ones.broadcast_to([RB - base, HEADS, SEQ])).then_inc(filled, 16)

        def queries(sp, b):
            for g, part in enumerate(QUERY_PART):
                sp.dma_start(QS[g * DH:(g + 1) * DH, b % 2, :, :], scr["qk"][b, part, 0:HEADS * DH].rearrange("(h e) t -> e h t", e=DH)).then_inc(loaded_q[b % 2], 16)

        def keys(sp, b, filling=False):
            for g, part in enumerate(KEY_PART):
                sp.dma_start(KS[g * DH:(g + 1) * DH, b % NK, :, :], scr["qk"][b if not shared else 0, part, HEADS * DH:].rearrange("(h e) t -> e h t", e=DH)).then_inc(loaded_k[b % 2], 16)
            if filling:
                fill(sp)
                sp.wait_ge(filled, 16 * (2 + NK))
            for j in range(POS):
                sp.dma_start(KS[base + j:base + j + 1, b % NK, :, :], scr["pos"][j:j + 1, b]).then_inc(loaded_k[b % 2], 16)

        K_DMAS = PAIRS + POS

        def peeled(b, half):
            return half == 0 or b == BATCH - 1

        with s.block() as block:
            @block.sync
            def _(sp):
                if shared:
                    sp.dma_start(set_rows32[:], core.dram["set_rows"]).then_inc(sets_in, 16)

                def loads(b):
                    if b >= 2:
                        sp.wait_ge(scored, (b - 1) * HEADS * 2)
                    queries(sp, b)
                    if not shared or b == 0:
                        keys(sp, b, filling=b == 0)
                    if shared and b == 0:
                        sp.wait_ge(sets_made, 1)
                        for k in range(SETS):
                            for j in range(PARTS):
                                r = RA + PARTS * k + j
                                sp.dma_start(KS[r:r + 1, 0, :, :], set_rows[k:k + 1, :].unsqueeze(1).broadcast_to([1, HEADS, SEQ])).then_inc(sets_written, 16)

                loads(0)
                for b in range(BATCH):
                    for i in range(UNITS):
                        sp.wait_ge(m_split, b * UNITS + i + 1)
                        for k in range(SETS):
                            n = UNIT * QT
                            for j in range(PARTS):
                                r = RA + PARTS * k + j
                                sp.dma_start(QS[r:r + 1, b % 2, UNIT * i:UNIT * (i + 1), :], mparts[n * k:n * (k + 1), j, :]).then_inc(maxima_in, 16)
                        if i == 0 and b + 1 < BATCH:
                            loads(b + 1)

            @block.tensor
            def _(pe):
                def rows(b, h, n, which=range(NR)):
                    for i in which:
                        q, k0, kn, masked, _ = plan.rows[i]
                        if i >= 2 or not (isinstance(n, int) and n == 0):
                            pe.wait_ge(row_max, n * NR + i - 1)
                        out = core.ps[:, row_banks[i % 2], 0:kn]
                        m = pe.matmul(out, QS[0:RA, b % 2, h, q * P:(q + 1) * P], KS[0:RA, b % NK, h, k0:k0 + kn], start=True, stop=not masked)
                        if masked:
                            m = pe.matmul(out[:, kn - P:kn], core.ident_bf[:], core.mask_q[:], start=False, stop=True)
                        m.then_inc(row_scores, 1)

                def turn(u, m):
                    pe.wait_ge(mx_copied, u + 1)
                    if not (isinstance(m, int) and m == 0):
                        pe.wait_ge(normed, m)
                    pe.transpose(core.ps[0:MXR, 7, 0:P], mxs[:], core.ident[:]).then_inc(turned, 1)

                def weigh(b, h, n, g):
                    group = plan.cols[g]
                    if not (isinstance(n, int) and n == 0):
                        pe.wait_ge(weighed, 2 * n + (g - 1))
                    for slot, col, kt, q0, qn, masked in group:
                        out = core.ps[:, 2 + slot, col:col + qn]
                        m = pe.matmul(out, KS[0:RB, b % NK, h, kt * P:(kt + 1) * P], QS[0:RB, b % 2, h, q0:q0 + qn], start=True, stop=not masked)
                        if masked:
                            m = pe.matmul(out[:, 0:P], core.ident_bf[:], core.mask_k[:], start=False, stop=True)
                    m.then_inc(scored, 1)

                def values(j, par, n, m):
                    if j == 0 and not (isinstance(m, int) and m == 0):
                        pe.wait_ge(taken, m)
                    pe.wait_ge(staged, n + 1)
                    for g, group in enumerate(plan.cols):
                        pe.wait_ge(weighed, 2 * n + (g + 1))
                        for slot, col, kt, q0, qn, masked in group:
                            off = plan.exps[g][2] + (slot - plan.exps[g][0]) * BANK + col
                            kset = kt // 2 if shared else 0
                            r = 32 * (j * SETS + kset)
                            lead = kt % 2 == 0 if shared else kt == 0
                            tail = kt % 2 == 1 if shared else (g == 1 and (slot, col, kt, q0, qn, masked) == group[-1])
                            mm = pe.matmul(core.ps[r:r + 32, 6, q0:q0 + qn], VS[:, par, kt, :], PT[:, par, off:off + qn], start=lead, stop=tail, skip_group_check=True)
                    mm.then_inc(valued, 1)

                def turn_out(m, u):
                    pe.wait_ge(taken, m + 1)
                    pe.wait_ge(negated, u)
                    if not (isinstance(m, int) and m == 0):
                        pe.wait_ge(normed, m)
                    for q in range(QT):
                        mm = pe.transpose(core.ps[:, 7, q * P:(q + 1) * P], ST[:, q * P:(q + 1) * P], core.ident[:])
                    mm.then_inc(turned_out, 1)

                def body(b, half, i):
                    g = i + (b * UNITS + 2 * half)
                    first, last = isinstance(g, int) and g == 0, b == BATCH - 1
                    rb, rh = (b, 2) if half == 0 else (b + 1, 0)
                    m0 = G * g
                    more = not (last and half == 1 and i == 1)
                    units_turned = g + 2 if more else g + 1
                    if more and POS:
                        turn(g + 1, 0 if first else m0 - 1)
                    pe.wait_ge(maxima_in, 16 * PARTS * SETS * (g + 1))
                    for j in range(UNIT):
                        h = UNIT * i + (j + 2 * UNIT * half)
                        n = UNIT * g + j
                        m = m0 + j // U
                        for k, which in enumerate(((0, 1), (2,))):
                            if rb < BATCH:
                                rows(rb, UNIT * i + (j + rh * UNIT), n + 2 * UNIT, which)
                            weigh(b, h, n, k)
                        if rb < BATCH:
                            rows(rb, UNIT * i + (j + rh * UNIT), n + 2 * UNIT, (3,))
                        if j == 0 and more and not POS:
                            turn(g + 1, 0 if first else m0 - 1)
                        if j % U == 1 and not (first and j == 1):
                            turn_out(m - 1, units_turned)
                        if not (first and j == 0):
                            values((j - 1) % U, (j - 1) % 2, n - 1, m if j % U else m - 1)

                pe.wait_ge(loaded_q[0], 16 * PAIRS)
                pe.wait_ge(loaded_k[0], 16 * K_DMAS)
                if POS:
                    pe.wait_ge(filled, 16 * (2 + NK))
                for j in range(UNIT):
                    rows(0, j, j)
                turn(0, 0)
                for j in range(UNIT, 2 * UNIT):
                    rows(0, j, j)
                pe.wait_ge(negated, 1)
                if not POS:
                    pe.wait_ge(filled, 16 * (2 + NK))
                if shared:
                    pe.wait_ge(sets_written, 16 * SETS * PARTS)
                for b in range(BATCH):
                    for half in range(2):
                        if half == 1 and b < BATCH - 1:
                            pe.wait_ge(loaded_q[(b + 1) % 2], 16 * PAIRS * ((b + 1) // 2 + 1))
                            if not shared:
                                pe.wait_ge(loaded_k[(b + 1) % 2], 16 * K_DMAS * ((b + 1) // 2 + 1))
                        if peeled(b, half):
                            body(b, half, 0)
                            body(b, half, 1)
                        else:
                            with pe.Fori(0, 2) as i:
                                body(b, half, i)
                values(U - 1, 1, BATCH * HEADS - 1, BATCH * HEADS // U - 1)
                turn_out(BATCH * HEADS // U - 1, BATCH * UNITS)

            @block.scalar
            def _(a):
                def exps(par, n):
                    for g, (slot, cols, at) in enumerate(plan.exps):
                        a.wait_ge(scored, 2 * n + (g + 1))
                        if not (isinstance(n, int) and n < 2):
                            a.wait_ge(valued, n - 1)
                        if cols > BANK:
                            a.activation(PT[:, par, at:at + cols].rearrange("p (s n) -> p s n", s=2), core.ps[:, 2 + slot:4 + slot, :], ACT.Exp).then_inc(weighed, 1)
                        else:
                            a.activation(PT[:, par, at:at + cols], core.ps[:, 2 + slot, 0:cols], ACT.Exp).then_inc(weighed, 1)

                def take(m):
                    a.wait_ge(valued, U * m + U)
                    if not (isinstance(m, int) and m == 0):
                        a.wait_ge(turned_out, m)
                    a.activation(ST[:], core.ps[:, 6, :], ACT.Copy).then_inc(taken, 1)

                def negate(u):
                    a.wait_ge(turned, u + 1)
                    if not (isinstance(u, int) and u == 0):
                        a.wait_ge(m_split, u)
                        a.wait_ge(maxima_in, 16 * PARTS * SETS * u)
                    a.activation(nm[:], core.ps[0:MXR, 7, 0:P], ACT.Copy, scale=2.0).then_inc(negated, 1)
                    a.wait_ge(negated, u + 1)
                    a.activation(mparts[:, 0, :], nm[:], ACT.Copy).then_inc(m_hi, 1)

                def middle(u):
                    a.wait_ge(m_rest, u + 1)
                    a.activation(mparts[:, 1, :], nm[:], ACT.Copy).then_inc(m_mid, 1)

                def body(b, half, i):
                    g = i + (b * UNITS + 2 * half)
                    first, last = isinstance(g, int) and g == 0, b == BATCH - 1 and half == 1 and i == 1
                    for j in range(UNIT):
                        n = UNIT * g + j
                        m = G * g + j // U
                        exps(j % 2, n)
                        if j % U == 0 and not (first and j == 0):
                            take(m - 1)
                        if j == 0 and not last:
                            negate(g + 1)
                        if j == 1 and not last:
                            middle(g + 1)

                a.activation(warm[:], core.half_neg[0:1, 0:1], ACT.Exp).then_inc(table_in, 1)
                negate(0)
                middle(0)
                for b in range(BATCH):
                    for half in range(2):
                        if peeled(b, half):
                            body(b, half, 0)
                            body(b, half, 1)
                        else:
                            with a.Fori(0, 2) as i:
                                body(b, half, i)
                take(BATCH * HEADS // U - 1)

            @block.gpsimd
            def _(g):
                g.memset(VS[:], 0.0).then_inc(padded, 1)
                g.wait_ge(padded, 1)

                def stage(b, h, par, n):
                    if not (isinstance(n, int) and n < 2):
                        g.wait_ge(valued, n - 1)
                    g.tensor_copy(VS[:, par, :, 0:W], V[:, 0 if shared else b * QT:QT if shared else (b + 1) * QT, h, :]).then_inc(staged, 1)

                def copy_maxima(u):
                    g.wait_ge(row_max, (u + 1) * (UNIT * NR))
                    if not (isinstance(u, int) and u == 0):
                        g.wait_ge(turned, u)
                    flat = mx[:].rearrange("p k h q -> p (k h q)")
                    g.tensor_tensor(mxs[:], flat, core.half_neg[:, 0:1].broadcast_to([P, MXR]), ALU.mult).then_inc(mx_copied, 1)

                def body(b, half, i):
                    u = i + (b * UNITS + 2 * half)
                    if not (b == BATCH - 1 and half == 1 and i == 1):
                        copy_maxima(u + 1)
                    for j in range(UNIT):
                        stage(b, UNIT * i + (j + 2 * UNIT * half), j % 2, UNIT * u + j)

                copy_maxima(0)
                for b in range(BATCH):
                    for half in range(2):
                        if peeled(b, half):
                            body(b, half, 0)
                            body(b, half, 1)
                        else:
                            with g.Fori(0, 2) as i:
                                body(b, half, i)

            @block.vector
            def _(v):
                if shared:
                    v.wait_ge(sets_in, 16)
                    v.tensor_copy(set_rows[:], set_rows32[:]).then_inc(sets_made, 1)

                def maxima(j, n, u):
                    if j == 0 and not (isinstance(u, int) and u == 0):
                        v.wait_ge(mx_copied, u)
                    for i, (q, k0, kn, _, _) in enumerate(plan.rows):
                        v.wait_ge(row_scores, n * NR + i + 1)
                        src = core.ps[:, row_banks[i % 2], 0:kn]
                        if shared:
                            v.tensor_reduce(mx[:, :, j, q], src.rearrange("p (k n) -> p k n", k=SETS), AX.X, ALU.max).then_inc(row_max, 1)
                        else:
                            v.tensor_reduce(mx[:, 0, j, q:q + 1], src, AX.X, ALU.max).then_inc(row_max, 1)

                def norm(b, i, m):
                    v.wait_ge(turned_out, m + 1)
                    acc = core.ps[:, 7, :].rearrange("p (q j c) -> p q j c", q=QT, j=4)
                    v.reciprocal(den[:], acc[:, :, :, DH]).then_inc(recips, 1)
                    v.wait_ge(recips, m + 1)
                    out = O[:, b * QT:(b + 1) * QT, bass.ds(i * (U * DH), U * DH)].rearrange("p q (j e) -> p q j e", j=U)
                    over = den[:].unsqueeze(3).broadcast_to([P, QT, 4, DH])
                    if not shared:
                        v.tensor_tensor(out, acc[:, :, :, 0:DH], over, ALU.mult).then_inc(normed, 1)
                    else:
                        v.tensor_tensor(tmp[:].rearrange("p q j k e -> p q (j k) e"), acc[:, :, :, 0:DH], over, ALU.mult).then_inc(normed, 1)
                        v.wait_ge(normed, m + 1)
                        v.tensor_tensor(out, tmp[:, :, :, 0], tmp[:, :, :, 1], ALU.add).then_inc(halves, 1)

                def rest(u):
                    v.wait_ge(m_hi, u + 1)
                    v.tensor_tensor(nm[:], nm[:], mparts[:, 0, :], ALU.subtract).then_inc(m_rest, 1)

                def low(u):
                    v.wait_ge(m_rest, u + 1)
                    v.wait_ge(m_mid, u + 1)
                    v.tensor_tensor(mparts[:, 2, :], nm[:], mparts[:, 1, :], ALU.subtract).then_inc(m_split, 1)

                def body(b, half, i):
                    g = i + (b * UNITS + 2 * half)
                    first, last = isinstance(g, int) and g == 0, b == BATCH - 1 and half == 1 and i == 1
                    for j in range(UNIT):
                        m = G * g + j // U
                        if not (b == BATCH - 1 and half == 1):
                            maxima(j, UNIT * g + (j + 2 * UNIT), g + 2)
                        if j == 1 and not last:
                            rest(g + 1)
                        if j == 2 and not last:
                            low(g + 1)
                        if j % U == 1 and not (first and j == 1):
                            if j // U == 0 and half == 0 and isinstance(i, int) and i == 0:
                                norm(b - 1, GROUPS - 1, m - 1)
                            else:
                                norm(b, G * i + (2 * G * half + j // U - 1), m - 1)

                for j in range(UNIT):
                    maxima(j, j, 0)
                rest(0)
                low(0)
                for j in range(UNIT):
                    maxima(j, j + UNIT, 1)
                for b in range(BATCH):
                    for half in range(2):
                        if peeled(b, half):
                            body(b, half, 0)
                            body(b, half, 1)
                        else:
                            with v.Fori(0, 2) as i:
                                body(b, half, i)
                norm(BATCH - 1, GROUPS - 1, BATCH * HEADS // U - 1)


def l0_finish(core, buf):
    d = core.dram
    V, G, O = buf["V"], buf["gate"], buf["O"]
    with Scope(core, "l0f") as s:
        wo = s.sb("wo", [P, 2, D])
        ln = s.sb("ln", [P, 2, D])
        gT = s.sb("gT", [P, 4, 2, P])
        y = s.sb("y", [P, TILES, D])
        stats = s.sb("stats", [P, TILES, 6])
        mv = s.sb("mv", [P, TILES, 2])
        rstd = s.sb("rstd", [P, TILES])
        x_ln = s.sb("x_ln", [P, TILES, D])
        stats2 = s.sb("stats2", [P, TILES, 6])
        mv2 = s.sb("mv2", [P, TILES, 2])
        rstd2 = s.sb("rstd2", [P, TILES])
        x_ready = s.sem("x_ready")
        loaded, gated, turned, copied = s.sem("loaded"), s.sem("gated"), s.sem("turned"), s.sem("copied")
        made, taken = s.sem("made"), s.sem("taken")
        ve_done, pool_done, chain_s = s.sem("ve_done"), s.sem("pool_done"), s.sem("ve_chain")
        ve_done2, pool_done2 = s.sem("ve_done2"), s.sem("pool_done2")
        with s.block() as block:
            @block.sync
            def _(sp):
                sp.dma_start(wo[:], d["l0_w_outT"].rearrange("(c p) n -> p c n", p=P)).then_inc(loaded, 16)
                sp.dma_start(ln[:], d["l0_out_ln"].rearrange("(a c) n -> a c n", a=1).broadcast_to([P, 2, D])).then_inc(loaded, 16)

            @block.tensor
            def _(pe):
                pe.wait_ge(loaded, 32)

                def project(t):
                    pe.wait_ge(copied, t + 1)
                    if t >= 4:
                        pe.wait_ge(taken, t - 3)
                    for c in range(2):
                        m = pe.matmul(core.ps[:, 4 + t % 4, 0:D], gT[:, t % 4, c, :], wo[:, c, :], start=(c == 0), stop=(c == 1))
                    m.then_inc(made, 1)

                for t in range(TILES):
                    pe.wait_ge(gated, t // 4 + 1)
                    if t >= 4:
                        pe.wait_ge(copied, t - 3)
                    for c in range(2):
                        m = pe.transpose(core.ps[:, t % 4, c * P:(c + 1) * P], G[:, t, c * P:(c + 1) * P], core.ident[:])
                    m.then_inc(turned, 1)
                    if t >= 1:
                        project(t - 1)
                project(TILES - 1)

            @block.scalar
            def _(a):
                for t in range(TILES):
                    a.wait_ge(turned, t + 1)
                    if t >= 4:
                        a.wait_ge(made, t - 3)
                    a.activation(gT[:, t % 4, :, :], core.ps[:, t % 4, 0:2 * P].rearrange("p (c n) -> p c n", c=2), ACT.Copy).then_inc(copied, 1)

            @block.gpsimd
            def _(g):
                g.wait_ge(loaded, 32)
                g.tensor_tensor(x_ln[:], core.X[:], ln[:, 1, :].unsqueeze(1).broadcast_to([P, TILES, D]), ALU.add).then_inc(x_ready, 1)
                for n in range(4):
                    rstd_group(g, core, pool_done, ve_done, mv, rstd, n)
                    if n >= 1:
                        rstd_group(g, core, pool_done2, ve_done2, mv2, rstd2, n - 1)
                rstd_group(g, core, pool_done2, ve_done2, mv2, rstd2, 3)

            @block.vector
            def _(v):
                own = Chain(v, chain_s)
                for b in range(BATCH):
                    v.tensor_tensor(G[:, b * QT:(b + 1) * QT, :], G[:, b * QT:(b + 1) * QT, :], O[:, b * QT:(b + 1) * QT, :], ALU.mult).then_inc(gated, 1)

                def second(n):
                    v.wait_ge(x_ready, 1)
                    norm_apply(v, pool_done, own, y, y, mv, rstd, n)
                    own.wait()
                    yg = y[:, n * GROUP:(n + 1) * GROUP]
                    own(v.tensor_tensor(yg, yg, ln[:, 0, :].unsqueeze(1).broadcast_to([P, GROUP, D]), ALU.mult))
                    own(v.tensor_tensor(yg, yg, x_ln[:, n * GROUP:(n + 1) * GROUP], ALU.add))
                    norm_stats(v, ve_done2, own, y, stats2, mv2, n)

                for t in range(TILES):
                    v.wait_ge(made, t + 1)
                    v.tensor_copy(y[:, t, :], core.ps[:, 4 + t % 4, 0:D]).then_inc(taken, 1)
                    if t % GROUP == GROUP - 1:
                        v.wait_ge(taken, t + 1)
                        norm_stats(v, ve_done, own, y, stats, mv, t // GROUP)
                        if t >= GROUP:
                            second(t // GROUP - 1)
                second(3)
                for n in range(4):
                    norm_apply(v, pool_done2, own, y, core.X, mv2, rstd2, n)


def store(core, out):
    with core.nc.Block() as block:
        @block.sync
        def _(sp):
            sp.dma_start(out.rearrange("b (q p) d -> p (b q) d", p=P), core.X[:]).then_inc(core.stored, 16)
            sp.wait_ge(core.stored, 16)


def turn_tokens(pe, core, turned, src, free=None):
    for t in range(TILES):
        m = pe.transpose(core.ps[:, t // 4, (t % 4) * P:(t % 4 + 1) * P], src[:, t, :], core.ident[:])
        if t % 4 == 3:
            m.then_inc(turned, 1)


def keep_turned(a, core, turned, kept):
    for g in range(4):
        a.wait_ge(turned, g + 1)
        a.activation(core.XT[:, g * BANK:(g + 1) * BANK], core.ps[:, g, :], ACT.Copy).then_inc(kept, 1)


def pick_two(v, own, rank, vals, work, hots, tops, E):
    key, best = work
    for k in range(2):
        own(v.tensor_reduce(tops[k][:], vals, AX.X, ALU.max))
        own(v.tensor_tensor(key[:], vals, tops[k][:].unsqueeze(2).broadcast_to([P, TILES, E]), ALU.is_equal))
        own(v.tensor_tensor(key[:], key[:], rank[:, 0:E].unsqueeze(1).broadcast_to([P, TILES, E]), ALU.mult))
        own(v.tensor_reduce(best[:], key[:], AX.X, ALU.max))
        own(v.tensor_tensor(hots[k][:], key[:], best[:].unsqueeze(2).broadcast_to([P, TILES, E]), ALU.is_equal))
        if k == 0:
            own(v.scalar_tensor_tensor(out=hots[1][:], in0=hots[0][:], scalar=MASKED, in1=vals, op0=ALU.mult, op1=ALU.add))
            vals = hots[1][:]


def mixture(core, name, E, ws, routed):
    d = core.dram
    H = E // 8
    UNITS = TILES * H
    with Scope(core, name) as s:
        gate_w = s.sb("gate_w", [P, E])
        rank = s.sb("rank", [P, 16])
        L = s.sb("L", [P, TILES, E])
        gates = s.sb("gates", [P, TILES, E])
        hots = [s.sb(f"hot{k}", [P, TILES, E]) for k in range(2)]
        key = s.sb("key", [P, TILES, E])
        best = s.sb("best", [P, TILES])
        tops = [s.sb(f"top{k}", [P, TILES]) for k in range(2)]
        e2 = s.sb("e2", [P, TILES])
        Z = s.sb("Z", [P, 2, 4, D])
        Z2 = s.sb("Z2", [P, 2, 2, D])
        R = s.sb("R", [P, UNITS, D])
        Y = s.sb("Y", [P, TILES, D])
        stats = s.sb("stats", [P, TILES, 6])
        mv = s.sb("mv", [P, TILES, 2])
        rstd = s.sb("rstd", [P, TILES])
        if routed:
            bias = s.sb("bias", [P, E])
            shared_w = s.sb("shared_w", [P, MOE1_S, D])
            shared_b = s.sb("shared_b", [MOE1_S, D])
            expert_b = s.sb("expert_b", [E, D])
            gT = s.sb("gT", [E, TOK])
            two = s.sb("two", [MOE1_S, P])
        loaded = s.sem("loaded")
        turned, kept, scored = s.sem("turned"), s.sem("kept"), s.sem("scored")
        made, weighed_v, weighed_a, added = s.sem("made"), s.sem("weighed_by_v"), s.sem("weighed_by_a"), s.sem("added")
        differ, exped, gated = s.sem("differences"), s.sem("exponentials"), s.sem("gated")
        gates_turned, gates_kept, extra, extra_read = s.sem("gates_turned"), s.sem("gates_kept"), s.sem("extra"), s.sem("extra_read")
        ve_done, pool_done, chain_s, pool_chain, twos = s.sem("ve_done"), s.sem("pool_done"), s.sem("ve_chain"), s.sem("pool_chain"), s.sem("twos")
        LOADS = 6 if routed else 2
        with s.block() as block:
            @block.sync
            def _(sp):
                sp.dma_start(gate_w[:], d["moe1_gateT" if routed else "moe0_gateT"]).then_inc(loaded, 16)
                sp.dma_start(rank[:], d["rank"].broadcast_to([P, 16])).then_inc(loaded, 16)
                if routed:
                    sp.dma_start(bias[:], d["L1_ffn_expert_biases"].rearrange("(a n) -> a n", a=1).broadcast_to([P, E])).then_inc(loaded, 16)
                    sp.dma_start(shared_w[:], d["moe1_sharedT"].rearrange("e i o -> i e o")).then_inc(loaded, 16)
                    sp.dma_start(shared_b[:], d["L1_ffn_bs"]).then_inc(loaded, 16)
                    sp.dma_start(expert_b[:], d["L1_ffn_br"]).then_inc(loaded, 16)

            @block.tensor
            def _(pe):
                turn_tokens(pe, core, turned, core.X)
                pe.wait_ge(loaded, 16 * LOADS)
                for t in range(TILES):
                    pe.wait_ge(kept, t // 4 + 1)
                    m = pe.matmul(core.ps[:, 7, t * E:(t + 1) * E], core.XT[:, t * P:(t + 1) * P], gate_w[:], start=True, stop=True)
                m.then_inc(scored, 1)
                if routed:
                    pe.wait_ge(twos, 1)
                    pe.wait_ge(core.w_routed_in, 16)

                def extras(t):
                    pe.wait_ge(gates_kept, t // 4 + 1)
                    if t >= 1:
                        pe.wait_ge(extra_read, t)
                    x = core.XT[:, t * P:(t + 1) * P]
                    for k in range(MOE1_S):
                        pe.matmul(core.ps[:, 6, 0:D], x, shared_w[:, k, :], start=(k == 0), stop=False)
                    pe.matmul(core.ps[:, 6, 0:D], two[:], shared_b[:], start=False, stop=True)
                    pe.matmul(core.ps[:, 6, D:2 * D], gT[:, t * P:(t + 1) * P], expert_b[:], start=True, stop=True).then_inc(extra, 1)

                for u in range(UNITS):
                    t, h = divmod(u, H)
                    if u >= 3:
                        pe.wait_ge(weighed_v, u - 2)
                        pe.wait_ge(weighed_a, u - 2)
                    for k in range(2):
                        c = (h * 8 + k * 4) * D
                        m = pe.matmul(core.ps[:, 2 * (u % 3) + k, :], core.XT[:, t * P:(t + 1) * P], ws[:, c:c + BANK], start=True, stop=True)
                    m.then_inc(made, 1)
                    if routed and u == 2:
                        pe.wait_ge(gated, 1)
                        for g in range(4):
                            if g:
                                pe.wait_ge(gates_kept, g)
                            for i in range(4):
                                m = pe.transpose(core.ps[0:E, 7, i * P:(i + 1) * P], gates[:, 4 * g + i, :], core.ident[:])
                            m.then_inc(gates_turned, 1)
                    if routed and t >= 2 and h == 1:
                        extras(t - 2)
                if routed:
                    extras(TILES - 2)
                    extras(TILES - 1)

            @block.scalar
            def _(a):
                keep_turned(a, core, turned, kept)
                a.wait_ge(differ, 1)
                if routed:
                    a.activation(L[:], L[:], ACT.Exp).then_inc(exped, 1)
                else:
                    a.activation(e2[:], e2[:], ACT.Exp).then_inc(exped, 1)
                a.wait_ge(gated, 1)
                for u in range(UNITS):
                    t, h = divmod(u, H)
                    if routed and u == 3:
                        for g in range(4):
                            a.wait_ge(gates_turned, g + 1)
                            a.activation(gT[:, g * BANK:(g + 1) * BANK], core.ps[0:E, 7, :], ACT.Copy).then_inc(gates_kept, 1)
                    a.wait_ge(made, u + 1)
                    if u >= 2:
                        a.wait_ge(added, u - 1)
                    for k in range(4):
                        e = h * 8 + 4 + k
                        m = a.activation(Z[:, u % 2, k, :], core.ps[:, 2 * (u % 3) + 1, k * D:(k + 1) * D], ACT.Copy, scale=gates[:, t, e:e + 1])
                    m.then_inc(weighed_a, 1)

            @block.gpsimd
            def _(g):
                own = Chain(g, pool_chain)
                if routed:
                    g.memset(two[:], 1.0).then_inc(twos, 1)
                for u in range(UNITS):
                    g.wait_ge(weighed_a, u + 1)
                    own(g.tensor_tensor(Z2[:, u % 2], Z[:, u % 2, 0:2], Z[:, u % 2, 2:4], ALU.add))
                    g.tensor_tensor(R[:, u, :], Z2[:, u % 2, 0], Z2[:, u % 2, 1], ALU.add).then_inc(added, 1)
                    t, h = divmod(u, H)
                    if h == H - 1 and t >= GROUP + 2 and t % GROUP == 2:
                        rstd_group(g, core, pool_done, ve_done, mv, rstd, t // GROUP - 1)
                rstd_group(g, core, pool_done, ve_done, mv, rstd, 3)

            @block.vector
            def _(v):
                own = Chain(v, chain_s)
                v.wait_ge(loaded, 16 * LOADS)
                v.wait_ge(scored, 1)
                scores = core.ps[:, 7, 0:TILES * E].rearrange("p (t e) -> p t e", e=E)

                def each(x):
                    return x[:].unsqueeze(2).broadcast_to([P, TILES, E])

                if routed:
                    own(v.tensor_tensor(L[:], scores, bias[:].unsqueeze(1).broadcast_to([P, TILES, E]), ALU.add))
                    own(v.tensor_reduce(best[:], L[:], AX.X, ALU.max))
                    v.tensor_tensor(L[:], L[:], each(best), ALU.subtract).then_inc(differ, 1)
                    v.wait_ge(exped, 1)
                    own(v.tensor_reduce(best[:], L[:], AX.X, ALU.add))
                    own(v.reciprocal(best[:], best[:]))
                    own(v.tensor_tensor(L[:], L[:], each(best), ALU.mult))
                    pick_two(v, own, rank, L[:], (key, best), hots, tops, E)
                    own(v.tensor_tensor(hots[0][:], hots[0][:], hots[1][:], ALU.add))
                    v.tensor_tensor(gates[:], hots[0][:], L[:], ALU.mult).then_inc(gated, 1)
                else:
                    own(v.tensor_copy(L[:], scores))
                    pick_two(v, own, rank, L[:], (key, best), hots, tops, E)
                    v.tensor_tensor(e2[:], tops[1][:], tops[0][:], ALU.subtract).then_inc(differ, 1)
                    v.wait_ge(exped, 1)
                    own(v.tensor_scalar(best[:], e2[:], 1.0, None, ALU.add))
                    own(v.reciprocal(tops[0][:], best[:]))
                    own(v.tensor_tensor(tops[1][:], e2[:], tops[0][:], ALU.mult))
                    own(v.tensor_tensor(hots[0][:], hots[0][:], each(tops[0]), ALU.mult))
                    own(v.tensor_tensor(hots[1][:], hots[1][:], each(tops[1]), ALU.mult))
                    v.tensor_tensor(gates[:], hots[0][:], hots[1][:], ALU.add).then_inc(gated, 1)
                v.wait_ge(gated, 1)

                def finish(t):
                    for h in range(H):
                        u = t * H + h
                        v.wait_ge(added, u + 1)
                        own(v.tensor_tensor(Y[:, t, :], Y[:, t, :], R[:, u, :], ALU.add))
                    if routed:
                        v.wait_ge(extra, t + 1)
                        own(v.scalar_tensor_tensor(out=Y[:, t, :], in0=core.ps[:, 6, 0:D], scalar=1.0 / MOE1_S, in1=Y[:, t, :], op0=ALU.mult, op1=ALU.add))
                        v.tensor_tensor(Y[:, t, :], core.ps[:, 6, D:2 * D], Y[:, t, :], ALU.add).then_inc(extra_read, 1)
                        v.wait_ge(extra_read, t + 1)
                    g, last = divmod(t, GROUP)
                    if last == GROUP - 1:
                        norm_stats(v, ve_done, own, Y, stats, mv, g)
                    elif last == 2 and g > 0:
                        norm_apply(v, pool_done, own, Y, core.X, mv, rstd, g - 1)

                if routed:
                    own(v.tensor_scalar(Y[:], core.X[:], 2.0, None, ALU.mult))
                for u in range(UNITS):
                    t, h = divmod(u, H)
                    v.wait_ge(made, u + 1)
                    for k in range(4):
                        e = h * 8 + k
                        into = core.X[:, t, :] if (k == 0 and h == 0 and not routed) else Y[:, t, :]
                        m = v.scalar_tensor_tensor(out=Y[:, t, :], in0=core.ps[:, 2 * (u % 3), k * D:(k + 1) * D], scalar=gates[:, t, e:e + 1], in1=into, op0=ALU.mult, op1=ALU.add)
                        if k < 3:
                            own(m)
                    m.then_inc(weighed_v, 1)
                    v.wait_ge(weighed_v, u + 1)
                    if h == H - 1 and t >= 2:
                        finish(t - 2)
                finish(TILES - 2)
                finish(TILES - 1)
                norm_apply(v, pool_done, own, Y, core.X, mv, rstd, 3)


def experts0(core, M):
    d = core.dram
    with Scope(core, "ex0") as s:
        w_in = s.sb("w_in", [P, MOE0_E, 4, D])
        w_out = s.sb("w_out", [P, MOE0_E, 4, D])
        loaded = [s.sem(f"loaded{e}") for e in range(4)]
        made, kept = s.sem("made"), s.sem("kept")
        with s.block() as block:
            @block.sync
            def _(sp):
                for g in range(4):
                    es = slice(2 * g, 2 * g + 2)
                    sp.dma_start(w_in[:, es].rearrange("p e c i -> p (e c) i"), d["L0_ffn_w_in"][es].rearrange("e (c p) i -> p (e c) i", p=P)).then_inc(loaded[g], 16)
                    sp.dma_start(w_out[:, es].rearrange("p e c i -> p (e c) i"), d["moe0_w_outT"][es].rearrange("e (c p) o -> p (e c) o", p=P)).then_inc(loaded[g], 16)

            @block.tensor
            def _(pe):
                for e in range(MOE0_E):
                    pe.wait_ge(loaded[e // 2], 32)
                    for c in range(4):
                        m = pe.matmul(core.ps[:, e // 4, (e % 4) * D:(e % 4 + 1) * D], w_in[:, e, c, :], w_out[:, e, c, :], start=(c == 0), stop=(c == 3))
                    if e % 4 == 3:
                        m.then_inc(made, 1)

            @block.scalar
            def _(a):
                for g in range(2):
                    a.wait_ge(made, g + 1)
                    a.activation(M[:, g * BANK:(g + 1) * BANK], core.ps[:, g, :], ACT.Copy).then_inc(kept, 1)


class Split:

    def __init__(self, s, chunks, batches=BATCH):
        self.src = s.sb("split_src", [P, 2, chunks, SEQ])
        self.parts = s.sb("split_parts", [P, 2, PARTS, chunks, SEQ], BF16)
        self.hi, self.rest, self.mid, self.low = (s.sem(f"split_{n}") for n in ("hi", "rest", "mid", "low"))
        self.written = [s.sem(f"split_written{b}") for b in range(batches)]

    def may_fill(self, eng, b):
        if b >= 2:
            eng.wait_ge(self.low, b - 1)

    def scalar(self, a, b):
        if b >= 2:
            a.wait_ge(self.written[b - 2], 16)
        a.activation(self.parts[:, b % 2, 0], self.src[:, b % 2], ACT.Copy).then_inc(self.hi, 1)
        a.wait_ge(self.rest, b + 1)
        a.activation(self.parts[:, b % 2, 1], self.src[:, b % 2], ACT.Copy).then_inc(self.mid, 1)

    def vector(self, v, b):
        v.wait_ge(self.hi, b + 1)
        v.tensor_tensor(self.src[:, b % 2], self.src[:, b % 2], self.parts[:, b % 2, 0], ALU.subtract).then_inc(self.rest, 1)
        v.wait_ge(self.rest, b + 1)
        v.wait_ge(self.mid, b + 1)
        v.tensor_tensor(self.parts[:, b % 2, 2], self.src[:, b % 2], self.parts[:, b % 2, 1], ALU.subtract).then_inc(self.low, 1)

    def store(self, sp, b, dst):
        sp.wait_ge(self.low, b + 1)
        sp.dma_start(dst.rearrange("j (c p) t -> p (j c) t", p=P), self.parts[:, b % 2].rearrange("p j c t -> p (j c) t")).then_inc(self.written[b], 16)

    def stored(self, sp):
        for w in self.written:
            sp.wait_ge(w, 16)


L1_SCALE = float(L1_DH) ** -0.5


def l1_project(core, V, RV, scr, rscr):
    d = core.dram
    JOBS = BATCH + 1
    with Scope(core, "l1p") as s:
        w = s.sb("w", [P, 5, D])
        cols = s.sb("cols", [P, 3])
        rows = s.sb("rows", [P, 2, D])
        pastT = s.sb("pastT", [P, PAST_SETS * PAST])
        bq = s.sb("bq", [P, 1])
        sp_ = Split(s, 2, JOBS)
        loaded, turned, kept, scaled = s.sem("loaded"), s.sem("turned"), s.sem("kept"), s.sem("scaled")
        made, filled, vals, chain_s = s.sem("made"), s.sem("filled"), s.sem("values"), s.sem("ve_chain")
        with s.block() as block:
            @block.sync
            def _(sp):
                sp.dma_start(w[:], d["l1_w"].rearrange("k p n -> p k n")).then_inc(loaded, 16)
                sp.dma_start(cols[:], d["l1_cols"]).then_inc(loaded, 16)
                sp.dma_start(rows[:], d["l1_rows"].rearrange("(a c) n -> a c n", a=1).broadcast_to([P, 2, D])).then_inc(loaded, 16)
                sp.dma_start(pastT[:], d["pastT"]).then_inc(loaded, 16)
                for b in range(JOBS):
                    sp_.store(sp, b, scr[b] if b < BATCH else rscr[0])
                sp_.stored(sp)

            @block.tensor
            def _(pe):
                turn_tokens(pe, core, turned, core.X)
                pe.wait_ge(loaded, 64)
                for b in range(JOBS):
                    if b < BATCH:
                        pe.wait_ge(kept, b + 1)
                        x, wk, wv, which = core.XT[:, b * SEQ:(b + 1) * SEQ], w[:, 1], w[:, 2], (0, 1)
                    else:
                        x, wk, wv, which = pastT[:], w[:, 3], w[:, 4], (3,)
                    if b >= 1:
                        pe.wait_ge(filled, 2 * b)
                        pe.wait_ge(vals, b)
                    for k in which:
                        pe.matmul(core.ps[:, 4 + min(k, 1), :], w[:, k, :], x, start=True, stop=True).then_inc(made, 1)
                    for q in range(QT):
                        m = pe.matmul(core.ps[:, 6, q * P:(q + 1) * P], x[:, q * P:(q + 1) * P], wv, start=True, stop=True)
                    m.then_inc(made, 1)

            @block.scalar
            def _(a):
                a.wait_ge(loaded, 64)
                a.activation(bq[:], cols[:, 0:1], ACT.Copy, scale=L1_SCALE).then_inc(scaled, 1)
                keep_turned(a, core, turned, kept)
                a.wait_ge(scaled, 1)
                for b in range(BATCH):
                    sp_.may_fill(a, b)
                    a.wait_ge(made, 3 * b + 1)
                    a.activation(sp_.src[:, b % 2, 0], core.ps[:, 4, :], ACT.Identity, scale=L1_SCALE, bias=bq[:]).then_inc(filled, 1)
                    a.wait_ge(made, 3 * b + 2)
                    a.activation(sp_.src[:, b % 2, 1], core.ps[:, 5, :], ACT.Identity, bias=cols[:, 1:2]).then_inc(filled, 1)
                    a.wait_ge(filled, 2 * b + 2)
                    sp_.scalar(a, b)
                b = BATCH
                sp_.may_fill(a, b)
                a.wait_ge(made, 3 * b + 1)
                for c in range(2):
                    a.activation(sp_.src[:, b % 2, c], core.ps[:, 5, :], ACT.Identity, bias=cols[:, 2:3]).then_inc(filled, 1)
                a.wait_ge(filled, 2 * b + 2)
                sp_.scalar(a, b)

            @block.vector
            def _(v):
                own = Chain(v, chain_s)
                own.mark(v.memset(V[:, :, :, L1_DH:], 1.0))
                own.mark(v.memset(RV[:, :, :, L1_DH:], 1.0))
                v.wait_ge(loaded, 64)
                for b in range(JOBS):
                    v.wait_ge(made, 3 * b + 3 if b < BATCH else 3 * b + 2)
                    out = V[:, b * QT:(b + 1) * QT] if b < BATCH else RV[:]
                    bias = rows[:, 0 if b < BATCH else 1, :].rearrange("p (h e) -> p h e", h=HEADS)
                    for q in range(QT):
                        m = v.tensor_tensor(out[:, q, :, 0:L1_DH], core.ps[:, 6, q * P:(q + 1) * P].rearrange("p (h e) -> p h e", h=HEADS), bias, ALU.add)
                    m.then_inc(vals, 1)
                    sp_.vector(v, b)


def l1_between(core, O, OT, rscr):
    d = core.dram
    with Scope(core, "l1m") as s:
        w = s.sb("w", [P, 2, D])
        cols = s.sb("cols", [P, 2])
        bq = s.sb("bq", [P, 1])
        cT = s.sb("cT", [P, 2, SEQ])
        sp_ = Split(s, 1)
        loaded, scaled, turned, kept = s.sem("loaded"), s.sem("scaled"), s.sem("turned"), s.sem("kept")
        made, outed, made2, filled = s.sem("made"), s.sem("outed"), s.sem("queried"), s.sem("filled")
        with s.block() as block:
            @block.sync
            def _(sp):
                sp.dma_start(w[:], d["l1_w2"].rearrange("k p n -> p k n")).then_inc(loaded, 16)
                sp.dma_start(cols[:], d["l1_cols2"]).then_inc(loaded, 16)
                for b in range(BATCH):
                    sp_.store(sp, b, rscr[b][:, 0:P])
                sp_.stored(sp)

            @block.tensor
            def _(pe):
                pe.wait_ge(loaded, 32)

                def turn(b):
                    if b >= 2:
                        pe.wait_ge(kept, b - 1)
                    for q in range(QT):
                        m = pe.transpose(core.ps[:, b % 2, q * P:(q + 1) * P], O[:, b * QT + q, :], core.ident[:])
                    m.then_inc(turned, 1)

                turn(0)
                for b in range(BATCH):
                    if b < BATCH - 1:
                        turn(b + 1)
                    pe.wait_ge(kept, b + 1)
                    if b >= 2:
                        pe.wait_ge(outed, b - 1)
                    pe.matmul(core.ps[:, 2 + b % 2, :], w[:, 0, :], cT[:, b % 2, :], start=True, stop=True).then_inc(made, 1)
                    pe.wait_ge(outed, b + 1)
                    if b >= 2:
                        pe.wait_ge(filled, b - 1)
                    pe.matmul(core.ps[:, 4 + b % 2, :], w[:, 1, :], OT[:, b * SEQ:(b + 1) * SEQ], start=True, stop=True).then_inc(made2, 1)

            @block.scalar
            def _(a):
                a.wait_ge(loaded, 32)
                a.activation(bq[:], cols[:, 1:2], ACT.Copy, scale=L1_SCALE).then_inc(scaled, 1)
                a.wait_ge(scaled, 1)
                for b in range(BATCH):
                    a.wait_ge(turned, b + 1)
                    if b >= 2:
                        a.wait_ge(made, b - 1)
                    a.activation(cT[:, b % 2, :], core.ps[:, b % 2, :], ACT.Copy).then_inc(kept, 1)
                    a.wait_ge(made, b + 1)
                    a.activation(OT[:, b * SEQ:(b + 1) * SEQ], core.ps[:, 2 + b % 2, :], ACT.Identity, bias=cols[:, 0:1]).then_inc(outed, 1)
                    a.wait_ge(made2, b + 1)
                    sp_.may_fill(a, b)
                    a.activation(sp_.src[:, b % 2, 0], core.ps[:, 4 + b % 2, :], ACT.Identity, scale=L1_SCALE, bias=bq[:]).then_inc(filled, 1)
                    a.wait_ge(filled, b + 1)
                    sp_.scalar(a, b)

            @block.vector
            def _(v):
                for b in range(BATCH):
                    sp_.vector(v, b)


def l1_finish(core, O, OT):
    d = core.dram
    with Scope(core, "l1f") as s:
        w = s.sb("w", [P, 2, D])
        bg = s.sb("bg", [P, 1])
        rT = s.sb("rT", [P, 2, SEQ])
        gate = s.sb("gate", [P, 2, SEQ])
        diff = s.sb("diff", [P, 2, SEQ])
        Y = s.sb("Y", [P, TILES, D])
        stats = s.sb("stats", [P, TILES, 6])
        mv = s.sb("mv", [P, TILES, 2])
        rstd = s.sb("rstd", [P, TILES])
        loaded, turned, kept, made, gated = s.sem("loaded"), s.sem("turned"), s.sem("kept"), s.sem("made"), s.sem("gated")
        mixed, back, chain_s, summed = s.sem("mixed"), s.sem("back"), s.sem("ve_chain"), s.sem("summed")
        ve_done, pool_done = s.sem("ve_done"), s.sem("pool_done")
        with s.block() as block:
            @block.sync
            def _(sp):
                sp.dma_start(w[:], d["L1_attn_Wg"].rearrange("(k p) n -> p k n", p=P)).then_inc(loaded, 16)
                sp.dma_start(bg[:], d["L1_attn_bg"].rearrange("(p a) -> p a", a=1)).then_inc(loaded, 16)

            @block.tensor
            def _(pe):
                pe.wait_ge(loaded, 32)

                def turn(b):
                    if b >= 2:
                        pe.wait_ge(kept, b - 1)
                    for q in range(QT):
                        m = pe.transpose(core.ps[:, b % 2, q * P:(q + 1) * P], O[:, b * QT + q, :], core.ident[:])
                    m.then_inc(turned, 1)

                turn(0)
                for b in range(BATCH):
                    if b < BATCH - 1:
                        turn(b + 1)
                    pe.wait_ge(kept, b + 1)
                    if b >= 2:
                        pe.wait_ge(gated, b - 1)
                    pe.matmul(core.ps[:, 2 + b % 2, :], w[:, 0, :], OT[:, b * SEQ:(b + 1) * SEQ], start=True, stop=False)
                    pe.matmul(core.ps[:, 2 + b % 2, :], w[:, 1, :], rT[:, b % 2, :], start=False, stop=True).then_inc(made, 1)
                    pe.wait_ge(mixed, b + 1)
                    if b >= 2:
                        pe.wait_ge(summed, b - 1)
                    for q in range(QT):
                        m = pe.transpose(core.ps[:, 4 + b % 2, q * P:(q + 1) * P], diff[:, b % 2, q * P:(q + 1) * P], core.ident[:])
                    m.then_inc(back, 1)

            @block.scalar
            def _(a):
                a.wait_ge(loaded, 32)
                for b in range(BATCH):
                    a.wait_ge(turned, b + 1)
                    if b >= 2:
                        a.wait_ge(mixed, b - 1)
                    a.activation(rT[:, b % 2, :], core.ps[:, b % 2, :], ACT.Copy, scale=1.0 / PAST_SETS).then_inc(kept, 1)
                    a.wait_ge(made, b + 1)
                    a.activation(gate[:, b % 2, :], core.ps[:, 2 + b % 2, :], ACT.Sigmoid, bias=bg[:]).then_inc(gated, 1)

            @block.gpsimd
            def _(g):
                rstd_tokens(g, core, pool_done, ve_done, mv, rstd)

            @block.vector
            def _(v):
                own = Chain(v, chain_s)
                for b in range(BATCH):
                    out = OT[:, b * SEQ:(b + 1) * SEQ]
                    v.wait_ge(kept, b + 1)
                    if b >= 2:
                        v.wait_ge(back, b - 1)
                    own(v.tensor_tensor(diff[:, b % 2], rT[:, b % 2], out, ALU.subtract))
                    v.wait_ge(gated, b + 1)
                    own(v.tensor_tensor(diff[:, b % 2], diff[:, b % 2], gate[:, b % 2], ALU.mult))
                    v.tensor_tensor(diff[:, b % 2], diff[:, b % 2], out, ALU.add).then_inc(mixed, 1)
                    v.wait_ge(back, b + 1)
                    v.tensor_tensor(Y[:, b * QT:(b + 1) * QT], core.ps[:, 4 + b % 2, :].rearrange("p (q d) -> p q d", q=QT), core.X[:, b * QT:(b + 1) * QT], ALU.add).then_inc(summed, 1)
                    v.wait_ge(summed, b + 1)
                    norm_stats(v, ve_done, own, Y, stats, mv, b)
                    if b >= 1:
                        norm_apply(v, pool_done, own, Y, core.X, mv, rstd, b - 1)
                norm_apply(v, pool_done, own, Y, core.X, mv, rstd, BATCH - 1)


STEPS = 64
COLS = 2 * BATCH


def l2_ssm(core, cat, sign):
    d = core.dram
    with Scope(core, "ssm") as s:
        cols = s.sb("cols", [P, 5])
        bw = s.sb("bw", [P, 2, P])
        A = s.sb("A", [P, 1])
        apow = s.sb("apow", [P, SEQ])
        inv = s.sb("inv", [P, SEQ])
        ones = s.sb("ones", [P, SEQ])
        zeros = s.sb("zeros", [P, SEQ])
        xn = s.sb("xn", [P, TILES, D])
        u = s.sb("u", [P, 2, SEQ])
        cum = s.sb("cum", [P, 2, SEQ])
        states = s.sb("states", [P, 2, SEQ])
        stats = s.sb("stats", [P, TILES, 6])
        mv = s.sb("mv", [P, TILES, 2])
        rstd = s.sb("rstd", [P, TILES])
        loaded, decay, turned, kept, made = s.sem("loaded"), s.sem("decay"), s.sem("turned"), s.sem("kept"), s.sem("made")
        scaled, stated, projected, out_kept = s.sem("scaled"), s.sem("stated"), s.sem("projected"), s.sem("out_kept")
        ve_done, pool_done, chain_s = s.sem("ve_done"), s.sem("pool_done"), s.sem("ve_chain")
        with s.block() as block:
            @block.sync
            def _(sp):
                sp.dma_start(cols[:], d["ssm_cols"]).then_inc(loaded, 16)
                sp.dma_start(bw[:], d["ssm_w"].rearrange("k p n -> p k n")).then_inc(loaded, 16)
                sp.dma_start(sign[:], d["sign"]).then_inc(loaded, 16)

            @block.tensor
            def _(pe):
                for t in range(TILES):
                    pe.wait_ge(ve_done, t + 5)
                    m = pe.transpose(core.ps[:, t // 4, (t % 4) * P:(t % 4 + 1) * P], xn[:, t, :], core.ident[:])
                    if t % 4 == 3:
                        m.then_inc(turned, 1)
                def project(b):
                    pe.wait_ge(stated, b + 1)
                    if b >= 2:
                        pe.wait_ge(out_kept, b - 1)
                    pe.matmul(core.ps[:, 6 + b % 2, :], bw[:, 1, :], states[:, b % 2, :], start=True, stop=True).then_inc(projected, 1)

                pe.wait_ge(loaded, 48)
                for b in range(BATCH):
                    pe.wait_ge(kept, b + 1)
                    if b >= 2:
                        pe.wait_ge(scaled, b - 1)
                    pe.matmul(core.ps[:, 4 + b % 2, :], bw[:, 0, :], core.XT[:, b * SEQ:(b + 1) * SEQ], start=True, stop=True).then_inc(made, 1)
                    if b >= 1:
                        project(b - 1)
                project(BATCH - 1)

            @block.scalar
            def _(a):
                a.wait_ge(loaded, 48)
                a.activation(A[:], cols[:, 4:5], ACT.Sigmoid).then_inc(decay, 1)
                for g in range(4):
                    a.wait_ge(turned, g + 1)
                    a.activation(core.XT[:, g * BANK:(g + 1) * BANK], core.ps[:, g, :], ACT.Identity, scale=cols[:, 0:1], bias=cols[:, 1:2]).then_inc(kept, 1)
                for b in range(BATCH):
                    a.wait_ge(projected, b + 1)
                    a.activation(cat[:, b, 0:SEQ], core.ps[:, 6 + b % 2, :], ACT.Identity, bias=cols[:, 3:4]).then_inc(out_kept, 1)

            @block.gpsimd
            def _(g):
                rstd_tokens(g, core, pool_done, ve_done, mv, rstd)

            @block.vector
            def _(v):
                own = Chain(v, chain_s)
                norm_tokens(v, pool_done, ve_done, own, core.X, xn, stats, mv, rstd)
                own.mark(v.memset(ones[:], 1.0))
                own.mark(v.memset(zeros[:], 0.0))
                own.mark(v.memset(cat[:, :, SEQ:], 0.0))
                own(v.memset(apow[:, 0:1], 1.0))
                v.wait_ge(decay, 1)
                own(v.tensor_tensor_scan(apow[:, 1:], A[:].broadcast_to([P, SEQ - 1]), zeros[:, 1:], 1.0, ALU.mult, ALU.add))
                own(v.tensor_scalar(inv[:], apow[:], 1e-8, None, ALU.max))
                own(v.reciprocal(inv[:], inv[:]))
                for b in range(BATCH):
                    v.wait_ge(made, b + 1)
                    v.scalar_tensor_tensor(out=u[:, b % 2], in0=core.ps[:, 4 + b % 2, :], scalar=cols[:, 2:3], in1=inv[:], op0=ALU.add, op1=ALU.mult).then_inc(scaled, 1)
                    v.wait_ge(scaled, b + 1)
                    own(v.tensor_tensor_scan(cum[:, b % 2], ones[:], u[:, b % 2], 0.0, ALU.mult, ALU.add))
                    if b >= 2:
                        v.wait_ge(projected, b - 1)
                    v.tensor_tensor(states[:, b % 2], cum[:, b % 2], apow[:], ALU.mult).then_inc(stated, 1)


def l2_scan(core, cat, history, rows_sign):
    d = core.dram
    RING = 2 * STEPS
    with Scope(core, "rnn") as s:
        wx = s.sb("wx", [P, 3, P])
        wh = s.sb("wh", [P, 3, P])
        bias = s.sb("bias", [1, 3, P])
        ones = s.sb("ones", [1, STEPS])
        half = s.sb("half", [P, 1])
        ring = s.sb("ring", [P, RING, BATCH])
        act = s.sb("act", [P, 2, COLS])
        warm = s.sb("warm", [P, 1])
        loaded, weights, chain_s = s.sem("loaded"), s.sem("weights"), s.sem("ve_chain")
        gate_summed = s.sem("gate_summed")
        summed, bent, stepped, copied, primed = s.sem("summed"), s.sem("bent"), s.sem("stepped"), s.sem("copied"), s.sem("primed")
        with s.block() as block:
            @block.sync
            def _(sp):
                sp.dma_start(wx[:], d["rnn_wx"].rearrange("k p n -> p k n")).then_inc(loaded, 16)
                sp.dma_start(wh[:], d["rnn_wh"].rearrange("k p n -> p k n")).then_inc(loaded, 16)
                sp.dma_start(bias[:], d["rnn_b"].rearrange("(a k) n -> a k n", a=1)).then_inc(loaded, 16)

            @block.tensor
            def _(pe):
                pe.wait_ge(weights, 1)
                pe.wait_ge(copied, 2)

                def inputs(bank, chunk, piece, kind):
                    n = STEPS // 4
                    k, M = kind // 2, P if kind < 2 else RNN_H
                    out = core.ps[0:M, bank + 2 * k, piece * n * BATCH:(piece + 1) * n * BATCH].rearrange("p (t c) -> p t c", c=BATCH)
                    if kind % 2 == 0:
                        src = cat[:, 0:BATCH, bass.ds(chunk * STEPS + piece * n, n)].rearrange("p b t -> p t b")
                        pe.matmul(out, wx[:, k, 0:M], src, start=(piece == 0), stop=False, skip_group_check=True)
                    else:
                        pe.matmul(out, bias[:, k, 0:M], ones[:, 0:n].unsqueeze(2).broadcast_to([1, n, BATCH]), start=False, stop=False, skip_group_check=True)

                for piece in range(4):
                    for kind in range(4):
                        inputs(0, 0, piece, kind)
                with pe.Fori(0, SEQ // RING) as i:
                    for k in range(RING):
                        bank, t = divmod(k, STEPS)
                        pe.wait_ge(stepped, RING * i + (k + 1))
                        prev = ring[:, (k - 1) % RING, :]
                        cols = slice(t * BATCH, (t + 1) * BATCH)
                        pe.matmul(core.ps[0:RNN_H, 2 + bank, cols], wh[:, 1, 0:RNN_H], prev, start=False, stop=True, skip_group_check=True).then_inc(gate_summed, 1)
                        pe.matmul(core.ps[:, bank, cols], wh[:, 0, :], prev, start=False, stop=True, skip_group_check=True).then_inc(summed, 1)
                        if 4 <= t < 20:
                            inputs(1 - bank, 2 * i + (bank + 1), (t - 4) // 4, (t - 4) % 4)

            @block.scalar
            def _(a):
                a.wait_ge(weights, 1)
                a.activation(warm[:], half[:], ACT.Tanh).then_inc(primed, 1)
                with a.Fori(0, SEQ // RING) as i:
                    for k in range(RING):
                        bank, t = divmod(k, STEPS)
                        cols = slice(t * BATCH, (t + 1) * BATCH)
                        a.wait_ge(gate_summed, RING * i + (k + 1))
                        for hf in range(2):
                            a.activation(act[hf * RNN_H:(hf + 1) * RNN_H, k % 2, BATCH:], core.ps[0:RNN_H, 2 + bank, cols], ACT.Tanh).then_inc(bent, 1)
                        a.wait_ge(summed, RING * i + (k + 1))
                        a.activation(act[:, k % 2, 0:BATCH], core.ps[:, bank, cols], ACT.Tanh).then_inc(bent, 1)

            @block.gpsimd
            def _(g):
                g.memset(ones[:], 1.0).then_inc(copied, 2)
                with g.Fori(0, SEQ // RING) as i:
                    for hf in range(2):
                        g.wait_ge(stepped, RING * i + (hf + 1) * STEPS + 1)
                        g.tensor_copy(history[:, bass.ds((2 * i + hf) * (STEPS * BATCH), STEPS * BATCH)], ring[:, hf * STEPS:(hf + 1) * STEPS, :].rearrange("p t b -> p (t b)")).then_inc(copied, 1)

            @block.vector
            def _(v):
                own = Chain(v, chain_s)
                v.wait_ge(loaded, 48)
                own(v.tensor_scalar(half[:], rows_sign[:], 0.5, None, ALU.mult))
                for w in (wx, wh, bias):
                    own(v.tensor_scalar(w[:, 1, :], w[:, 1, :], 0.05, None, ALU.mult))
                    own(v.scalar_tensor_tensor(out=w[:, 1, :], in0=w[:, 2, :], scalar=0.5, in1=w[:, 1, :], op0=ALU.mult, op1=ALU.add))
                v.tensor_scalar(wh[:, 0:2, :], wh[:, 0:2, :], half[:], None, ALU.mult).then_inc(weights, 1)
                v.memset(ring[:, RING - 1, :], 0.0).then_inc(stepped, 1)
                with v.Fori(0, SEQ // RING) as i:
                    for k in range(RING):
                        if k % STEPS == 0:
                            v.wait_ge(copied, 2 * i + (k // STEPS + 1))
                        v.wait_ge(bent, 3 * RING * i + 3 * (k + 1))
                        v.scalar_tensor_tensor(out=ring[:, k, :], in0=act[:, k % 2, BATCH:COLS], scalar=rows_sign[:], in1=act[:, k % 2, 0:BATCH], op0=ALU.add, op1=ALU.mult).then_inc(stepped, 1)


def l2_finish(core, history, rows_sign):
    d = core.dram
    with Scope(core, "l2f") as s:
        w = s.sb("w", [P, D])
        half = s.sb("half", [P, 1])
        ob = s.sb("ob", [P, D])
        Y = s.sb("Y", [P, TILES, D])
        stats = s.sb("stats", [P, TILES, 6])
        mv = s.sb("mv", [P, TILES, 2])
        rstd = s.sb("rstd", [P, TILES])
        loaded, weights, made, chain_s = s.sem("loaded"), s.sem("weights"), s.sem("made"), s.sem("ve_chain")
        ve_done, pool_done = s.sem("ve_done"), s.sem("pool_done")
        with s.block() as block:
            @block.sync
            def _(sp):
                sp.dma_start(w[:], d["rnn_out"]).then_inc(loaded, 16)
                sp.dma_start(ob[:], d["L2_attn_out_b"].rearrange("(a n) -> a n", a=1).broadcast_to([P, D])).then_inc(loaded, 16)

            @block.tensor
            def _(pe):
                pe.wait_ge(weights, 1)
                for t in range(TILES):
                    b, q = divmod(t, QT)
                    src = history[:].rearrange("p (t b) -> p b t", b=BATCH)[:, b, q * P:(q + 1) * P]
                    m = pe.matmul(core.ps[:, t // 4, (t % 4) * D:(t % 4 + 1) * D], src, w[:], start=True, stop=True)
                    if t % 4 == 3:
                        m.then_inc(made, 1)

            @block.gpsimd
            def _(g):
                rstd_tokens(g, core, pool_done, ve_done, mv, rstd)

            @block.vector
            def _(v):
                own = Chain(v, chain_s)
                v.wait_ge(loaded, 32)
                own(v.tensor_scalar(half[:], rows_sign[:], 0.5, None, ALU.mult))
                v.tensor_scalar(w[:], w[:], half[:], None, ALU.mult).then_inc(weights, 1)
                own(v.scalar_tensor_tensor(out=Y[:], in0=core.X[:], scalar=2.0, in1=ob[:].unsqueeze(1).broadcast_to([P, TILES, D]), op0=ALU.mult, op1=ALU.add))
                for g in range(4):
                    v.wait_ge(made, g + 1)
                    m = v.tensor_tensor(Y[:, 4 * g:4 * g + 4], core.ps[:, g, :].rearrange("p (q d) -> p q d", q=4), Y[:, 4 * g:4 * g + 4], ALU.add)
                    own(m)
                    norm_stats(v, ve_done, own, Y, stats, mv, g)
                for g in range(4):
                    norm_apply(v, pool_done, own, Y, core.X, mv, rstd, g)


def bit_mlp(core):
    d = core.dram
    C = BIT_H // P
    with Scope(core, "bit") as s:
        wf = s.sb("wf", [P, C, P])
        wp = s.sb("wp", [P, BIT_H])
        mag = s.sb("mag", [P, BIT_H])
        neg = s.sb("neg", [P, BIT_H])
        scale = s.sb("scale", [P, C + 1])
        up = s.sb("up", [P, C + 1])
        down = s.sb("down", [P, C + 1])
        fastT = s.sb("fastT", [BIT_R, BIT_R])
        vw = s.sb("vw", [BIT_R, P])
        uT = s.sb("uT", [BIT_R, BIT_H])
        fv = s.sb("fv", [BIT_R, P])
        gate = s.sb("gate", [P, 1])
        w1 = s.sb("w1", [P, BIT_H])
        w2 = s.sb("w2", [P, C, P])
        r0 = s.sb("r0", [P, 2, SEQ])
        r = s.sb("r", [P, 2, C, SEQ])
        Y = s.sb("Y", [P, TILES, D])
        stats = s.sb("stats", [P, TILES, 6])
        mv = s.sb("mv", [P, TILES, 2])
        rstd = s.sb("rstd", [P, TILES])
        loaded, turned, kept, ternary = s.sem("loaded"), s.sem("turned"), s.sem("kept"), s.sem("ternary")
        turned_w, low1, low1_kept, low2, w_kept, w_ready = (s.sem(n) for n in ("turned_w", "low1", "low1_kept", "low2", "w_kept", "w_ready"))
        hidden, relu, squared, out, summed = (s.sem(n) for n in ("hidden", "relu", "squared", "out", "summed"))
        ve_done, pool_done, chain_s = s.sem("ve_done"), s.sem("pool_done"), s.sem("ve_chain")
        with s.block() as block:
            @block.sync
            def _(sp):
                sp.dma_start(wf[:], d["L2_ffn_w_fc"].rearrange("(c p) n -> p c n", p=P)).then_inc(loaded, 16)
                sp.dma_start(wp[:], d["L2_ffn_w_proj"]).then_inc(loaded, 16)
                sp.dma_start(fastT[:], d["bit_fastT"]).then_inc(loaded, 16)
                sp.dma_start(vw[:], d["L2_ffn_v"]).then_inc(loaded, 16)
                sp.dma_start(uT[:], d["bit_uT"]).then_inc(loaded, 16)
                sp.dma_start(gate[:], d["bit_gate"].broadcast_to([P, 1])).then_inc(loaded, 16)

            @block.tensor
            def _(pe):
                turn_tokens(pe, core, turned, core.X)
                pe.wait_ge(loaded, 96)
                pe.matmul(core.ps[0:BIT_R, 4, 0:P], fastT[:], vw[:], start=True, stop=True).then_inc(low1, 1)
                pe.wait_ge(ternary, 1)
                for c in range(C):
                    m = pe.transpose(core.ps[:, 5, c * P:(c + 1) * P], wf[:, c, :], core.ident[:])
                m.then_inc(turned_w, 1)
                for c in range(C):
                    m = pe.transpose(core.ps[:, 6, c * P:(c + 1) * P], wp[:, c * P:(c + 1) * P], core.ident[:])
                m.then_inc(turned_w, 1)
                pe.wait_ge(low1_kept, 1)
                pe.matmul(core.ps[:, 7, :], fv[:], uT[:], start=True, stop=True).then_inc(low2, 1)
                pe.wait_ge(w_ready, 1)

                def project(b):
                    if b >= 2:
                        pe.wait_ge(summed, b - 1)
                    pe.wait_ge(squared, C * b + C)
                    for q in range(QT):
                        for c in range(C):
                            m = pe.matmul(core.ps[:, 6 + b % 2, q * P:(q + 1) * P], r[:, b % 2, c, q * P:(q + 1) * P], w2[:, c, :], start=(c == 0), stop=(c == C - 1))
                    m.then_inc(out, 1)

                for b in range(BATCH):
                    pe.wait_ge(kept, b + 1)
                    for c in range(C):
                        n = b * C + c
                        if n >= 6:
                            pe.wait_ge(squared, n - 5)
                        else:
                            pe.wait_ge(kept, 4)
                        pe.matmul(core.ps[:, n % 6, :], w1[:, c * P:(c + 1) * P], core.XT[:, b * SEQ:(b + 1) * SEQ], start=True, stop=True).then_inc(hidden, 1)
                    if b >= 1:
                        project(b - 1)
                project(BATCH - 1)

            @block.scalar
            def _(a):
                keep_turned(a, core, turned, kept)
                a.wait_ge(low1, 1)
                a.activation(fv[:], core.ps[0:BIT_R, 4, 0:P], ACT.Copy).then_inc(low1_kept, 1)
                a.wait_ge(turned_w, 1)
                a.activation(w1[:], core.ps[:, 5, :], ACT.Copy).then_inc(w_kept, 1)
                a.wait_ge(turned_w, 2)
                a.activation(w2[:], core.ps[:, 6, :].rearrange("p (c n) -> p c n", c=C), ACT.Copy).then_inc(w_kept, 1)
                for n in range(BATCH * C):
                    a.wait_ge(hidden, n + 1)
                    if n >= 2:
                        a.wait_ge(squared, n - 1)
                    a.activation(r0[:, n % 2], core.ps[:, n % 6, :], ACT.Relu).then_inc(relu, 1)

            @block.gpsimd
            def _(g):
                rstd_tokens(g, core, pool_done, ve_done, mv, rstd)

            @block.vector
            def _(v):
                own = Chain(v, chain_s)
                v.wait_ge(loaded, 96)
                own(v.scalar_tensor_tensor(out=mag[:], in0=wp[:], scalar=-1.0, in1=wp[:], op0=ALU.mult, op1=ALU.max))
                own(v.tensor_reduce(scale[:, C:C + 1], mag[:], AX.X, ALU.add))
                own(v.tensor_scalar(scale[:, C:C + 1], scale[:, C:C + 1], 1.0 / BIT_H, 1e-5, ALU.mult, ALU.max))
                own(v.scalar_tensor_tensor(out=mag[:], in0=wf[:].rearrange("p c n -> p (c n)"), scalar=-1.0, in1=wf[:].rearrange("p c n -> p (c n)"), op0=ALU.mult, op1=ALU.max))
                own(v.tensor_reduce(scale[:, 0:C], mag[:].rearrange("p (c n) -> p c n", c=C), AX.X, ALU.add))
                own(v.tensor_scalar(scale[:, 0:C], scale[:, 0:C], 1.0 / D, 1e-5, ALU.mult, ALU.max))
                own(v.tensor_scalar(up[:], scale[:], 0.5, None, ALU.mult))
                own(v.tensor_scalar(down[:], scale[:], -0.5, None, ALU.mult))
                for c in range(C):
                    own(v.tensor_scalar(neg[:, c * P:(c + 1) * P], wf[:, c, :], down[:, c:c + 1], scale[:, c:c + 1], ALU.is_lt, ALU.mult))
                    own(v.tensor_scalar(wf[:, c, :], wf[:, c, :], up[:, c:c + 1], scale[:, c:c + 1], ALU.is_gt, ALU.mult))
                own(v.tensor_tensor(wf[:].rearrange("p c n -> p (c n)"), wf[:].rearrange("p c n -> p (c n)"), neg[:], ALU.subtract))
                own(v.tensor_scalar(neg[:], wp[:], down[:, C:C + 1], scale[:, C:C + 1], ALU.is_lt, ALU.mult))
                own(v.tensor_scalar(wp[:], wp[:], up[:, C:C + 1], scale[:, C:C + 1], ALU.is_gt, ALU.mult))
                v.tensor_tensor(wp[:], wp[:], neg[:], ALU.subtract).then_inc(ternary, 1)
                v.wait_ge(low2, 1)
                v.wait_ge(w_kept, 2)
                v.scalar_tensor_tensor(out=w1[:], in0=core.ps[:, 7, :], scalar=gate[:], in1=w1[:], op0=ALU.mult, op1=ALU.add).then_inc(w_ready, 1)

                def residual(b):
                    v.wait_ge(out, b + 1)
                    v.tensor_tensor(Y[:, b * QT:(b + 1) * QT], core.ps[:, 6 + b % 2, :].rearrange("p (q d) -> p q d", q=QT), core.X[:, b * QT:(b + 1) * QT], ALU.add).then_inc(summed, 1)
                    v.wait_ge(summed, b + 1)
                    norm_stats(v, ve_done, own, Y, stats, mv, b)
                    if b >= 1:
                        norm_apply(v, pool_done, own, Y, core.X, mv, rstd, b - 1)

                for n in range(BATCH * C):
                    b, c = divmod(n, C)
                    v.wait_ge(relu, n + 1)
                    if c == 0 and b >= 2:
                        v.wait_ge(out, b - 1)
                    v.scalar_tensor_tensor(out=r[:, b % 2, c, :], in0=core.ps[:, n % 6, :], scalar=0.0, in1=r0[:, n % 2], op0=ALU.max, op1=ALU.mult).then_inc(squared, 1)
                    if c == C - 1 and b >= 1:
                        residual(b - 1)
                residual(BATCH - 1)
                norm_apply(v, pool_done, own, Y, core.X, mv, rstd, BATCH - 1)


def rms_tokens(v, pool_done, ve_done, chain, src, stats, mv, ms):
    for g in range(4):
        cols = slice(g * GROUP, (g + 1) * GROUP)
        for t in range(g * GROUP, (g + 1) * GROUP):
            chain.mark(v.bn_stats(stats[:, t, :], src[:, t, :]))
        chain.wait()
        for t in range(g * GROUP, (g + 1) * GROUP):
            chain.mark(v.bn_aggr(mv[:, t, :], stats[:, t, :]))
        chain.wait()
        chain(v.tensor_tensor(ms[:, cols], mv[:, cols, 0], mv[:, cols, 0], ALU.mult))
        v.tensor_tensor(ms[:, cols], ms[:, cols], mv[:, cols, 1], ALU.add).then_inc(ve_done, 1)


def rstd_ms(g, core, pool_done, ve_done, ms, rstd):
    for n in range(4):
        cols = slice(n * GROUP, (n + 1) * GROUP)
        g.wait_ge(ve_done, n + 1)
        g.tensor_scalar(rstd[:, cols], ms[:, cols], EPS, None, ALU.add).then_inc(pool_done, 1)
        g.wait_ge(pool_done, 2 * n + 1)
        g.tensor_tensor(rstd[:, cols], rstd[:, cols], core.half_neg[:, cols], ALU.pow).then_inc(pool_done, 1)


M_ROWS = PARTS * M_HEADS
DA_W = 32 + M_ROWS
RH = 3
CH = 4


def mamba_layer(core, l, H, m):
    d = core.dram
    ms = m
    with Scope(core, "ma") as s:
        w = s.sb("w", [P, M_PROJ])
        stats = s.sb("stats", [P, TILES, 6])
        mv = s.sb("mv", [P, TILES, 2])
        msq = s.sb("msq", [P, TILES])
        rstd = s.sb("rstd", [P, TILES])
        xn = s.sb("xn", [P, TILES, D])
        cv = s.sb("cv", [P, 4, SEQ])
        dt0 = s.sb("dt0", [P, TILES, M_HEADS])
        dt1 = s.sb("dt1", [P, TILES, M_HEADS])
        da = s.sb("da", [P, TILES, DA_W])
        Arow = s.sb("Arow", [P, M_HEADS])
        rounded = s.sb("rounded", [DA_W, 2, TOK], BF16)
        left = s.sb("left", [DA_W, TOK])
        rows_rest, rows_mid = s.sem("rows_rest"), s.sem("rows_mid")
        loaded, loaded_w = s.sem("loaded"), s.sem("loaded_w")
        turned, kept, made, zmade = s.sem("turned"), s.sem("kept"), s.sem("made"), s.sem("zmade")
        tap, conv, silued, zsilued, dts = s.sem("tap"), s.sem("conv"), s.sem("silued"), s.sem("zsilued"), s.sem("dts")
        ve_done, pool_done, chain_s, padded = s.sem("ve_done"), s.sem("pool_done"), s.sem("ve_chain"), s.sem("padded")
        neg_abs, exp_dt, plus_one, lned, da_ready, a_ready = (s.sem(n) for n in ("neg_abs", "exp_dt", "plus_one", "lned", "da_ready", "a_ready"))
        sums, diffs, exps, rows_sum, rows_kept, factors = (s.sem(n) for n in ("sums", "diffs", "exps", "rows_sum", "rows_kept", "factors"))
        with s.block() as block:
            @block.sync
            def _(sp):
                sp.dma_start(ms.cols[:], d["m_cols"][bass.ds(l, 1)].rearrange("a p n -> p (a n)")).then_inc(loaded, 16)
                sp.dma_start(ms.rows[:], d["m_rows"][bass.ds(l, 1)].broadcast_to([P, 3 * M_HEADS])).then_inc(loaded, 16)
                sp.dma_start(w[:], d["L3_attn_W_in"][bass.ds(l, 1)].rearrange("a p n -> p (a n)")).then_inc(loaded_w, 16)
                sp.dma_start(ms.wo[:], d["L3_attn_W_out"][bass.ds(l, 1)].rearrange("a (c p) n -> p (a c) n", p=P)).then_inc(loaded_w, 16)

            @block.tensor
            def _(pe):
                for t in range(TILES):
                    pe.wait_ge(ve_done, t + 5)
                    mm = pe.transpose(core.ps[:, t // 4, (t % 4) * P:(t % 4 + 1) * P], xn[:, t, :], core.ident[:])
                    if t % 4 == 3:
                        mm.then_inc(turned, 1)
                pe.wait_ge(loaded_w, 32)
                for b in range(BATCH):
                    pe.wait_ge(kept, BATCH)
                    for j in range(CH):
                        n = b * CH + j
                        if n >= 4:
                            pe.wait_ge(conv, n - 3)
                        pe.matmul(core.ps[:, 4 + n % 4, :], w[:, M_INNER + j * P:M_INNER + (j + 1) * P], core.XT[:, b * SEQ:(b + 1) * SEQ], start=True, stop=True).then_inc(made, 1)
                    for q in range(QT):
                        t = b * QT + q
                        if t >= 4:
                            pe.wait_ge(dts, t - 3)
                        x = core.XT[:, t * P:(t + 1) * P]
                        pe.matmul(core.ps[:, t % 4, 0:M_INNER], x, w[:, 0:M_INNER], start=True, stop=True)
                        pe.matmul(core.ps[:, t % 4, M_INNER:M_INNER + M_HEADS], x, w[:, M_PROJ - M_HEADS:], start=True, stop=True).then_inc(zmade, 1)
                pe.wait_ge(da_ready, 1)
                dense = da[:, :, 0:M_HEADS]
                pe.matmul(core.ps[:, 0, 0:TILES * M_HEADS], core.tri[:], dense, start=True, stop=True)
                pe.matmul(core.ps[:, 0, P:P + TILES * M_HEADS], core.all_ones[:], dense, start=True, stop=True).then_inc(sums, 1)
                for t in range(TILES):
                    mm = pe.matmul(core.ps[0:DA_W, 4 + t // 4, (t % 4) * P:(t % 4 + 1) * P], da[:, t, :], core.tri[:], start=True, stop=True)
                    if t % 4 == 3:
                        mm.then_inc(rows_sum, 1)

            @block.scalar
            def _(a):
                def middle(g):
                    a.wait_ge(rows_rest, g + 1)
                    a.activation(rounded[:, 1, g * BANK:(g + 1) * BANK], left[:, g * BANK:(g + 1) * BANK], ACT.Copy).then_inc(rows_mid, 1)

                a.wait_ge(loaded, 32)
                a.activation(Arow[:], ms.rows[:, M_HEADS:2 * M_HEADS], ACT.Exp).then_inc(a_ready, 1)
                for g in range(4):
                    a.wait_ge(turned, g + 1)
                    a.activation(core.XT[:, g * BANK:(g + 1) * BANK], core.ps[:, g, :], ACT.Copy, scale=ms.cols[:, 0:1]).then_inc(kept, 1)

                def silu(n):
                    b, j = divmod(n, CH)
                    a.wait_ge(conv, n + 1)
                    a.activation(ms.xs[:, j, b * SEQ:(b + 1) * SEQ], cv[:, n % 4, :], ACT.Silu).then_inc(silued, 1)

                for b in range(BATCH):
                    for j in range(CH):
                        n = b * CH + j
                        a.wait_ge(made, n + 1)
                        if n >= 4:
                            a.wait_ge(silued, n - 3)
                        a.activation(cv[:, n % 4, :], core.ps[:, 4 + n % 4, :], ACT.Identity, scale=ms.cols[:, 1 + j * 4 + 3:1 + j * 4 + 4], bias=ms.cols[:, 17 + j:18 + j]).then_inc(tap, 1)
                        if n >= 2:
                            silu(n - 2)
                    for q in range(QT):
                        t = b * QT + q
                        a.wait_ge(zmade, t + 1)
                        a.activation(ms.zs[:, t, :], core.ps[:, t % 4, 0:M_INNER], ACT.Silu).then_inc(zsilued, 1)
                silu(BATCH * CH - 2)
                silu(BATCH * CH - 1)
                a.wait_ge(neg_abs, 1)
                a.activation(dt1[:], dt1[:], ACT.Exp).then_inc(exp_dt, 1)
                a.wait_ge(plus_one, 1)
                a.activation(dt1[:], dt1[:], ACT.Ln).then_inc(lned, 1)
                a.wait_ge(diffs, 1)
                a.activation(ms.fac[:], ms.fac[:], ACT.Exp).then_inc(exps, 1)
                for g in range(4):
                    a.wait_ge(rows_sum, g + 1)
                    a.activation(rounded[:, 0, g * BANK:(g + 1) * BANK], core.ps[0:DA_W, 4 + g, :], ACT.Copy).then_inc(rows_kept, 1)
                    if g >= 1:
                        middle(g - 1)
                middle(3)

            @block.gpsimd
            def _(g):
                g.memset(da[:], 0.0).then_inc(padded, 1)
                rstd_ms(g, core, pool_done, ve_done, msq, rstd)

            @block.vector
            def _(v):
                own = Chain(v, chain_s)
                rms_tokens(v, pool_done, ve_done, own, H, stats, mv, msq)
                for t in range(TILES):
                    if t % GROUP == 0:
                        v.wait_ge(pool_done, 2 * (t // GROUP) + 2)
                    v.tensor_scalar(xn[:, t, :], H[:, t, :], rstd[:, t:t + 1], None, ALU.mult).then_inc(ve_done, 1)
                v.wait_ge(loaded, 32)
                for b in range(BATCH):
                    for j in range(CH):
                        n = b * CH + j
                        v.wait_ge(tap, n + 1)
                        for k in (2, 1, 0):
                            lag = 3 - k
                            mm = v.scalar_tensor_tensor(out=cv[:, n % 4, lag:], in0=core.ps[:, 4 + n % 4, 0:SEQ - lag], scalar=ms.cols[:, 1 + j * 4 + k:2 + j * 4 + k], in1=cv[:, n % 4, lag:], op0=ALU.mult, op1=ALU.add)
                            if k:
                                own(mm)
                        mm.then_inc(conv, 1)
                    for q in range(QT):
                        t = b * QT + q
                        v.wait_ge(zsilued, t + 1)
                        v.tensor_tensor(dt0[:, t, :], core.ps[:, t % 4, M_INNER:M_INNER + M_HEADS], ms.rows[:, 0:M_HEADS], ALU.add).then_inc(dts, 1)
                v.wait_ge(dts, TILES)
                v.scalar_tensor_tensor(out=dt1[:], in0=dt0[:], scalar=-1.0, in1=dt0[:], op0=ALU.mult, op1=ALU.min).then_inc(neg_abs, 1)
                v.wait_ge(exp_dt, 1)
                v.tensor_scalar(dt1[:], dt1[:], 1.0, None, ALU.add).then_inc(plus_one, 1)
                v.wait_ge(lned, 1)
                own(v.scalar_tensor_tensor(out=ms.dt[:], in0=dt0[:], scalar=0.0, in1=dt1[:], op0=ALU.max, op1=ALU.add))
                v.wait_ge(a_ready, 1)
                v.wait_ge(padded, 1)
                arow = Arow[:].unsqueeze(1).broadcast_to([P, TILES, M_HEADS])
                own(v.scalar_tensor_tensor(out=da[:, :, 0:M_HEADS], in0=ms.dt[:], scalar=-1.0, in1=arow, op0=ALU.mult, op1=ALU.mult))
                for r, n in ((M_HEADS, PARTS - 1), (32, PARTS)):
                    mm = v.tensor_copy(da[:, :, r:r + n * M_HEADS].rearrange("p t (k h) -> p t k h", k=n), da[:, :, 0:M_HEADS].unsqueeze(2).broadcast_to([P, TILES, n, M_HEADS]))
                    if r == M_HEADS:
                        own(mm)
                mm.then_inc(da_ready, 1)
                v.wait_ge(sums, 1)
                n = TILES * M_HEADS
                own(v.tensor_copy(ms.fac[:, 0:2, :].rearrange("p k n -> p (k n)"), core.ps[:, 0, 0:2 * n]))
                v.tensor_tensor(ms.fac[:, 2, :], ms.fac[:, 1, :], ms.fac[:, 0, :], ALU.subtract).then_inc(diffs, 1)
                v.wait_ge(exps, 1)
                own(v.tensor_tensor(ms.fac[:, 2, :], ms.fac[:, 2, :], ms.dt[:].rearrange("p t h -> p (t h)"), ALU.mult))
                for g in range(4):
                    v.wait_ge(rows_kept, g + 1)
                    cols = slice(g * BANK, (g + 1) * BANK)
                    v.scalar_tensor_tensor(out=left[:, cols], in0=rounded[:, 0, cols], scalar=ms.less[:, 0:1], in1=core.ps[0:DA_W, 4 + g, :], op0=ALU.mult, op1=ALU.add).then_inc(rows_rest, 1)
                for g in range(4):
                    v.wait_ge(rows_mid, g + 1)
                    cols = slice(g * BANK, (g + 1) * BANK)
                    for out, rows in ((ms.lh, slice(0, M_ROWS)), (ms.csT, slice(32, DA_W))):
                        v.scalar_tensor_tensor(out=out[rows, cols], in0=rounded[rows, 1, cols], scalar=ms.less[rows, 1:2], in1=left[rows, cols], op0=ALU.mult, op1=ALU.add).then_inc(factors, 1)

    mamba_chunks(core, H, m)
    mamba_output(core, H, m)


class MambaBuffers:

    def __init__(self, s):
        self.cols = s.sb("cols", [P, 23])
        self.rows = s.sb("rows", [P, 3 * M_HEADS])
        self.wo = s.sb("wo", [P, 2, D])
        self.xs = s.sb("xs", [P, CH, TOK])
        self.zs = s.sb("zs", [P, TILES, M_INNER])
        self.dt = s.sb("dt", [P, TILES, M_HEADS])
        self.fac = s.sb("fac", [P, 3, TILES * M_HEADS])
        self.csT = s.sb("csT", [DA_W, TOK], BF16)
        self.lh = s.sb("lh", [DA_W, TOK], BF16)
        self.rh = s.sb("rh", [DA_W, RH, M_HEADS, P], BF16)
        self.delta = s.sb("delta", [DA_W, M_HEADS, P], BF16)
        self.less = s.sb("less", [DA_W, 2])
        self.yz = s.sb("yz", [P, TILES, M_INNER])
        self.ss = s.sb("ss", [P, TILES])
        self.state = s.sb("state", [P, BATCH, M_INNER])


def mamba_begin(core, H, m):
    with Scope(core, "mc") as s:
        loaded, set_ = s.sem("loaded"), s.sem("set")
        with s.block() as block:
            @block.sync
            def _(sp):
                for i in range(RH):
                    sp.dma_start(m.rh[:, i], core.dram["m_delta"]).then_inc(loaded, 16)
                sp.dma_start(m.delta[:], core.dram["m_delta"]).then_inc(loaded, 16)
                sp.dma_start(m.less[:], core.dram["m_less"]).then_inc(loaded, 16)
                sp.dma_start(m.lh[:], core.dram["m_rows_of_ones"]).then_inc(loaded, 16)
                sp.dma_start(core.tri[:], core.dram["tri"]).then_inc(loaded, 16)
                sp.wait_ge(loaded, 16 * (RH + 4))

            @block.gpsimd
            def _(g):
                g.memset(core.all_ones[:], 1.0).then_inc(set_, 1)

            @block.vector
            def _(v):
                v.tensor_copy(H[:], core.X[:]).then_inc(set_, 1)


def mamba_chunks(core, H, m):
    with Scope(core, "mb") as s:
        L = s.sb("L", [P, 2, M_HEADS, P])
        M = s.sb("M", [P, 2, M_HEADS, P])
        Bt = s.sb("Bt", [P, 2, P])
        xt = s.sb("xt", [P, 2, M_INNER])
        dtx = s.sb("dtx", [P, 2, M_INNER])
        wx = s.sb("wx", [P, 2, M_INNER])
        side = s.sb("side", [P, 2, M_INNER])
        off = s.sb("off", [P, 2, M_INNER])
        y = s.sb("y", [P, 2, M_INNER])
        sq = s.sb("sq", [P, 2, M_INNER])
        names = ("rows_in", "args", "decays", "inner", "turned", "x_kept", "b_kept", "dtx_made", "wx_made", "mixed",
                 "skipped", "sided", "inside", "outside", "state_in", "off_made", "y_made", "gated", "squares", "shrunk", "state_made")
        sem = {n: s.sem(n) for n in names}
        NT = TILES

        def tile(u):
            return (u % BATCH) * QT + u // BATCH

        def heads(x):
            return x.rearrange("p (h e) -> p h e", h=M_HEADS)

        def each(row):
            return row.unsqueeze(2).broadcast_to([P, M_HEADS, M_HD])

        def fac(k, t):
            return each(m.fac[:, k, t * M_HEADS:(t + 1) * M_HEADS])

        with s.block() as block:
            @block.tensor
            def _(pe):
                def first(u):
                    cols = slice(tile(u) * P, (tile(u) + 1) * P)
                    pe.wait_ge(sem["rows_in"], u + 1)
                    if u >= 1:
                        pe.wait_ge(sem["decays"], u)
                    for k in range(2):
                        pe.matmul(core.ps[:, k, :], m.lh[:, cols], m.rh[:, u % RH, 4 * k:4 * k + 4, :], start=True, stop=False)
                        mm = pe.matmul(core.ps[:, k, :], core.ident_bf[:], core.mask_k[:].unsqueeze(1).broadcast_to([P, 4, P]), start=False, stop=True)
                    mm.then_inc(sem["args"], 1)
                    if u >= 1:
                        pe.wait_ge(sem["x_kept"], u)
                        pe.wait_ge(sem["b_kept"], u)
                    for k in range(2):
                        pe.transpose(core.ps[:, 3, k * P:(k + 1) * P], m.xs[:, k, cols], core.ident[:])
                    pe.transpose(core.ps[:, 4, 0:P], m.xs[:, 2, cols], core.ident[:]).then_inc(sem["turned"], 1)
                    if u >= 1:
                        pe.wait_ge(sem["mixed"], u)
                    pe.matmul(core.ps[:, 2, 0:P], m.xs[:, 2, cols], m.xs[:, 3, cols], start=True, stop=True).then_inc(sem["inner"], 1)

                def second(u):
                    t, c, b = tile(u), u // BATCH, u % BATCH
                    if c > 0:
                        pe.wait_ge(sem["state_made"], u - BATCH + 1)
                        if u > BATCH:
                            pe.wait_ge(sem["off_made"], u - BATCH)
                        pe.matmul(core.ps[:, 6, 0:M_INNER], m.xs[:, 3, t * P:(t + 1) * P], m.state[:, b, :], start=True, stop=True).then_inc(sem["outside"], 1)
                    if u >= 1:
                        pe.wait_ge(sem["y_made"], u)
                    pe.wait_ge(sem["dtx_made"], u + 1)
                    pe.wait_ge(sem["mixed"], u + 1)
                    for h in range(M_HEADS):
                        mm = pe.matmul(core.ps[:, 5, h * M_HD:(h + 1) * M_HD], M[:, u % 2, h, :], dtx[:, u % 2, h * M_HD:(h + 1) * M_HD], start=True, stop=True)
                    mm.then_inc(sem["inside"], 1)
                    pe.wait_ge(sem["wx_made"], u + 1)
                    if u >= 1:
                        pe.wait_ge(sem["state_made"], u)
                    pe.wait_ge(sem["b_kept"], u + 1)
                    pe.matmul(core.ps[:, 7, 0:M_INNER], Bt[:, u % 2, :], wx[:, u % 2, :], start=True, stop=True).then_inc(sem["state_in"], 1)

                first(0)
                for u in range(NT):
                    if u + 1 < NT:
                        first(u + 1)
                    second(u)

            @block.scalar
            def _(a):
                def square(u):
                    a.wait_ge(sem["gated"], u + 1)
                    if u >= 2:
                        a.wait_ge(sem["squares"], u - 1)
                    a.activation(sq[:, u % 2], m.yz[:, tile(u), :], ACT.Square, accum_out=m.ss[:, tile(u):tile(u) + 1]).then_inc(sem["squares"], 1)

                for u in range(NT):
                    a.wait_ge(sem["args"], u + 1)
                    if u >= 2:
                        a.wait_ge(sem["mixed"], u - 1)
                    a.activation(L[:, u % 2].rearrange("p (k h) q -> p k (h q)", k=2), core.ps[:, 0:2, :], ACT.Exp).then_inc(sem["decays"], 1)
                    a.wait_ge(sem["turned"], u + 1)
                    if u >= 2:
                        a.wait_ge(sem["skipped"], u - 1)
                        a.wait_ge(sem["wx_made"], u - 1)
                        a.wait_ge(sem["state_in"], u - 1)
                    a.activation(xt[:, u % 2], core.ps[:, 3, 0:M_INNER], ACT.Copy).then_inc(sem["x_kept"], 1)
                    a.activation(Bt[:, u % 2], core.ps[:, 4, 0:P], ACT.Copy).then_inc(sem["b_kept"], 1)
                    if u >= 3:
                        square(u - 3)
                for u in range(NT - 3, NT):
                    square(u)

            @block.gpsimd
            def _(g):
                def rows(u):
                    if u >= RH:
                        g.wait_ge(sem["args"], u - RH + 1)
                    t = tile(u)
                    g.tensor_tensor(m.rh[32:DA_W, u % RH], m.csT[32:DA_W, t * P:(t + 1) * P].unsqueeze(1).broadcast_to([M_ROWS, M_HEADS, P]), m.delta[32:DA_W], ALU.mult).then_inc(sem["rows_in"], 1)
                    g.wait_ge(sem["rows_in"], u + 1)

                for u in range(2):
                    rows(u)
                for u in range(NT):
                    c, b = u // BATCH, u % BATCH
                    if u + 2 < NT:
                        if u > BATCH:
                            g.wait_ge(sem["sided"], u - BATCH)
                        rows(u + 2)
                    g.wait_ge(sem["x_kept"], u + 1)
                    if u >= 2:
                        g.wait_ge(sem["y_made"], u - 1)
                    g.tensor_tensor(heads(side[:, u % 2]), heads(xt[:, u % 2]), each(m.rows[:, 2 * M_HEADS:]), ALU.mult).then_inc(sem["skipped"], 1)
                    g.wait_ge(sem["skipped"], u + 1)
                    if c > 0:
                        g.wait_ge(sem["state_made"], u - BATCH + 1)
                        g.wait_ge(sem["outside"], u - BATCH + 1)
                        g.tensor_tensor(heads(m.state[:, b, :]), heads(m.state[:, b, :]), fac(1, tile(u)), ALU.mult).then_inc(sem["shrunk"], 1)
                        g.wait_ge(sem["off_made"], u - BATCH + 1)
                        g.tensor_tensor(side[:, u % 2], off[:, u % 2], side[:, u % 2], ALU.add).then_inc(sem["sided"], 1)

            @block.vector
            def _(v):
                def prepare(u):
                    t = tile(u)
                    v.wait_ge(sem["x_kept"], u + 1)
                    if u >= 2:
                        v.wait_ge(sem["inside"], u - 1)
                    v.tensor_tensor(heads(dtx[:, u % 2]), heads(xt[:, u % 2]), each(m.dt[:, t, :]), ALU.mult).then_inc(sem["dtx_made"], 1)
                    if u >= 2:
                        v.wait_ge(sem["state_in"], u - 1)
                    v.tensor_tensor(heads(wx[:, u % 2]), heads(xt[:, u % 2]), fac(2, t), ALU.mult).then_inc(sem["wx_made"], 1)
                    v.wait_ge(sem["decays"], u + 1)
                    v.wait_ge(sem["inner"], u + 1)
                    v.tensor_tensor(M[:, u % 2], core.ps[:, 2, 0:P].unsqueeze(1).broadcast_to([P, M_HEADS, P]), L[:, u % 2], ALU.mult).then_inc(sem["mixed"], 1)

                prepare(0)
                for u in range(NT):
                    t, c, b = tile(u), u // BATCH, u % BATCH
                    if c > 0:
                        v.wait_ge(sem["outside"], u - BATCH + 1)
                        if u >= 2 + BATCH:
                            v.wait_ge(sem["sided"], u - BATCH - 1)
                        v.tensor_tensor(heads(off[:, u % 2]), heads(core.ps[:, 6, 0:M_INNER]), fac(0, t), ALU.mult).then_inc(sem["off_made"], 1)
                    if u + 1 < NT:
                        prepare(u + 1)
                    v.wait_ge(sem["inside"], u + 1)
                    if c > 0:
                        v.wait_ge(sem["sided"], u - BATCH + 1)
                    else:
                        v.wait_ge(sem["skipped"], u + 1)
                    if u >= 2:
                        v.wait_ge(sem["gated"], u - 1)
                    v.tensor_tensor(y[:, u % 2], core.ps[:, 5, 0:M_INNER], side[:, u % 2], ALU.add).then_inc(sem["y_made"], 1)
                    v.wait_ge(sem["state_in"], u + 1)
                    if c > 0:
                        v.wait_ge(sem["shrunk"], u - BATCH + 1)
                        v.tensor_tensor(m.state[:, b, :], core.ps[:, 7, 0:M_INNER], m.state[:, b, :], ALU.add).then_inc(sem["state_made"], 1)
                    else:
                        v.tensor_copy(m.state[:, b, :], core.ps[:, 7, 0:M_INNER]).then_inc(sem["state_made"], 1)
                    v.wait_ge(sem["y_made"], u + 1)
                    v.tensor_tensor(m.yz[:, t, :], y[:, u % 2], m.zs[:, t, :], ALU.mult).then_inc(sem["gated"], 1)


def mamba_output(core, H, m):
    with Scope(core, "mo") as s:
        yT = s.sb("yT", [P, 4, 2, P])
        rstd = s.sb("rstd", [P, TILES])
        turned, kept, made, added, pool_done, first = (s.sem(n) for n in ("turned", "kept", "made", "added", "pool_done", "first"))
        with s.block() as block:
            @block.tensor
            def _(pe):
                def project(t):
                    pe.wait_ge(kept, 2 * t + 2)
                    if t >= 4:
                        pe.wait_ge(added, t - 3)
                    for c in range(2):
                        mm = pe.matmul(core.ps[:, 4 + t % 4, 0:D], yT[:, t % 4, c, :], m.wo[:, c, :], start=(c == 0), stop=(c == 1))
                    mm.then_inc(made, 1)

                for t in range(TILES):
                    if t >= 4:
                        pe.wait_ge(kept, 2 * (t - 3))
                    for c in range(2):
                        mm = pe.transpose(core.ps[:, t % 4, c * P:(c + 1) * P], m.yz[:, t, c * P:(c + 1) * P], core.ident[:])
                    mm.then_inc(turned, 1)
                    if t >= 1:
                        project(t - 1)
                project(TILES - 1)

            @block.scalar
            def _(a):
                for t in range(TILES):
                    a.wait_ge(turned, t + 1)
                    if t >= 4:
                        a.wait_ge(made, t - 3)
                    for c in range(2):
                        a.activation(yT[:, t % 4, c, :], core.ps[:, t % 4, c * P:(c + 1) * P], ACT.Copy, scale=m.cols[:, 21 + c:22 + c]).then_inc(kept, 1)

            @block.gpsimd
            def _(g):
                g.tensor_scalar(rstd[:], m.ss[:], 1.0 / M_INNER, EPS, ALU.mult, ALU.add).then_inc(first, 1)
                g.wait_ge(first, 1)
                g.tensor_tensor(rstd[:], rstd[:], core.half_neg[:], ALU.pow).then_inc(pool_done, 1)

            @block.vector
            def _(v):
                v.wait_ge(pool_done, 1)
                for t in range(TILES):
                    v.wait_ge(made, t + 1)
                    v.scalar_tensor_tensor(out=H[:, t, :], in0=core.ps[:, 4 + t % 4, 0:D], scalar=rstd[:, t:t + 1], in1=H[:, t, :], op0=ALU.mult, op1=ALU.add).then_inc(added, 1)


def mamba_end(core, H):
    with Scope(core, "me") as s:
        fw = s.sb("fw", [P, D])
        Y = s.sb("Y", [P, TILES, D])
        stats = s.sb("stats", [P, TILES, 6])
        mv = s.sb("mv", [P, TILES, 2])
        msq = s.sb("msq", [P, TILES])
        rstd = s.sb("rstd", [P, TILES])
        rstd2 = s.sb("rstd2", [P, TILES])
        loaded, chain_s = s.sem("loaded"), s.sem("ve_chain")
        ve_done, pool_done, ve_done2, pool_done2 = s.sem("ve_done"), s.sem("pool_done"), s.sem("ve_done2"), s.sem("pool_done2")
        with s.block() as block:
            @block.sync
            def _(sp):
                sp.dma_start(fw[:], core.dram["L3_attn_final_norm_w"].rearrange("(a n) -> a n", a=1).broadcast_to([P, D])).then_inc(loaded, 16)

            @block.gpsimd
            def _(g):
                rstd_ms(g, core, pool_done, ve_done, msq, rstd)
                rstd_tokens(g, core, pool_done2, ve_done2, mv, rstd2)

            @block.vector
            def _(v):
                own = Chain(v, chain_s)
                rms_tokens(v, pool_done, ve_done, own, H, stats, mv, msq)
                v.wait_ge(loaded, 16)
                for n in range(4):
                    v.wait_ge(pool_done, 2 * n + 2)
                    for t in range(n * GROUP, (n + 1) * GROUP):
                        own.mark(v.scalar_tensor_tensor(out=Y[:, t, :], in0=H[:, t, :], scalar=rstd[:, t:t + 1], in1=fw[:], op0=ALU.mult, op1=ALU.mult))
                    own.wait()
                    cols = slice(n * GROUP, (n + 1) * GROUP)
                    own(v.tensor_tensor(Y[:, cols], Y[:, cols], core.X[:, cols], ALU.add))
                    norm_stats(v, ve_done2, own, Y, stats, mv, n)
                for n in range(4):
                    norm_apply(v, pool_done2, own, Y, core.X, mv, rstd2, n)


def gated_mixture(core):
    d = core.dram
    E = MOE3_E
    W = TILES * E
    UNITS = E * BATCH
    with Scope(core, "moe3") as s:
        gate_w = s.sb("gate_w", [P, E])
        rank = s.sb("rank", [P, 16])
        sim = s.sb("sim", [E, E])
        rep = s.sb("rep", [E, W])
        blocks = s.sb("blocks", [W, TILES, E])
        w_gu = s.sb("w_gu", [P, E, 2 * MOE3_F])
        w_down = s.sb("w_down", [P, E, D])
        ones = s.sb("ones", [P, E])
        L = s.sb("L", [P, TILES, E])
        key = s.sb("key", [P, TILES, E])
        hots = [s.sb(f"hot{k}", [P, TILES, E]) for k in range(2)]
        tops = [s.sb(f"top{k}", [P, TILES]) for k in range(2)]
        best = s.sb("best", [P, TILES])
        gates = s.sb("gates", [P, TILES, E])
        gatesT = s.sb("gatesT", [W, P])
        count = s.sb("count", [P, E])
        used = s.sb("used", [E, E])
        unused = s.sb("unused", [E, E])
        own_use = s.sb("own_use", [E, 1])
        sim_key = s.sb("sim_key", [E, E])
        sim_top = s.sb("sim_top", [E, 2])
        moved = s.sb("moved", [E, 1])
        R = s.sb("R", [E, E])
        R2 = s.sb("R2", [E, E])
        Rrep = s.sb("Rrep", [W, TILES, E])
        dense = s.sb("dense", [P, TILES, E])
        sg = s.sb("sg", [P, 2, SEQ])
        hm = s.sb("hm", [P, 2, SEQ])
        stats = s.sb("stats", [P, TILES, 6])
        mv = s.sb("mv", [P, TILES, 2])
        rstd = s.sb("rstd", [P, TILES])
        names = ("loaded", "loaded_w", "turned", "kept", "scored", "differ", "exped", "first_two", "counted", "gated",
                 "weights_turned", "weights_kept", "rerouted", "spread", "spread_kept", "summed", "weights",
                 "made", "silued", "hidden", "down", "added", "ve_done", "pool_done", "chain", "ones_set")
        sem = {n: s.sem(n) for n in names}
        with s.block() as block:
            @block.sync
            def _(sp):
                sp.dma_start(gate_w[:], d["moe3_gateT"]).then_inc(sem["loaded"], 16)
                sp.dma_start(rank[:], d["rank"].broadcast_to([P, 16])).then_inc(sem["loaded"], 16)
                sp.dma_start(sim[:], d["L3_ffn_similarity_matrix"]).then_inc(sem["loaded"], 16)
                sp.dma_start(rep[:], d["moe3_rep"]).then_inc(sem["loaded"], 16)
                sp.dma_start(blocks[:].rearrange("p t e -> p (t e)"), d["moe3_blocks"]).then_inc(sem["loaded"], 16)
                sp.dma_start(w_gu[:], d["moe3_gate_upT"]).then_inc(sem["loaded_w"], 16)
                sp.dma_start(w_down[:], d["moe3_downT"]).then_inc(sem["loaded_w"], 16)

            @block.tensor
            def _(pe):
                turn_tokens(pe, core, sem["turned"], core.X)
                pe.wait_ge(sem["loaded"], 80)
                for t in range(TILES):
                    pe.wait_ge(sem["kept"], t // 4 + 1)
                    m = pe.matmul(core.ps[:, 7, t * E:(t + 1) * E], core.XT[:, t * P:(t + 1) * P], gate_w[:], start=True, stop=True)
                m.then_inc(sem["scored"], 1)

                def route():
                    pe.wait_ge(sem["ones_set"], 1)
                    pe.wait_ge(sem["first_two"], 1)
                    pe.matmul(core.ps[0:E, 7, 0:E], ones[:], count[:], start=True, stop=True)
                    pe.matmul(core.ps[0:E, 7, E:E + 1], count[:], ones[:, 0:1], start=True, stop=True).then_inc(sem["counted"], 1)
                    pe.wait_ge(sem["gated"], 1)
                    pe.wait_ge(sem["rerouted"], 1)
                    pe.transpose(core.ps[:, 7, P:2 * P], gates[:].rearrange("p t e -> p (t e)"), core.ident[:]).then_inc(sem["weights_turned"], 1)
                    pe.matmul(core.ps[:, 7, 2 * P:2 * P + E], rep[:], R[:], start=True, stop=True).then_inc(sem["spread"], 1)
                    pe.wait_ge(sem["weights_kept"], 1)
                    pe.wait_ge(sem["spread_kept"], 1)
                    pe.matmul(core.ps[:, 7, 3 * P:3 * P + W], gatesT[:], Rrep[:].rearrange("p t e -> p (t e)"), start=True, stop=True).then_inc(sem["summed"], 1)

                def down(u):
                    b, e = divmod(u, E)
                    pe.wait_ge(sem["hidden"], u + 1)
                    if u >= 2:
                        pe.wait_ge(sem["added"], QT * (u - 1))
                    for q in range(QT):
                        m = pe.matmul(core.ps[:, 4 + u % 2, q * D:(q + 1) * D], hm[:, u % 2, q * P:(q + 1) * P], w_down[:, e, :], start=True, stop=True)
                    m.then_inc(sem["down"], 1)

                pe.wait_ge(sem["loaded_w"], 32)
                for u in range(UNITS):
                    b, e = divmod(u, E)
                    x = core.XT[:, b * SEQ:(b + 1) * SEQ]
                    pe.wait_ge(sem["kept"], 4)
                    if u >= 2:
                        pe.wait_ge(sem["hidden"], u - 1)
                    for k in range(2):
                        m = pe.matmul(core.ps[:, 2 * (u % 2) + k, :], w_gu[:, e, k * P:(k + 1) * P], x, start=True, stop=True)
                    m.then_inc(sem["made"], 1)
                    if u == 1:
                        route()
                    if u >= 1:
                        down(u - 1)
                down(UNITS - 1)

            @block.scalar
            def _(a):
                keep_turned(a, core, sem["turned"], sem["kept"])
                a.wait_ge(sem["differ"], 1)
                a.activation(L[:], L[:], ACT.Exp).then_inc(sem["exped"], 1)

                def silu(u):
                    a.wait_ge(sem["made"], u + 1)
                    if u >= 2:
                        a.wait_ge(sem["hidden"], u - 1)
                    a.activation(sg[:, u % 2], core.ps[:, 2 * (u % 2), :], ACT.Silu).then_inc(sem["silued"], 1)

                silu(0)
                silu(1)
                a.wait_ge(sem["weights_turned"], 1)
                a.wait_ge(sem["spread"], 1)
                a.activation(gatesT[:], core.ps[:, 7, P:2 * P], ACT.Copy).then_inc(sem["weights_kept"], 1)
                for u in range(2, UNITS):
                    silu(u)

            @block.gpsimd
            def _(g):
                g.memset(ones[:], 1.0).then_inc(sem["ones_set"], 1)
                rstd_tokens(g, core, sem["pool_done"], sem["ve_done"], mv, rstd)

            @block.vector
            def _(v):
                own = Chain(v, sem["chain"])

                def each(x):
                    return x[:].unsqueeze(2).broadcast_to([P, TILES, E])

                v.wait_ge(sem["loaded"], 80)
                v.wait_ge(sem["scored"], 1)
                own(v.tensor_copy(L[:], core.ps[:, 7, 0:W].rearrange("p (t e) -> p t e", e=E)))
                own(v.tensor_reduce(best[:], L[:], AX.X, ALU.max))
                v.tensor_tensor(L[:], L[:], each(best), ALU.subtract).then_inc(sem["differ"], 1)
                v.wait_ge(sem["exped"], 1)
                own(v.tensor_reduce(best[:], L[:], AX.X, ALU.add))
                own(v.reciprocal(best[:], best[:]))
                own(v.tensor_tensor(L[:], L[:], each(best), ALU.mult))
                pick_two(v, own, rank, L[:], (key, best), hots, tops, E)
                v.tensor_reduce(count[:], hots[0][:].rearrange("p t e -> p e t"), AX.X, ALU.add).then_inc(sem["first_two"], 1)
                own(v.tensor_tensor(best[:], tops[0][:], tops[1][:], ALU.add))
                own(v.tensor_scalar(best[:], best[:], 1e-12, None, ALU.max))
                own(v.reciprocal(best[:], best[:]))
                for k in range(2):
                    own(v.tensor_tensor(tops[k][:], tops[k][:], best[:], ALU.mult))
                    own(v.tensor_tensor(hots[k][:], hots[k][:], each(tops[k]), ALU.mult))
                v.tensor_tensor(gates[:], hots[0][:], hots[1][:], ALU.add).then_inc(sem["gated"], 1)
                v.wait_ge(sem["counted"], 1)
                own(v.tensor_scalar(used[:], core.ps[0:E, 7, 0:E], 0.5, None, ALU.is_gt))
                own(v.tensor_scalar(own_use[:], core.ps[0:E, 7, E:E + 1], 0.5, None, ALU.is_lt))
                own(v.tensor_scalar(unused[:], used[:], -1.0, 1.0, ALU.mult, ALU.add))
                own(v.tensor_tensor(sim_key[:], sim[:], used[:], ALU.mult))
                own(v.scalar_tensor_tensor(out=sim_key[:], in0=unused[:], scalar=MASKED, in1=sim_key[:], op0=ALU.mult, op1=ALU.add))
                own(v.tensor_reduce(sim_top[:, 0:1], sim_key[:], AX.X, ALU.max))
                own(v.tensor_tensor(sim_key[:], sim_key[:], sim_top[:, 0:1].broadcast_to([E, E]), ALU.is_equal))
                own(v.tensor_tensor(sim_key[:], sim_key[:], rank[0:E, 0:E], ALU.mult))
                own(v.tensor_reduce(sim_top[:, 1:2], sim_key[:], AX.X, ALU.max))
                own(v.tensor_tensor(R2[:], sim_key[:], sim_top[:, 1:2].broadcast_to([E, E]), ALU.is_equal))
                own(v.tensor_scalar(moved[:], sim_top[:, 0:1], THRESHOLD, None, ALU.is_ge))
                own(v.tensor_tensor(moved[:], moved[:], own_use[:], ALU.mult))
                own(v.tensor_tensor(R2[:], R2[:], core.ident[0:E, 0:E], ALU.subtract))
                v.scalar_tensor_tensor(out=R[:], in0=R2[:], scalar=moved[:], in1=core.ident[0:E, 0:E], op0=ALU.mult, op1=ALU.add).then_inc(sem["rerouted"], 1)
                v.wait_ge(sem["spread"], 1)
                v.wait_ge(sem["weights_kept"], 1)
                v.tensor_tensor(Rrep[:], blocks[:], core.ps[:, 7, 2 * P:2 * P + E].unsqueeze(1).broadcast_to([W, TILES, E]), ALU.mult).then_inc(sem["spread_kept"], 1)
                v.wait_ge(sem["summed"], 1)
                v.tensor_copy(dense[:], core.ps[:, 7, 3 * P:3 * P + W].rearrange("p (t e) -> p t e", e=E)).then_inc(sem["weights"], 1)

                v.wait_ge(sem["weights"], 1)

                def weigh(u):
                    b, e = divmod(u, E)
                    v.wait_ge(sem["down"], u + 1)
                    if u:
                        v.wait_ge(sem["added"], QT * u)
                    if e == 1 and b >= 1:
                        norm_apply(v, sem["pool_done"], own, core.X, core.X, mv, rstd, b - 1)
                    for q in range(QT):
                        t = b * QT + q
                        v.scalar_tensor_tensor(out=core.X[:, t, :], in0=core.ps[:, 4 + u % 2, q * D:(q + 1) * D], scalar=dense[:, t, e:e + 1], in1=core.X[:, t, :], op0=ALU.mult, op1=ALU.add).then_inc(sem["added"], 1)
                    if e == E - 1:
                        v.wait_ge(sem["added"], QT * (u + 1))
                        norm_stats(v, sem["ve_done"], own, core.X, stats, mv, b)

                for u in range(UNITS):
                    v.wait_ge(sem["silued"], u + 1)
                    if u >= 2:
                        v.wait_ge(sem["down"], u - 1)
                    v.tensor_tensor(hm[:, u % 2], core.ps[:, 2 * (u % 2) + 1, :], sg[:, u % 2], ALU.mult).then_inc(sem["hidden"], 1)
                    if u >= 1:
                        weigh(u - 1)
                weigh(UNITS - 1)
                norm_apply(v, sem["pool_done"], own, core.X, core.X, mv, rstd, BATCH - 1)


def program(nc, dram, out):
    with ExitStack() as ctx:
        core = Core(nc, ctx, dram)
        scratch = {
            "qk": nc.dram_tensor("scratch_qk", (BATCH, PARTS, 2 * L0_EXP, SEQ), BF16, kind="Internal").ap(),
            "pos": nc.dram_tensor("scratch_pos", (PARTS, BATCH, HEADS, SEQ), BF16, kind="Internal").ap(),
        }
        prepare(core)
        M = ctx.enter_context(nc.sbuf_tensor("expert_products", [P, MOE0_E * D], F32))
        experts0(core, M)
        with Scope(core, "l0") as s:
            buf = {
                "V": s.sb("V", [P, TILES, HEADS, L0_DH + 1]),
                "gate": s.sb("gate", [P, TILES, L0_EXP]),
            }
            l0_project(core, buf, scratch)
            buf["O"] = s.sb("O", [P, TILES, L0_EXP])
            attention(core, "l0a", causal_plan(), scratch, buf["V"], buf["O"])
            l0_finish(core, buf)
        mixture(core, "moe0", MOE0_E, M, routed=False)
        with Scope(core, "l1") as s:
            scr = {"qk": nc.dram_tensor("scratch_qk1", (BATCH, PARTS, 2 * D, SEQ), BF16, kind="Internal").ap()}
            rscr = {"qk": nc.dram_tensor("scratch_rqk", (BATCH, PARTS, 2 * D, SEQ), BF16, kind="Internal").ap()}
            V = s.sb("V", [P, TILES, HEADS, L1_DH + 1])
            RV = s.sb("RV", [P, QT, HEADS, L1_DH + 1])
            O = s.sb("O", [P, TILES, D])
            OT = s.sb("OT", [P, TOK])
            l1_project(core, V, RV, scr["qk"], rscr["qk"])
            attention(core, "l1a", full_plan(), scr, V, O)
            l1_between(core, O, OT, rscr["qk"])
            attention(core, "l1r", recursive_plan(), rscr, RV, O)
            l1_finish(core, O, OT)
        mixture(core, "moe1", MOE1_E, core.w_routed, routed=True)
        with Scope(core, "l2") as s:
            cat = s.sb("cat", [P, BATCH, SEQ + STEPS])
            history = s.sb("history", [P, TOK])
            sign = s.sb("sign", [P, 1])
            l2_ssm(core, cat, sign)
            l2_scan(core, cat, history, sign)
            l2_finish(core, history, sign)
        bit_mlp(core)
        with Scope(core, "l3") as s:
            H = s.sb("H", [P, TILES, D])
            buffers = MambaBuffers(s)
            mamba_begin(core, H, buffers)
            with nc.Fori(0, M_LAYERS) as l:
                mamba_layer(core, l, H, buffers)
            mamba_end(core, H)
        gated_mixture(core)
        store(core, out)


_USED = [
    "L0_attn_x", "L0_attn_b_in", "L0_ffn_w_in", "L1_attn_Wg", "L1_attn_bg",
    "L1_ffn_expert_biases", "L1_ffn_bs", "L1_ffn_br", "L2_attn_out_b", "L2_ffn_w_fc", "L2_ffn_w_proj", "L2_ffn_v",
    "L3_attn_W_in", "L3_attn_W_out", "L3_attn_final_norm_w",
    "L3_ffn_similarity_matrix",
]


def kernel(**inputs):
    import numpy as _np
    import concourse.bacc as _bacc
    from concourse import mybir as _mybir
    from concourse.bass_utils import run_bass_kernel_spmd as _run

    i = {k: _np.asarray(v) for k, v in inputs.items()}
    f = _np.float32
    arrays = {name: i[name] for name in _USED}
    k_, q_ = _np.meshgrid(_np.arange(128), _np.arange(128))
    arrays["ident"] = _np.eye(128, dtype=f)
    arrays["masks"] = _np.stack([_np.where(k_ > q_, f(-1e30), f(0)), _np.where(q_ > k_, f(-1e30), f(0))]).astype(f)
    sets = _np.zeros((2, 512), f)
    sets[0, :256] = 1
    sets[1, 256:] = 1
    arrays["set_rows"] = sets
    arrays["ones"] = _np.ones((1, 512), _mybir.dt.np(_mybir.dt.bfloat16))
    arrays["l0_out_ln"] = _np.stack([i["L0_attn_out_ln_w"], i["L0_attn_out_ln_b"]])
    arrays["l0_w_inT"] = i["L0_attn_W_in"].T
    arrays["l0_w_outT"] = i["L0_attn_W_out"].T
    arrays["l0_cols"] = _np.concatenate([
        i["L0_attn_in_ln_w"][None], i["L0_attn_in_ln_b"][None],
        _np.repeat(i["L0_attn_log_scale"], 16).reshape(2, 128),
        _np.repeat(i["L0_attn_smear_factor"], 16).reshape(2, 128),
        i["L0_attn_b_in"][:512].reshape(4, 128)]).T
    arrays["rank"] = _np.arange(16, 0, -1, dtype=f)[None]
    arrays["moe0_gateT"] = i["L0_ffn_w_gate"].T
    arrays["moe0_w_outT"] = i["L0_ffn_w_out"].transpose(0, 2, 1)
    arrays["l1_w"] = _np.stack([i[f"L1_attn_W{k}"] for k in ("q", "k", "v", "rk", "rv")])
    arrays["l1_cols"] = _np.stack([i[f"L1_attn_b{k}"] for k in ("q", "k", "rk")]).T
    arrays["l1_rows"] = _np.stack([i[f"L1_attn_b{k}"] for k in ("v", "rv")])
    arrays["l1_w2"] = _np.stack([i[f"L1_attn_W{k}"] for k in ("o", "rq")])
    arrays["l1_cols2"] = _np.stack([i[f"L1_attn_b{k}"] for k in ("o", "rq")]).T
    arrays["pastT"] = i["L1_attn_past_states"].reshape(512, 128).T
    arrays["moe1_gateT"] = i["L1_ffn_centroids"].T
    arrays["moe1_sharedT"] = i["L1_ffn_Ws"].transpose(0, 2, 1)
    arrays["moe1_wT"] = i["L1_ffn_Wr"].transpose(2, 0, 1).reshape(128, -1)
    arrays["ssm_cols"] = _np.stack([i[f"L2_attn_{k}"] for k in ("norm_g", "norm_b", "B_b", "C_b", "A_log")]).T
    arrays["ssm_w"] = _np.stack([i["L2_attn_B_w"].T, i["L2_attn_C_w"].T])
    ff1, ff2, ta, tb = (i[f"L2_attn_{k}_w"].T for k in ("ff1", "ff2", "ta", "tb"))
    rnn = _np.stack([_np.concatenate(p, axis=1) for p in ((ff1, ff2), (ta, ta), (tb, tb))])
    arrays["rnn_wx"] = rnn[:, :128]
    arrays["rnn_wh"] = _np.concatenate([rnn[:, 128:], rnn[:, 128:]], axis=1)
    arrays["rnn_b"] = _np.stack([_np.concatenate([i[f"L2_attn_{p}_b"], i[f"L2_attn_{q}_b"]]) for p, q in (("ff1", "ff2"), ("ta", "ta"), ("tb", "tb"))])
    arrays["rnn_out"] = _np.concatenate([i["L2_attn_out_w"].T] * 2)
    arrays["sign"] = _np.concatenate([-_np.ones((64, 1), f), _np.ones((64, 1), f)])
    arrays["bit_fastT"] = i["L2_ffn_fast_b"].T
    arrays["bit_uT"] = i["L2_ffn_u"].T
    arrays["bit_gate"] = i["L2_ffn_gate"].reshape(1, 1)
    arrays["m_cols"] = _np.concatenate([
        i["L3_attn_block_norm_w"][:, :, None],
        i["L3_attn_conv_w"].reshape(4, 4, 128, 4).transpose(0, 2, 1, 3).reshape(4, 128, 16),
        i["L3_attn_conv_b"].reshape(4, 4, 128).transpose(0, 2, 1),
        i["L3_attn_gate_norm_w"].reshape(4, 2, 128).transpose(0, 2, 1)], axis=2)
    arrays["m_rows"] = _np.concatenate([i["L3_attn_dt_bias"], i["L3_attn_A_log"], i["L3_attn_D"]], axis=1)
    bf = _mybir.dt.np(_mybir.dt.bfloat16)
    delta = _np.zeros((56, 8, 128), bf)
    delta[0:24] = _np.tile(-_np.eye(8), (3, 1))[:, :, None]
    delta[32:56] = _np.tile(_np.eye(8), (3, 1))[:, :, None]
    arrays["m_delta"] = delta
    less = _np.zeros((56, 2), f)
    for side in (0, 32):
        less[side + 8:side + 24, 0] = -1
        less[side + 16:side + 24, 1] = -1
    arrays["m_less"] = less
    rows_of_ones = _np.zeros((56, 2048), bf)
    rows_of_ones[32:] = 1
    arrays["m_rows_of_ones"] = rows_of_ones
    arrays["tri"] = _np.triu(_np.ones((128, 128), f))
    arrays["moe3_gateT"] = i["L3_ffn_gate_weight"].T
    arrays["moe3_gate_upT"] = i["L3_ffn_gate_up_proj"].transpose(2, 0, 1)
    arrays["moe3_downT"] = i["L3_ffn_down_proj"].transpose(2, 0, 1)
    arrays["moe3_rep"] = _np.tile(_np.eye(8, dtype=f), (1, 16))
    arrays["moe3_blocks"] = _np.kron(_np.eye(16, dtype=f), _np.ones((8, 8), f))

    nc = _bacc.Bacc("TRN2", target_bir_lowering=False, num_devices=1)
    feed, dram = {}, {}
    for name, a in arrays.items():
        a = _np.ascontiguousarray(a)
        feed[f"in_{name}"] = a
        dram[name] = nc.dram_tensor(f"in_{name}", a.shape, _mybir.dt.from_np(a.dtype), kind="ExternalInput").ap()
    out = nc.dram_tensor("out_x", (4, 512, 128), _mybir.dt.float32, kind="ExternalOutput").ap()
    program(nc, dram, out)
    r = _run(nc, [feed], core_ids=[0])
    return r.results[0]["out_x"]
```
